# Optimizing a Trainium2 kernel written in Bass

```python
import numpy as np
import jax
import jax.numpy as jnp

def _softmax(x, axis=-1):
    return jax.nn.softmax(x, axis=axis)

def _gelu(x):
    return jax.nn.gelu(x, approximate=True)

def _silu(x):
    return jax.nn.silu(x)

def _sigmoid(x):
    return jax.nn.sigmoid(x)

def _layernorm(x, axis=-1, eps=1e-05):
    m = jnp.mean(x, axis=axis, keepdims=True)
    v = jnp.var(x, axis=axis, keepdims=True)
    return (x - m) / jnp.sqrt(v + eps)

def _scatter_add(tgt, idx, src, axis=0):
    return tgt.at[idx].add(src)

def _segment_sum(src, seg, n):
    return jax.ops.segment_sum(src, seg, n)
kernel_name = 'mk_flamingo_gated_d4_seqx_r8_39d388'

def setup_inputs(seed: int=0):
    np.random.seed(seed)
    _w = jnp.asarray

    def _rec_inputs():
        import jax
        import jax.numpy as jnp
        _rk = jax.random.key(seed)
        x = 7.22e-05 + 1 * jax.random.normal(jax.random.fold_in(_rk, 1), (32, 64, 128), jnp.float32)
        _lenS = 64 - jax.random.randint(jax.random.fold_in(_rk, 7), (32,), 0, max(1, 64 // 4) + 1, jnp.int32)
        _lenS2 = 64 - jax.random.randint(jax.random.fold_in(_rk, 8), (32,), 0, max(1, 64 // 4) + 1, jnp.int32)
        _ctx_768P = jax.random.normal(jax.random.fold_in(_rk, 11), (32, 16, 96), jnp.float32)
        _ctx_768c = jax.random.dirichlet(jax.random.fold_in(_rk, 511), 0.3 * jnp.ones((16,), jnp.float32), (32, 64))
        _ctx_768t = jnp.einsum('bsk,bkd->bsd', _ctx_768c, _ctx_768P)
        _ctx_768t = _ctx_768t * jax.lax.rsqrt(jnp.mean(jnp.square(_ctx_768t)) + 1e-12) * 0.953939
        ctx_768 = -0.000191848 + 0.999787 * (_ctx_768t + 0.3 * jax.random.normal(jax.random.fold_in(_rk, 611), (32, 64, 96), jnp.float32))
        _g = jax.random.normal(jax.random.fold_in(_rk, 9001), (2, 4), jnp.float32)
        _g = jnp.sign(_g) * jnp.maximum(jnp.abs(_g), 1.0) + (_g == 0) * 1.0
        g_xattn = _g[0]
        g_ffn = _g[1]
        return (x, ctx_768, g_xattn, g_ffn)
    x, ctx_768, g_xattn, g_ffn = _rec_inputs()

    def _L0_xattn_setup():
        import jax, jax.numpy as jnp
        import numpy as np
        B, LQ, LK = (4, 256, 256)
        D1, D2, H = (128, 96, 128)
        key = jax.random.key(seed)
        ks = jax.random.split(key, 9)
        s1, s2, sh = (1.0 / np.sqrt(D1), 1.0 / np.sqrt(D2), 1.0 / np.sqrt(H))
        return {'query': jax.random.normal(ks[0], (B, LQ, D1), jnp.float32), 'key': jax.random.normal(ks[1], (B, LK, D2), jnp.float32), 'value': jax.random.normal(ks[2], (B, LK, D2), jnp.float32), 'Wq': jax.random.normal(ks[3], (D1, H), jnp.float32) * s1, 'bq': jax.random.normal(ks[4], (H,), jnp.float32) * s1, 'Wk': jax.random.normal(ks[5], (D2, H), jnp.float32) * s2, 'bk': jax.random.normal(ks[6], (H,), jnp.float32) * s2, 'Wv': jax.random.normal(ks[7], (D2, H), jnp.float32) * s2, 'bv': jax.random.normal(ks[8], (H,), jnp.float32) * s2}
    _L0_xattn_all = _L0_xattn_setup()
    _L0_xattn_in = {k: v for k, v in _L0_xattn_all.items() if k in ('Wq', 'bq', 'Wk', 'bk', 'Wv', 'bv')}
    del _L0_xattn_all

    def _L0_ffn_setup():
        import jax, jax.numpy as jnp
        import numpy as np
        HIDDEN = 128
        INNER = 512

        def _weight_quant(w):
            scale = 1.0 / jnp.clip(jnp.mean(jnp.abs(w)), 1e-05)
            wq = jnp.clip(jnp.round(w * scale), -1.0, 1.0) / scale
            return w + jax.lax.stop_gradient(wq - w)

        def _act_quant(x):
            scale = 127.0 / jnp.clip(jnp.max(jnp.abs(x), axis=-1, keepdims=True), 1e-05)
            xq = jnp.clip(jnp.round(x * scale), -128.0, 127.0) / scale
            return x + jax.lax.stop_gradient(xq - x)

        def _bitlinear(x, w):
            return jnp.einsum('bsi,oi->bso', _act_quant(x), _weight_quant(w))
        key = jax.random.key(seed)
        k0, k1, k2, k3 = jax.random.split(key, 4)
        x = jax.random.normal(k0, (4, 256, HIDDEN), dtype=jnp.float32)
        w_gate = jax.random.normal(k1, (INNER, HIDDEN), dtype=jnp.float32) / np.sqrt(HIDDEN)
        w_up = jax.random.normal(k2, (INNER, HIDDEN), dtype=jnp.float32) / np.sqrt(HIDDEN)
        w_down = jax.random.normal(k3, (HIDDEN, INNER), dtype=jnp.float32) / np.sqrt(INNER)
        return {'x': x, 'w_gate': w_gate, 'w_up': w_up, 'w_down': w_down}
    _L0_ffn_all = _L0_ffn_setup()
    _L0_ffn_in = {k: v for k, v in _L0_ffn_all.items() if k in ('w_gate', 'w_up', 'w_down')}
    del _L0_ffn_all

    def _L1_xattn_setup():
        import jax, jax.numpy as jnp
        import numpy as np
        EPS = 1e-05

        def layernorm(x, g, b):
            mu = jnp.mean(x, axis=-1, keepdims=True)
            var = jnp.mean(jnp.square(x - mu), axis=-1, keepdims=True)
            return (x - mu) * jax.lax.rsqrt(var + EPS) * g + b
        key = jax.random.key(seed)
        ks = jax.random.split(key, 12)
        B, L1, L2 = (8, 256, 256)
        D1, D2, E = (128, 96, 128)
        s1, s2, se = (D1 ** (-0.5), D2 ** (-0.5), E ** (-0.5))
        return {'modality1': jax.random.normal(ks[0], (B, L1, D1), jnp.float32), 'modality2': jax.random.normal(ks[1], (B, L2, D2), jnp.float32), 'ln1_g': jnp.ones((D1,), jnp.float32), 'ln1_b': jnp.zeros((D1,), jnp.float32), 'ln2_g': jnp.ones((D2,), jnp.float32), 'ln2_b': jnp.zeros((D2,), jnp.float32), 'Wq': jax.random.normal(ks[2], (D1, E), jnp.float32) * s1, 'bq': jax.random.normal(ks[3], (E,), jnp.float32) * 0.01, 'Wk': jax.random.normal(ks[4], (D2, E), jnp.float32) * s2, 'bk': jax.random.normal(ks[5], (E,), jnp.float32) * 0.01, 'Wv': jax.random.normal(ks[6], (D2, E), jnp.float32) * s2, 'bv': jax.random.normal(ks[7], (E,), jnp.float32) * 0.01, 'Wo': jax.random.normal(ks[8], (E, D1), jnp.float32) * se, 'bo': jax.random.normal(ks[9], (D1,), jnp.float32) * 0.01}
    _L1_xattn_all = _L1_xattn_setup()
    _L1_xattn_in = {k: v for k, v in _L1_xattn_all.items() if k in ('ln1_g', 'ln1_b', 'ln2_g', 'ln2_b', 'Wq', 'bq', 'Wk', 'bk', 'Wv', 'bv', 'Wo', 'bo')}
    del _L1_xattn_all

    def _L1_ffn_setup():
        import jax, jax.numpy as jnp
        import numpy as np
        TOP_K = 4
        key = jax.random.key(seed)
        ks = jax.random.split(key, 6)
        B, S, H, I, E = (2, 128, 128, 128, 16)
        SD = I * 1
        s = 0.02
        return {'hidden_states': jax.random.normal(ks[0], (B, S, H), jnp.float32), 'gate_w': jax.random.normal(ks[1], (E, H), jnp.float32) * s, 'w1': jax.random.normal(ks[2], (E, I, H), jnp.float32) * s, 'w2': jax.random.normal(ks[3], (E, H, I), jnp.float32) * s, 'shared_gu': jax.random.normal(ks[4], (2 * SD, H), jnp.float32) * s, 'shared_down': jax.random.normal(ks[5], (H, SD), jnp.float32) * s}
    _L1_ffn_all = _L1_ffn_setup()
    _L1_ffn_in = {k: v for k, v in _L1_ffn_all.items() if k in ('gate_w', 'w1', 'w2', 'shared_gu', 'shared_down')}
    del _L1_ffn_all

    def _L2_xattn_setup():
        import jax, jax.numpy as jnp
        import numpy as np
        EMBED_DIM = 128
        HIDDEN_DIM = 128
        NUM_HEADS = 16
        CONTEXT_DIM = 96
        HEAD_DIM = EMBED_DIM // NUM_HEADS
        SCALE = HEAD_DIM ** (-0.5)

        def _split_heads(x):
            b, n, _ = x.shape
            return x.reshape(b, n, NUM_HEADS, -1).transpose(0, 2, 1, 3)
        key = jax.random.key(seed)
        ks = jax.random.split(key, 7)
        B, N, M = (4, 512, 128)
        tokens = jax.random.normal(ks[0], (B, N, HIDDEN_DIM), dtype=jnp.float32)
        context = jax.random.normal(ks[1], (B, M, CONTEXT_DIM), dtype=jnp.float32)
        Wq = jax.random.normal(ks[2], (HIDDEN_DIM, EMBED_DIM), dtype=jnp.float32) * HIDDEN_DIM ** (-0.5)
        Wk = jax.random.normal(ks[3], (CONTEXT_DIM, EMBED_DIM), dtype=jnp.float32) * CONTEXT_DIM ** (-0.5)
        Wv = jax.random.normal(ks[4], (CONTEXT_DIM, HIDDEN_DIM), dtype=jnp.float32) * CONTEXT_DIM ** (-0.5)
        Wo = jax.random.normal(ks[5], (HIDDEN_DIM, HIDDEN_DIM), dtype=jnp.float32) * HIDDEN_DIM ** (-0.5)
        bo = jax.random.normal(ks[6], (HIDDEN_DIM,), dtype=jnp.float32) * 0.01
        return {'tokens': tokens, 'context': context, 'Wq': Wq, 'Wk': Wk, 'Wv': Wv, 'Wo': Wo, 'bo': bo}
    _L2_xattn_all = _L2_xattn_setup()
    _L2_xattn_in = {k: v for k, v in _L2_xattn_all.items() if k in ('Wq', 'Wk', 'Wv', 'Wo', 'bo')}
    del _L2_xattn_all

    def _L2_ffn_setup():
        import jax, jax.numpy as jnp
        import numpy as np
        B, S, D = (4, 256, 128)
        E, H, TOP_K = (8, 256, 2)
        key = jax.random.key(seed)
        k_x, k_g, k_w1, k_w2, k_w3 = jax.random.split(key, 5)
        s_d = 1.0 / np.sqrt(D)
        s_h = 1.0 / np.sqrt(H)
        return {'x': jax.random.normal(k_x, (B, S, D), dtype=jnp.float32), 'w_gate': jax.random.normal(k_g, (D, E), dtype=jnp.float32) * s_d, 'w1': jax.random.normal(k_w1, (E, D, H), dtype=jnp.float32) * s_d, 'w3': jax.random.normal(k_w3, (E, D, H), dtype=jnp.float32) * s_d, 'w2': jax.random.normal(k_w2, (E, H, D), dtype=jnp.float32) * s_h}
    _L2_ffn_all = _L2_ffn_setup()
    _L2_ffn_in = {k: v for k, v in _L2_ffn_all.items() if k in ('w_gate', 'w1', 'w3', 'w2')}
    del _L2_ffn_all

    def _L3_xattn_setup():
        import jax, jax.numpy as jnp
        import numpy as np
        N_HEADS = 16
        DIMS = 128
        D_CTX = 96
        HEAD = DIMS // N_HEADS
        key = jax.random.key(seed)
        ks = jax.random.split(key, 10)
        s_q = 1.0 / np.sqrt(DIMS)
        s_c = 1.0 / np.sqrt(D_CTX)
        return {'x': jax.random.normal(ks[0], (2, 256, DIMS), jnp.float32), 'context': jax.random.normal(ks[1], (2, 256, D_CTX), jnp.float32), 'w_q': jax.random.normal(ks[2], (DIMS, DIMS), jnp.float32) * s_q, 'b_q': jax.random.normal(ks[3], (DIMS,), jnp.float32) * 0.01, 'w_k': jax.random.normal(ks[4], (D_CTX, DIMS), jnp.float32) * s_c, 'b_k': jax.random.normal(ks[5], (DIMS,), jnp.float32) * 0.01, 'w_v': jax.random.normal(ks[6], (D_CTX, DIMS), jnp.float32) * s_c, 'b_v': jax.random.normal(ks[7], (DIMS,), jnp.float32) * 0.01, 'w_o': jax.random.normal(ks[8], (DIMS, DIMS), jnp.float32) * s_q, 'b_o': jax.random.normal(ks[9], (DIMS,), jnp.float32) * 0.01}
    _L3_xattn_all = _L3_xattn_setup()
    _L3_xattn_in = {k: v for k, v in _L3_xattn_all.items() if k in ('w_q', 'b_q', 'w_k', 'b_k', 'w_v', 'b_v', 'w_o', 'b_o')}
    del _L3_xattn_all

    def _L3_ffn_setup():
        import jax, jax.numpy as jnp
        import numpy as np
        TOP_K = 2
        key = jax.random.key(seed)
        ks = jax.random.split(key, 5)
        B, S, D, H, E = (2, 256, 128, 352, 8)
        x = jax.random.normal(ks[0], (B, S, D), dtype=jnp.float32)
        Wg = jax.random.normal(ks[1], (E, D), dtype=jnp.float32) * 0.02
        W1 = jax.random.normal(ks[2], (E, H, D), dtype=jnp.float32) * 0.02
        W2 = jax.random.normal(ks[3], (E, H, D), dtype=jnp.float32) * 0.02
        W3 = jax.random.normal(ks[4], (E, D, H), dtype=jnp.float32) * 0.02
        return {'x': x, 'Wg': Wg, 'W1': W1, 'W2': W2, 'W3': W3}
    _L3_ffn_all = _L3_ffn_setup()
    _L3_ffn_in = {k: v for k, v in _L3_ffn_all.items() if k in ('Wg', 'W1', 'W2', 'W3')}
    del _L3_ffn_all
    return {'x': x, 'ctx_768': ctx_768, 'g_xattn': g_xattn, 'g_ffn': g_ffn, 'L0_xattn_Wq': _L0_xattn_in['Wq'], 'L0_xattn_bq': _L0_xattn_in['bq'], 'L0_xattn_Wk': _L0_xattn_in['Wk'], 'L0_xattn_bk': _L0_xattn_in['bk'], 'L0_xattn_Wv': _L0_xattn_in['Wv'], 'L0_xattn_bv': _L0_xattn_in['bv'], 'L0_ffn_w_gate': _L0_ffn_in['w_gate'], 'L0_ffn_w_up': _L0_ffn_in['w_up'], 'L0_ffn_w_down': _L0_ffn_in['w_down'], 'L1_xattn_ln1_g': _L1_xattn_in['ln1_g'], 'L1_xattn_ln1_b': _L1_xattn_in['ln1_b'], 'L1_xattn_ln2_g': _L1_xattn_in['ln2_g'], 'L1_xattn_ln2_b': _L1_xattn_in['ln2_b'], 'L1_xattn_Wq': _L1_xattn_in['Wq'], 'L1_xattn_bq': _L1_xattn_in['bq'], 'L1_xattn_Wk': _L1_xattn_in['Wk'], 'L1_xattn_bk': _L1_xattn_in['bk'], 'L1_xattn_Wv': _L1_xattn_in['Wv'], 'L1_xattn_bv': _L1_xattn_in['bv'], 'L1_xattn_Wo': _L1_xattn_in['Wo'], 'L1_xattn_bo': _L1_xattn_in['bo'], 'L1_ffn_gate_w': _L1_ffn_in['gate_w'], 'L1_ffn_w1': _L1_ffn_in['w1'], 'L1_ffn_w2': _L1_ffn_in['w2'], 'L1_ffn_shared_gu': _L1_ffn_in['shared_gu'], 'L1_ffn_shared_down': _L1_ffn_in['shared_down'], 'L2_xattn_Wq': _L2_xattn_in['Wq'], 'L2_xattn_Wk': _L2_xattn_in['Wk'], 'L2_xattn_Wv': _L2_xattn_in['Wv'], 'L2_xattn_Wo': _L2_xattn_in['Wo'], 'L2_xattn_bo': _L2_xattn_in['bo'], 'L2_ffn_w_gate': _L2_ffn_in['w_gate'], 'L2_ffn_w1': _L2_ffn_in['w1'], 'L2_ffn_w3': _L2_ffn_in['w3'], 'L2_ffn_w2': _L2_ffn_in['w2'], 'L3_xattn_w_q': _L3_xattn_in['w_q'], 'L3_xattn_b_q': _L3_xattn_in['b_q'], 'L3_xattn_w_k': _L3_xattn_in['w_k'], 'L3_xattn_b_k': _L3_xattn_in['b_k'], 'L3_xattn_w_v': _L3_xattn_in['w_v'], 'L3_xattn_b_v': _L3_xattn_in['b_v'], 'L3_xattn_w_o': _L3_xattn_in['w_o'], 'L3_xattn_b_o': _L3_xattn_in['b_o'], 'L3_ffn_Wg': _L3_ffn_in['Wg'], 'L3_ffn_W1': _L3_ffn_in['W1'], 'L3_ffn_W2': _L3_ffn_in['W2'], 'L3_ffn_W3': _L3_ffn_in['W3']}

def reference(x, ctx_768, g_xattn, g_ffn, L0_xattn_Wq, L0_xattn_bq, L0_xattn_Wk, L0_xattn_bk, L0_xattn_Wv, L0_xattn_bv, L0_ffn_w_gate, L0_ffn_w_up, L0_ffn_w_down, L1_xattn_ln1_g, L1_xattn_ln1_b, L1_xattn_ln2_g, L1_xattn_ln2_b, L1_xattn_Wq, L1_xattn_bq, L1_xattn_Wk, L1_xattn_bk, L1_xattn_Wv, L1_xattn_bv, L1_xattn_Wo, L1_xattn_bo, L1_ffn_gate_w, L1_ffn_w1, L1_ffn_w2, L1_ffn_shared_gu, L1_ffn_shared_down, L2_xattn_Wq, L2_xattn_Wk, L2_xattn_Wv, L2_xattn_Wo, L2_xattn_bo, L2_ffn_w_gate, L2_ffn_w1, L2_ffn_w3, L2_ffn_w2, L3_xattn_w_q, L3_xattn_b_q, L3_xattn_w_k, L3_xattn_b_k, L3_xattn_w_v, L3_xattn_b_v, L3_xattn_w_o, L3_xattn_b_o, L3_ffn_Wg, L3_ffn_W1, L3_ffn_W2, L3_ffn_W3):
    import jax
    import jax.numpy as jnp

    def _L0_xattn_ref(query, key, value, Wq, bq, Wk, bk, Wv, bv):
        import jax, jax.numpy as jnp
        import numpy as np
        B, LQ, LK = (4, 256, 256)
        D1, D2, H = (128, 96, 128)
        q = jnp.einsum('bqd,dh->bqh', query, Wq) + bq
        k = jnp.einsum('bkd,dh->bkh', key, Wk) + bk
        v = jnp.einsum('bkd,dh->bkh', value, Wv) + bv
        scores = jnp.einsum('bqh,bkh->bqk', q, k)
        weights = jax.nn.softmax(scores, axis=-1)
        return jnp.einsum('bqk,bkh->bqh', weights, v)

    def _L0_ffn_ref(x, w_gate, w_up, w_down):
        import jax, jax.numpy as jnp
        import numpy as np
        HIDDEN = 128
        INNER = 512

        def _weight_quant(w):
            scale = 1.0 / jnp.clip(jnp.mean(jnp.abs(w)), 1e-05)
            wq = jnp.clip(jnp.round(w * scale), -1.0, 1.0) / scale
            return w + jax.lax.stop_gradient(wq - w)

        def _act_quant(x):
            scale = 127.0 / jnp.clip(jnp.max(jnp.abs(x), axis=-1, keepdims=True), 1e-05)
            xq = jnp.clip(jnp.round(x * scale), -128.0, 127.0) / scale
            return x + jax.lax.stop_gradient(xq - x)

        def _bitlinear(x, w):
            return jnp.einsum('bsi,oi->bso', _act_quant(x), _weight_quant(w))
        gate = jax.nn.silu(_bitlinear(x, w_gate))
        up = _bitlinear(x, w_up)
        return _bitlinear(gate * up, w_down)

    def _L1_xattn_ref(modality1, modality2, ln1_g, ln1_b, ln2_g, ln2_b, Wq, bq, Wk, bk, Wv, bv, Wo, bo):
        import jax, jax.numpy as jnp
        import numpy as np
        EPS = 1e-05

        def layernorm(x, g, b):
            mu = jnp.mean(x, axis=-1, keepdims=True)
            var = jnp.mean(jnp.square(x - mu), axis=-1, keepdims=True)
            return (x - mu) * jax.lax.rsqrt(var + EPS) * g + b
        E = Wq.shape[1]
        scaling = E ** (-0.5)
        x1 = layernorm(modality1, ln1_g, ln1_b)
        x2 = layernorm(modality2, ln2_g, ln2_b)
        q = x1 @ Wq + bq
        k = x2 @ Wk + bk
        v = x2 @ Wv + bv
        scores = jnp.einsum('bqe,bke->bqk', q, k) * scaling
        attn = jax.nn.softmax(scores, axis=-1)
        ctx = jnp.einsum('bqk,bke->bqe', attn, v)
        return ctx @ Wo + bo

    def _L1_ffn_ref(hidden_states, gate_w, w1, w2, shared_gu, shared_down):
        import jax, jax.numpy as jnp
        import numpy as np
        TOP_K = 4
        orig_shape = hidden_states.shape
        H = orig_shape[-1]
        x = hidden_states.reshape(-1, H)
        T = x.shape[0]
        E = gate_w.shape[0]
        logits = x @ gate_w.T
        probs = jax.nn.softmax(logits, axis=-1)
        topv, topi = jax.lax.top_k(probs, TOP_K)
        topv = topv / jnp.sum(topv, axis=-1, keepdims=True)
        W = jnp.zeros((T, E), x.dtype).at[jnp.arange(T)[:, None], topi].set(topv)
        h = jax.nn.silu(jnp.einsum('th,eih->tei', x, w1))
        routed = jnp.einsum('tei,ehi,te->th', h, w2, W)
        gu = x @ shared_gu.T
        gate, up = jnp.split(gu, 2, axis=-1)
        shared = jax.nn.silu(gate) * up @ shared_down.T
        return (routed + shared).reshape(orig_shape)

    def _L2_xattn_ref(tokens, context, Wq, Wk, Wv, Wo, bo):
        import jax, jax.numpy as jnp
        import numpy as np
        EMBED_DIM = 128
        HIDDEN_DIM = 128
        NUM_HEADS = 16
        CONTEXT_DIM = 96
        HEAD_DIM = EMBED_DIM // NUM_HEADS
        SCALE = HEAD_DIM ** (-0.5)

        def _split_heads(x):
            b, n, _ = x.shape
            return x.reshape(b, n, NUM_HEADS, -1).transpose(0, 2, 1, 3)
        Q = _split_heads(tokens @ Wq)
        K = _split_heads(context @ Wk)
        V = _split_heads(context @ Wv)
        scores = jnp.einsum('bhnd,bhmd->bhnm', Q, K) * SCALE
        attn = jax.nn.softmax(scores, axis=-1)
        out = jnp.einsum('bhnm,bhmd->bhnd', attn, V)
        b, h, n, d = out.shape
        out = out.transpose(0, 2, 1, 3).reshape(b, n, h * d)
        return out @ Wo + bo

    def _L2_ffn_ref(x, w_gate, w1, w3, w2):
        import jax, jax.numpy as jnp
        import numpy as np
        B, S, D = (4, 256, 128)
        E, H, TOP_K = (8, 256, 2)
        bsz, seq_len, embed_dim = x.shape
        xt = x.reshape(-1, embed_dim)
        T = xt.shape[0]
        logits = xt @ w_gate
        top_logits, sel = jax.lax.top_k(logits, TOP_K)
        probs = jax.nn.softmax(top_logits, axis=-1).astype(x.dtype)
        h = jax.nn.silu(jnp.einsum('td,edh->eth', xt, w1)) * jnp.einsum('td,edh->eth', xt, w3)
        y = jnp.einsum('eth,ehd->etd', h, w2)
        t_idx = jnp.arange(T)
        yk = y[sel.T, t_idx[None, :], :]
        out = jnp.einsum('ktd,tk->td', yk, probs)
        return out.reshape(bsz, seq_len, embed_dim)

    def _L3_xattn_ref(x, context, w_q, b_q, w_k, b_k, w_v, b_v, w_o, b_o):
        import jax, jax.numpy as jnp
        import numpy as np
        N_HEADS = 16
        DIMS = 128
        D_CTX = 96
        HEAD = DIMS // N_HEADS
        B, Lq, D = x.shape
        q = x @ w_q + b_q
        k = context @ w_k + b_k
        v = context @ w_v + b_v
        q = q.reshape(B, Lq, N_HEADS, HEAD)
        k = k.reshape(B, -1, N_HEADS, HEAD)
        v = v.reshape(B, -1, N_HEADS, HEAD)
        scale = 1.0 / np.sqrt(HEAD).astype(np.float32)
        scores = jnp.einsum('bqhd,bkhd->bhqk', q, k) * scale
        weights = jax.nn.softmax(scores, axis=-1)
        out = jnp.einsum('bhqk,bkhd->bqhd', weights, v).reshape(B, Lq, D)
        return out @ w_o + b_o

    def _L3_ffn_ref(x, Wg, W1, W2, W3):
        import jax, jax.numpy as jnp
        import numpy as np
        TOP_K = 2
        B, S, D = x.shape
        E = Wg.shape[0]
        xt = x.reshape(B * S, D)
        scores = xt @ Wg.T
        topk_scores, topk_idx = jax.lax.top_k(scores, TOP_K)
        gate = jax.nn.silu(jnp.einsum('td,ehd->teh', xt, W1))
        up = jnp.einsum('td,ehd->teh', xt, W2)
        y = jnp.einsum('teh,edh->ted', gate * up, W3)
        onehot = jax.nn.one_hot(topk_idx, E, dtype=x.dtype)
        w = jnp.einsum('tke,tk->te', onehot, topk_scores)
        out = jnp.einsum('te,ted->td', w, y)
        return out.reshape(B, S, D)
    x = x + jnp.tanh(g_xattn[0]) * _L0_xattn_ref(_layernorm(x, axis=-1), ctx_768, ctx_768, L0_xattn_Wq, L0_xattn_bq, L0_xattn_Wk, L0_xattn_bk, L0_xattn_Wv, L0_xattn_bv)
    x = x + jnp.tanh(g_ffn[0]) * _L0_ffn_ref(_layernorm(x, axis=-1), L0_ffn_w_gate, L0_ffn_w_up, L0_ffn_w_down)
    x = x + jnp.tanh(g_xattn[1]) * _L1_xattn_ref(_layernorm(x, axis=-1), ctx_768, L1_xattn_ln1_g, L1_xattn_ln1_b, L1_xattn_ln2_g, L1_xattn_ln2_b, L1_xattn_Wq, L1_xattn_bq, L1_xattn_Wk, L1_xattn_bk, L1_xattn_Wv, L1_xattn_bv, L1_xattn_Wo, L1_xattn_bo)
    x = x + jnp.tanh(g_ffn[1]) * _L1_ffn_ref(_layernorm(x, axis=-1), L1_ffn_gate_w, L1_ffn_w1, L1_ffn_w2, L1_ffn_shared_gu, L1_ffn_shared_down)
    x = x + jnp.tanh(g_xattn[2]) * _L2_xattn_ref(_layernorm(x, axis=-1), ctx_768, L2_xattn_Wq, L2_xattn_Wk, L2_xattn_Wv, L2_xattn_Wo, L2_xattn_bo)
    x = x + jnp.tanh(g_ffn[2]) * _L2_ffn_ref(_layernorm(x, axis=-1), L2_ffn_w_gate, L2_ffn_w1, L2_ffn_w3, L2_ffn_w2)
    x = x + jnp.tanh(g_xattn[3]) * _L3_xattn_ref(_layernorm(x, axis=-1), ctx_768, L3_xattn_w_q, L3_xattn_b_q, L3_xattn_w_k, L3_xattn_b_k, L3_xattn_w_v, L3_xattn_b_v, L3_xattn_w_o, L3_xattn_b_o)
    x = x + jnp.tanh(g_ffn[3]) * _L3_ffn_ref(_layernorm(x, axis=-1), L3_ffn_Wg, L3_ffn_W1, L3_ffn_W2, L3_ffn_W3)
    return x

_drawn_inputs = setup_inputs


def setup_inputs(seed=0):
    import zlib

    import numpy as np

    out = dict(_drawn_inputs(seed))
    spreads = {'L1_xattn_ln1_g': (1.0, 0.2),
     'L1_xattn_ln1_b': (0.0, 0.324),
     'L1_xattn_ln2_g': (1.0, 0.2),
     'L1_xattn_ln2_b': (0.0, 0.1)}
    factors = {'g_ffn': 8.0,
     'L0_xattn_bk': 8.0,
     'L1_xattn_bq': 8.0,
     'L1_xattn_bk': 8.0,
     'L1_xattn_bv': 4.411,
     'L1_xattn_bo': 3.266,
     'L1_ffn_gate_w': 4.294,
     'L1_ffn_w1': 4.295,
     'L1_ffn_w2': 3.855,
     'L1_ffn_shared_gu': 5.82,
     'L1_ffn_shared_down': 6.036,
     'L2_xattn_bo': 4.772,
     'L3_xattn_b_q': 8.0,
     'L3_xattn_b_k': 8.0,
     'L3_xattn_b_v': 8.0,
     'L3_xattn_b_o': 8.0,
     'L3_ffn_Wg': 8.0,
     'L3_ffn_W1': 8.0,
     'L3_ffn_W2': 8.0,
     'L3_ffn_W3': 8.0}
    for name, (base, spread) in spreads.items():
        noise = np.random.default_rng([zlib.crc32(name.encode()), seed]).standard_normal(out[name].shape)
        drawn = base * np.exp(spread * noise) if base else spread * noise
        out[name] = jnp.asarray(drawn.astype(out[name].dtype))
    for name, factor in factors.items():
        out[name] = (out[name] * factor).astype(out[name].dtype)
    return out
```

```python
from contextlib import ExitStack

import numpy as np

import concourse.bass as bass
from concourse import mybir

F32 = mybir.dt.float32
BF16 = mybir.dt.bfloat16
U32 = mybir.dt.uint32
I32 = mybir.dt.int32
ALU = mybir.AluOpType
ACT = mybir.ActivationFunctionType
AX = mybir.AxisListType

P = 128
SEQS, LEN, DIM = 32, 64, 128
CTX = 96
TILES = SEQS * LEN // P
GROUPS = TILES // 4
EPS = 1e-5
HEADS, HEAD = 16, 8
INNER = 512
ROUND = 1.5 * 2.0 ** 23
FAR = -1.0e30
ATT_DEPTH = 6
QFF_DEPTH = 4
ROUTE_DEPTH = 2

C_IDENT, C_HEAD, C_VALUE, C_SEQ, C_IOTA, C_END = 0, 128, 132, 260, 388, 404


def constants():
    c = np.zeros((P, C_END), np.float32)
    row = np.arange(P)
    c[:, C_IDENT:C_HEAD] = np.eye(P)
    c[:, C_HEAD:C_VALUE] = (row[:, None] // HEAD) % 4 == np.arange(4)[None, :]
    c[:, C_VALUE:C_SEQ] = (row[:, None] // LEN) == (row[None, :] // HEAD) % 2
    c[:, C_SEQ:C_IOTA] = np.where(row[:, None] // LEN == row[None, :] // LEN, 0.0, FAR)
    c[:, C_IOTA:C_END] = np.arange(16)[None, :]
    return c


class Tile:

    def __init__(self, pair, r, least_pair):
        self.t = pair * 2 + r
        self.par = r % 2
        self.half = pair + r // 2
        self.least = least_pair * 2 + r


def tile_steps(eng, body, depth):
    def steps(pair, least, ends):
        for r in range(2):
            def at(d, r=r):
                tile = Tile(pair, r - d, least)
                if ends and not 0 <= tile.t < TILES:
                    return None
                return tile
            body(at)

    first = (depth + 3) // 2
    for pair in range(first):
        steps(pair, pair, True)
    with eng.Fori(first, TILES // 2) as pair:
        steps(pair, first, False)
    for pair in range(TILES // 2, (TILES + depth + 1) // 2):
        steps(pair, pair, True)


def build(nc, a, out, stop_after=8):
    with ExitStack() as ctx:
        def sb(name, shape, dt=F32):
            return ctx.enter_context(nc.sbuf_tensor(name, shape, dt))

        def sem(name):
            return ctx.enter_context(nc.semaphore(name))

        x = sb("x", [P, TILES, DIM])
        const = sb("const", [P, C_END])
        ident = const[:, C_IDENT:C_HEAD]
        head_mask = const[:, C_HEAD:C_VALUE]
        value_mask = const[:, C_VALUE:C_SEQ]
        seq_mask = const[:, C_SEQ:C_IOTA]
        iota = const[:, C_IOTA:C_END]
        ident16 = sb("ident16", [P, P], BF16)
        ones = sb("ones", [P, P])
        gates = sb("gates", [P, 8])
        att_w = sb("att_w", [P, 4, 4, P])
        att_col = sb("att_col", [P, 4, 2])
        att_row = sb("att_row", [1, 4, 2, P])
        ln_col = sb("ln_col", [P, 4])
        key_bias4 = sb("key_bias4", [P, 4, 4])
        ctx_nat = sb("ctx_nat", [P, 2, P])
        ctx_norm = sb("ctx_norm", [P, 2, P])
        ctx_all = sb("ctx_all", [P, TILES, CTX])
        xn_all = sb("xn_all", [P, TILES, P])
        stats = sb("stats", [P, TILES, 6])
        moments = sb("moments", [P, 3, TILES, 2])
        rstd = sb("rstd", [P, 3, TILES])
        nr_a = sb("nr_a", [P, TILES])
        nr_i = sb("nr_i", [P, TILES], I32)
        nr_t = sb("nr_t", [P, TILES])
        xn = sb("xn", [P, 2, P])
        xnn = sb("xnn", [P, 2, P])
        inT = sb("inT", [P, 2, 2, P])
        ctx2 = sb("ctx2", [P, 2, 2, 2, LEN])
        qT = sb("qT", [P, 2, P])
        kT = sb("kT", [P, 2, P])
        kx = sb("kx", [P, 2, 2, 4, LEN])
        v1 = sb("v1", [P, 2, P])
        vx = sb("vx", [P, 2, 2, 8, 18])
        top = sb("top", [P, 2, HEADS])
        prob = sb("prob", [P, 2, HEADS * LEN])
        probT = sb("probT", [P, 2, 8, P])
        rsum = sb("rsum", [P, 2, HEADS])
        rinv = sb("rinv", [P, 2, HEADS])
        rgate = sb("rgate", [P, 2])
        on = sb("on", [P, 2, P])
        oT = sb("oT", [P, 2, P])
        q_nat = sb("q_nat", [P, 3, INNER])
        q_tmp = sb("q_tmp", [P, 3, INNER])
        q_int = sb("q_int", [P, 3, INNER], BF16)
        qw = sb("qw", [P, 3, INNER], BF16)
        q_sum = sb("q_sum", [P, 8])
        q_mean = sb("q_mean", [P, 8])
        q_scale = sb("q_scale", [P, 8])
        q_col = sb("q_col", [P, 2, 12])
        xq_t = sb("xq_t", [P, 2, P])
        xq = sb("xq", [P, 2, P], BF16)
        xqT = sb("xqT", [P, 2, P], BF16)
        sil = sb("sil", [P, 2, INNER])
        hid = sb("hid", [P, 2, INNER])
        hq_t = sb("hq_t", [P, 2, INNER])
        hq = sb("hq", [P, 2, INNER], BF16)
        hqT = sb("hqT", [P, 2, 4, P], BF16)
        xT = sb("xT", [P, TILES, P])
        xTs = sb("xTs", [P, 2, P])
        gate_nat = sb("gate_nat", [16, 2, P])
        gate_w = sb("gate_w", [P, 3, 16])
        logit = sb("logit", [P, TILES, 16])
        cent = sb("cent", [P, TILES, 16])
        ex = sb("ex", [P, TILES, 16])
        rmax = sb("rmax", [P, TILES])
        rz = sb("rz", [P, TILES])
        rzi = sb("rzi", [P, TILES])
        best = sb("best", [P, TILES, 8])
        besti = sb("besti", [P, TILES, 8], U32)
        bestf = sb("bestf", [P, TILES, 8])
        wk = sb("wk", [P, TILES, 4])
        hit = sb("hit", [P, TILES, 16])
        hitw = sb("hitw", [P, TILES, 16])
        ew = sb("ew", [P, TILES, 17])
        w_nat = sb("w_nat", [P, 2, 3, 384])
        w_up = sb("w_up", [P, 2, 2, 384])
        w_dn = sb("w_dn", [P, 2, 3, P])
        sg = sb("sg", [P, 2, 512])
        h = sb("h", [P, 2, 3, 512])

        ps = ctx.enter_context(nc.psum_tensor("ps", [P, 8, 512], F32))
        p_score = ps[:, 0:4, 0:256]
        p_oT = ps[:, 4, 0:P]
        p_o = ps[:, 5, 0:144]
        p_in = ps[:, 6, 0:256]
        p_qk = ps[:, 6, 0:256]
        p_v = ps[:, 7, 0:256]
        p_y = ps[:, 7, 0:P]

        setup_loaded = sem("setup_loaded")
        setup_const = sem("setup_const")
        setup_zero = sem("setup_zero")
        setup_pad = sem("setup_pad")
        setup_done = sem("setup_done")
        gates_done = sem("gates_done")
        ctx_loaded = [sem("ctx_loaded0"), sem("ctx_loaded1")]
        ln_link = sem("ln_link")
        xn_ready = sem("xn_ready")
        xnn_ready = sem("xnn_ready")
        xn_all_ready = sem("xn_all_ready")
        in_turned, in_copied = sem("in_turned"), sem("in_copied")
        qk_projected, v_projected = sem("qk_projected"), sem("v_projected")
        qk_copied, v_copied = sem("qk_copied"), sem("v_copied")
        scored, top_ready, centered, exped = sem("scored"), sem("top_ready"), sem("centered"), sem("exped")
        p_turned, p_copied_act, p_copied_dve = sem("p_turned"), sem("p_copied_act"), sem("p_copied_dve")
        attended, sum_inverted, normed = sem("attended"), sem("sum_inverted"), sem("normed")
        o_turned, o_copied, y_done = sem("o_turned"), sem("o_copied"), sem("y_done")
        x_done = sem("x_done")
        qw_step, qw_turned, qw_copied = sem("qw_step"), sem("qw_turned"), sem("qw_copied")
        q_link = sem("q_link")
        q_down = sem("q_down")
        xq_ready, xq_turned, xq_copied = sem("xq_ready"), sem("xq_turned"), sem("xq_copied")
        gu_ready, silu_done, hid_ready = sem("gu_ready"), sem("silu_done"), sem("hid_ready")
        hs_ready, hq_scaled, hq_ready = sem("hs_ready"), sem("hq_scaled"), sem("hq_ready")
        hq_turned, hq_copied = sem("hq_turned"), sem("hq_copied")
        x_turned, x_copied = sem("x_turned"), sem("x_copied")
        gate_turned, gate_copied = sem("gate_turned"), sem("gate_copied")
        logits_done, logits_copied = sem("logits_done"), sem("logits_copied")
        route_link, route_asked, route_exp = sem("route_link"), sem("route_asked"), sem("route_exp")
        w_loaded = [sem("w_loaded0"), sem("w_loaded1")]
        w_turned, w_copied = sem("w_turned"), sem("w_copied")
        units_up, units_silu, units_h = sem("units_up"), sem("units_silu"), sem("units_h")
        moe_y, moe_used = sem("moe_y"), sem("moe_used")
        stored = sem("stored")

        x_d = a["x"].rearrange("(t b) s d -> t (b s) d", b=2)
        ctx_d = a["ctx_768"].rearrange("(t b) s d -> t (b s) d", b=2)
        out_d = out.rearrange("(t b) s d -> (b s) t d", b=2)

        class Moe:
            def __init__(self, layer, experts, shared, pieces, turned):
                self.layer, self.experts, self.shared = layer, experts, shared
                self.pieces, self.turned = pieces, turned
                self.passes = experts + shared
                self.units = 4 * len(pieces)
        MOES = {1: Moe(1, 16, 1, [(0, 128)], True),
                2: Moe(2, 8, 0, [(0, 128), (128, 128)], False),
                3: Moe(3, 8, 0, [(0, 128), (128, 128), (256, 96)], True)}
        base_units, base_passes, base_turned, base_loads = {}, {}, {}, {}
        u = p_ = tn = 0
        for L, m in MOES.items():
            base_units[L], base_passes[L], base_turned[L] = u, p_, tn
            u += m.units * m.passes
            p_ += m.passes
            tn += m.passes if m.turned else 0
        LOADS = {1: 2, 2: 3, 3: 7}
        def loads_of(L, n):
            return 3 if L == 1 and n == 0 else LOADS[L]
        for par in range(2):
            c = 0
            for L, m in MOES.items():
                base_loads[L, par] = c
                c += sum(loads_of(L, n) for n in range(par, m.passes, 2))

        def loads_until(L, n, half):
            extra = 1 if L == 1 and n.par == 0 else 0
            return (half + 1) * LOADS[L] + base_loads[L, n.par] + extra

        def x_ready(eng, sub, tile=None):
            if sub == 0:
                return
            L = (sub - 1) // 2
            if sub % 2 == 0 and L >= 1:
                eng.wait_ge(moe_used, 4 * (base_passes[L] + MOES[L].passes))
            else:
                base = {1: 0, 2: 16, 3: 32, 5: 48, 7: 64}[sub]
                eng.wait_ge(x_done, base + (TILES if tile is None else tile.t + 1))
        xn_base = {0: 0, 1: 16, 3: 32, 4: 48, 5: 64, 6: 80, 7: 96}
        x_done_base = {0: 0, 1: 16, 2: 32, 4: 48, 6: 64}

        class Att:
            def __init__(self, L):
                self.L, self.sub, self.base = L, 2 * L, 16 * L
                self.multi = L >= 2
                self.mbase = 16 * (L - 2)
                self.obase = 16 * (L - 1)
                self.scale = [1.0, P ** -0.5, HEAD ** -0.5, HEAD ** -0.5][L]
                self.bias_v, self.bias_o = L != 2, L >= 1
        ATT = [Att(L) for L in range(4)]

        def free_again(eng, s, base, tile, lag, per=1):
            if base + per * (tile.least - lag + 1) > 0:
                eng.wait_ge(s, base + per * (tile.t - lag + 1))

        def att_sync(sp, A):
            def body(at):
                if (i := at(0)) is not None:
                    free_again(sp, in_turned, A.base, i, 2)
                    sp.dma_start(ctx_nat[:, i.par, 0:CTX], ctx_d[i.t]).then_inc(ctx_loaded[i.par], 16)
            if A.L != 1:
                tile_steps(sp, body, 0)

        def att_vector(dve, A):
            x_ready(dve, A.sub)
            norm_stats(dve, x, 0)
            if A.L == 1:
                for t in range(TILES):
                    ins = dve.tensor_scalar(xn_all[:, t, :], x[:, t, :], moments[:, 0, t, 0:1], rstd[:, 0, t:t + 1],
                                            ALU.subtract, ALU.mult)
                ins.then_inc(xn_all_ready, 1)
                dve.wait_ge(xn_all_ready, 1)
                norm_stats(dve, xn_all, 1)
                norm_stats(dve, ctx_all, 2)

            def body(at):
                if A.L >= 1 and (i := at(6)) is not None:
                    dve.wait_ge(y_done, A.obase + i.t + 1)
                    dve.scalar_tensor_tensor(x[:, i.t, :], p_y, gates[:, A.L:A.L + 1], x[:, i.t, :],
                                             ALU.mult, ALU.add).then_inc(x_done, 1)
                if A.multi and (i := at(4)) is not None:
                    dve.wait_ge(p_turned, A.base + i.t + 1)
                    free_again(dve, attended, A.base, i, 2)
                    dve.tensor_copy(probT[:, i.par, 4:8, :], ps[:, 5, :].rearrange("p (m q) -> p m q", q=P)).then_inc(p_copied_dve, 1)
                if (i := at(0)) is not None:
                    free_again(dve, in_turned, A.base, i, 2)
                    if A.L != 1:
                        norm_tile(dve, A.sub, i)
                    else:
                        r = i.par
                        dve.tensor_scalar(xnn[:, r, :], xn_all[:, i.t, :], moments[:, 1, i.t, 0:1], rstd[:, 1, bass.ds(i.t, 1)],
                                          ALU.subtract, ALU.mult)
                        dve.tensor_scalar(ctx_norm[:, r, 0:CTX], ctx_all[:, i.t, :], moments[:, 2, i.t, 0:1],
                                          rstd[:, 2, bass.ds(i.t, 1)], ALU.subtract, ALU.mult).then_inc(xnn_ready, 1)
                if (i := at(3)) is not None:
                    r = i.par
                    dve.wait_ge(scored, A.base + i.t + 1)
                    free_again(dve, p_turned, A.base, i, 2)
                    if A.multi:
                        sc = p_score.rearrange("p g (n k) -> p g n k", k=LEN)
                        tp = top[:, r, :].rearrange("p (g n) -> p g n", g=4)
                        dve.tensor_reduce(tp, sc, AX.X, ALU.max).then_inc(top_ready, 1)
                        dve.wait_ge(top_ready, A.base + i.t + 1)
                        dve.tensor_tensor(prob[:, r, :].rearrange("p (g n k) -> p g n k", g=4, k=LEN), sc,
                                          tp.unsqueeze(3).broadcast_to([P, 4, 4, LEN]), ALU.subtract).then_inc(centered, 1)
                    else:
                        dve.scalar_tensor_tensor(prob[:, r, 0:P], ps[:, 0, 0:P], A.scale, seq_mask, ALU.mult, ALU.add).then_inc(top_ready, 1)
                        dve.wait_ge(top_ready, A.base + i.t + 1)
                        dve.tensor_reduce(top[:, r, 0:1], prob[:, r, 0:P], AX.X, ALU.max, negate=True).then_inc(centered, 1)
                if (i := at(4)) is not None:
                    r = i.par
                    dve.wait_ge(attended, A.base + i.t + 1)
                    if A.multi:
                        o = p_o.rearrange("p (m c) -> p m c", c=18)
                        dve.reciprocal(rinv[:, r, :].rearrange("p (m j) -> p m j", j=2), o[:, :, 16:18]).then_inc(sum_inverted, 1)
                        free_again(dve, o_turned, A.obase, i, 2)
                        dve.wait_ge(sum_inverted, A.base + i.t + 1)
                        dve.tensor_tensor(on[:, r, :].rearrange("p (m j e) -> p m j e", j=2, e=HEAD),
                                          o[:, :, 0:16].rearrange("p m (j e) -> p m j e", j=2),
                                          rinv[:, r, :].rearrange("p (m j) -> p m j", j=2).unsqueeze(3).broadcast_to([P, 8, 2, HEAD]),
                                          ALU.mult).then_inc(normed, 1)
                    else:
                        dve.reciprocal(rinv[:, r, 0:1], rsum[:, r, 0:1]).then_inc(sum_inverted, 1)
                        dve.wait_ge(sum_inverted, A.base + i.t + 1)
                        if A.L == 0:
                            dve.tensor_scalar(rgate[:, r:r + 1], rinv[:, r, 0:1], gates[:, 0:1], None, ALU.mult).then_inc(normed, 1)
                            dve.wait_ge(normed, A.base + i.t + 1)
                            dve.scalar_tensor_tensor(x[:, i.t, :], ps[:, 5, 0:P], rgate[:, r:r + 1], x[:, i.t, :],
                                                     ALU.mult, ALU.add).then_inc(x_done, 1)
                        else:
                            free_again(dve, o_turned, A.obase, i, 2)
                            dve.tensor_scalar(on[:, r, :], ps[:, 5, 0:P], rinv[:, r, 0:1], None, ALU.mult).then_inc(normed, 1)
                if (i := at(2)) is not None:
                    r = i.par
                    dve.wait_ge(v_projected, A.base + i.t + 1)
                    free_again(dve, attended, A.base, i, 2)
                    if A.multi:
                        for b in range(2):
                            last = dve.tensor_tensor(vx[:, r, b, :, 0:16], p_v[:, P * b:P * b + P].rearrange("p (m c) -> p m c", c=16),
                                                     value_mask.rearrange("p (m c) -> p m c", c=16), ALU.mult)
                        last.then_inc(v_copied, 1)
                    else:
                        dve.tensor_copy(v1[:, r, :], p_v[:, 0:P]).then_inc(v_copied, 1)
            tile_steps(dve, body, ATT_DEPTH)

        ln_links = [0]

        def norm_stats(dve, src, which):
            def linked(ins):
                ln_links[0] += 1
                ins.then_inc(ln_link, 1)
                dve.wait_ge(ln_link, ln_links[0])
            for t in range(TILES):
                ins = dve.bn_stats(stats[:, t, :], src[:, t, :])
            linked(ins)
            for t in range(TILES):
                ins = dve.bn_aggr(moments[:, which, t, :], stats[:, t, :])
            linked(ins)
            root = rstd[:, which, :]
            linked(dve.tensor_scalar(nr_a[:, :], moments[:, which, :, 1], EPS, None, ALU.add))
            linked(dve.tensor_scalar(nr_i[:, :], nr_a[:, :].bitcast(I32), 1, None, ALU.arith_shift_right))
            linked(dve.tensor_scalar(root.bitcast(I32), nr_i[:, :], -1.0, float(0x5F3759DF), ALU.mult, ALU.add))
            for _ in range(3):
                linked(dve.tensor_tensor(nr_t[:, :], nr_a[:, :], root, ALU.mult))
                linked(dve.scalar_tensor_tensor(nr_t[:, :], nr_t[:, :], -0.5, root, ALU.mult, ALU.mult))
                linked(dve.scalar_tensor_tensor(root, nr_t[:, :], 1.5, root, ALU.add, ALU.mult))

        def norm_tile(dve, sub, i):
            dve.tensor_scalar(xn[:, i.par, :], x[:, i.t, :], moments[:, 0, i.t, 0:1], rstd[:, 0, bass.ds(i.t, 1)],
                              ALU.subtract, ALU.mult).then_inc(xn_ready, 1)

        def att_scalar(act, A):
            def body(at):
                if (i := at(1)) is not None:
                    r = i.par
                    act.wait_ge(in_turned, A.base + i.t + 1)
                    free_again(act, v_projected, A.base, i, 2)
                    if A.L == 1:
                        act.activation(inT[:, r, 0, :], p_in[:, 0:P], ACT.Identity, bias=ln_col[:, 1:2], scale=ln_col[:, 0:1])
                        act.activation(inT[:, r, 1, :], p_in[:, P:2 * P], ACT.Identity, bias=ln_col[:, 3:4],
                                       scale=ln_col[:, 2:3]).then_inc(in_copied, 1)
                    elif A.multi:
                        act.copy(inT[:, r, 0, :], p_in[:, 0:P])
                        act.copy(ctx2[:, r, :, :, :], p_in[:, P:2 * P].rearrange("p (b k) -> p b k", b=2).unsqueeze(2)
                                 .broadcast_to([P, 2, 2, LEN])).then_inc(in_copied, 1)
                    else:
                        act.copy(inT[:, r, :, :], p_in.rearrange("p (a q) -> p a q", a=2)).then_inc(in_copied, 1)
                if (i := at(4)) is not None:
                    act.wait_ge(p_turned, A.base + i.t + 1)
                    free_again(act, attended, A.base, i, 2)
                    if A.multi:
                        act.copy(probT[:, i.par, 0:4, :], ps[:, 4, :].rearrange("p (m q) -> p m q", q=P)).then_inc(p_copied_act, 1)
                    else:
                        act.copy(probT[:, i.par, 0, :], ps[:, 4, 0:P]).then_inc(p_copied_act, 1)
                if A.L >= 1 and (i := at(5)) is not None:
                    act.wait_ge(o_turned, A.obase + i.t + 1)
                    free_again(act, y_done, A.obase, i, 2)
                    act.copy(oT[:, i.par, :], p_oT).then_inc(o_copied, 1)
                if (i := at(3)) is not None:
                    r = i.par
                    act.wait_ge(centered, A.base + i.t + 1)
                    if A.multi:
                        act.activation(prob[:, r, :], prob[:, r, :], ACT.Exp, scale=A.scale).then_inc(exped, 1)
                    else:
                        free_again(act, sum_inverted, A.base, i, 2)
                        act.activation(prob[:, r, 0:P], prob[:, r, 0:P], ACT.Exp, bias=top[:, r, 0:1],
                                       accum_out=rsum[:, r, 0:1]).then_inc(exped, 1)
                if (i := at(2)) is not None:
                    r = i.par
                    act.wait_ge(qk_projected, A.base + i.t + 1)
                    free_again(act, scored, A.base, i, 2)
                    act.activation(qT[:, r, :], p_qk[:, 0:P], ACT.Identity, bias=att_col[:, A.L, 0:1])
                    if A.multi:
                        for n in range(4):
                            last = act.activation(kx[:, r, :, n, :], p_qk[:, P:2 * P].rearrange("p (b k) -> p b k", b=2),
                                                  ACT.Identity, bias=key_bias4[:, A.L, n:n + 1], scale=head_mask[:, n:n + 1])
                        last.then_inc(qk_copied, 1)
                    else:
                        act.activation(kT[:, r, :], p_qk[:, P:2 * P], ACT.Identity, bias=att_col[:, A.L, 1:2]).then_inc(qk_copied, 1)
            tile_steps(act, body, ATT_DEPTH)

        def att_tensor(pe, A):
            wq, wk_, wv, wo = (att_w[:, A.L, n, :] for n in range(4))

            def body(at):
                if (i := at(1)) is not None:
                    r = i.par
                    if A.L == 1:
                        pe.wait_ge(xnn_ready, i.t + 1)
                    else:
                        pe.wait_ge(xn_ready, xn_base[A.sub] + i.t + 1)
                        pe.wait_ge(ctx_loaded[r], 16 * (8 * (A.L - (A.L > 1)) + i.half + 1))
                    free_again(pe, qk_copied, A.base, i, 2)
                    free_again(pe, in_copied, A.base, i, 1)
                    pe.transpose(p_in[:, 0:P], (xnn if A.L == 1 else xn)[:, r, :], ident)
                    pe.transpose(p_in[:, P:2 * P], (ctx_norm if A.L == 1 else ctx_nat)[:, r, :], ident).then_inc(in_turned, 1)
                if A.L >= 1 and (i := at(6)) is not None:
                    pe.wait_ge(o_copied, A.obase + i.t + 1)
                    v = at(3)
                    pe.wait_ge(v_copied, A.base + (v.t + 1 if v is not None else TILES))
                    free_again(pe, x_done, x_done_base[A.sub], i, 1)
                    pe.matmul(p_y, oT[:, i.par, :], wo, start=True, stop=False)
                    pe.matmul(p_y, ones[0:1, :], att_row[0:1, A.L, 1, :], start=False, stop=True).then_inc(y_done, 1)
                if (i := at(4)) is not None:
                    r = i.par
                    pe.wait_ge(exped, A.base + i.t + 1)
                    if A.L >= 1:
                        free_again(pe, o_copied, A.obase, i, 2)
                    free_again(pe, p_copied_act, A.base, i, 1)
                    if A.multi:
                        free_again(pe, normed, A.base, i, 1)
                        for m in range(8):
                            last = pe.transpose(ps[:, 4 + m // 4, P * (m % 4):P * (m % 4) + P], prob[:, r, P * m:P * m + P], ident)
                    else:
                        last = pe.transpose(ps[:, 4, 0:P], prob[:, r, 0:P], ident)
                    last.then_inc(p_turned, 1)
                if (i := at(3)) is not None:
                    r = i.par
                    pe.wait_ge(qk_copied, A.base + i.t + 1)
                    free_again(pe, centered if A.multi else top_ready, A.base, i, 1)
                    if A.multi:
                        for b in range(2):
                            for g in range(4):
                                rows = slice(32 * g, 32 * g + 32)
                                last = pe.matmul(ps[LEN * b:LEN * b + LEN, g, 0:256], qT[rows, r, LEN * b:LEN * b + LEN],
                                                 kx[rows, r, b, :, :].rearrange("p n k -> p (n k)"), start=True, stop=True)
                    else:
                        last = pe.matmul(ps[:, 0, 0:P], qT[:, r, :], kT[:, r, :], start=True, stop=True)
                    last.then_inc(scored, 1)
                if A.L >= 1 and (i := at(5)) is not None:
                    pe.wait_ge(normed, A.base + i.t + 1)
                    p = at(4)
                    pe.wait_ge(p_copied_act, A.base + (p.t + 1 if p is not None else TILES))
                    free_again(pe, o_copied, A.obase, i, 1)
                    pe.transpose(p_oT, on[:, i.par, :], ident).then_inc(o_turned, 1)
                if (i := at(4)) is not None:
                    r = i.par
                    pe.wait_ge(p_copied_act, A.base + i.t + 1)
                    pe.wait_ge(v_copied, A.base + i.t + 1)
                    if A.multi:
                        pe.wait_ge(p_copied_dve, A.mbase + i.t + 1)
                        for b in range(2):
                            for m in range(8):
                                last = pe.matmul(p_o[LEN * b:LEN * b + LEN, 18 * m:18 * m + 18],
                                                 probT[:, r, m, LEN * b:LEN * b + LEN], vx[:, r, b, m, :], start=True, stop=True)
                    else:
                        free_again(pe, x_done if A.L == 0 else normed, A.base, i, 1)
                        last = pe.matmul(ps[:, 5, 0:P], probT[:, r, 0, :], v1[:, r, :], start=True, stop=True)
                    last.then_inc(attended, 1)
                if (i := at(2)) is not None:
                    r = i.par
                    n = at(1)
                    pe.wait_ge(in_copied, A.base + (n.t + 1 if n is not None else TILES))
                    free_again(pe, qk_copied, A.base, i, 1)
                    pe.matmul(p_qk[:, 0:P], wq, inT[:, r, 0, :], start=True, stop=True)
                    keys = ctx2[:, r, :, 0, :] if A.multi else inT[:, r, 1, :]
                    pe.matmul(p_qk[:, P:2 * P], wk_, keys, start=True, stop=True).then_inc(qk_projected, 1)
                    free_again(pe, v_copied, A.base, i, 1)
                    if A.L >= 1:
                        free_again(pe, x_done, x_done_base[A.sub], i, 4)
                    for b in range(2 if A.multi else 1):
                        to = p_v[:, P * b:P * b + P]
                        if A.multi:
                            keys = ctx2[:, r, b, :, :].rearrange("p j k -> p (j k)")
                        last = pe.matmul(to, keys, wv, start=True, stop=not A.bias_v)
                        if A.bias_v:
                            last = pe.matmul(to, ones[0:1, :], att_row[0:1, A.L, 0, :], start=False, stop=True)
                    last.then_inc(v_projected, 1)
            x_ready(pe, A.sub)
            tile_steps(pe, body, ATT_DEPTH)

        Q_G, Q_U, Q_T, Q_Y = (0, 1), (2, 3), 4, 6
        p16 = ps[:, 4:6, :].rearrange("p b n -> p (b n)").bitcast(BF16)
        p_xq = p16[:, 0:P]
        p_hq = p16[:, 1024:1024 + 512]

        def qff_prepare_vector(dve):
            link = [0]

            def linked(ins):
                link[0] += 1
                ins.then_inc(qw_step, 1)
                dve.wait_ge(qw_step, link[0])
            dve.wait_ge(setup_loaded, SETUP)
            linked(dve.tensor_reduce(q_sum[:, 0:3], q_nat[:, :, :], AX.X, ALU.add, apply_absolute_value=True))
            dve.wait_ge(qw_turned, 1)
            linked(dve.tensor_scalar(q_mean[:, 0:3], ps[:, 7, 0:3], 1.0 / (INNER * DIM), EPS, ALU.mult, ALU.max))
            linked(dve.reciprocal(q_scale[:, 0:3], q_mean[:, 0:3]))
            for n in range(3):
                linked(dve.tensor_scalar(q_tmp[:, n, :], q_nat[:, n, :], q_scale[:, n:n + 1], 1.0, ALU.mult, ALU.min))
                linked(dve.tensor_scalar(q_tmp[:, n, :], q_tmp[:, n, :], -1.0, ROUND, ALU.max, ALU.add))
                linked(dve.tensor_scalar(q_int[:, n, :], q_tmp[:, n, :], -ROUND, None, ALU.add))
            dve.wait_ge(gates_done, 1)
            linked(dve.tensor_scalar(q_mean[:, 4:7], q_mean[:, 0:3], 1.0 / 127.0, None, ALU.mult))
            linked(dve.tensor_scalar(q_mean[:, 6:7], q_mean[:, 6:7], gates[:, 4:5], None, ALU.mult))
            assert link[0] == QW_LINKS

        QW_LINKS = 14

        def qff_vector(dve):
            qff_prepare_vector(dve)
            x_ready(dve, 1)
            norm_stats(dve, x, 0)
            base = 16

            def body(at):
                if (i := at(3)) is not None:
                    r = i.par
                    dve.wait_ge(hq_scaled, i.t + 1)
                    free_again(dve, hq_turned, 0, i, 2)
                    dve.tensor_scalar(hq[:, r, :], hq_t[:, r, :], -ROUND, None, ALU.add).then_inc(hq_ready, 1)
                if (i := at(4)) is not None:
                    dve.wait_ge(q_down, i.t + 1)
                    dve.scalar_tensor_tensor(x[:, i.t, :], ps[:, Q_Y + i.par, 0:P], q_col[:, i.par, 10:11], x[:, i.t, :],
                                             ALU.mult, ALU.add).then_inc(x_done, 1)
                if (i := at(2)) is not None:
                    r, n = i.par, i.t
                    dve.wait_ge(silu_done, i.t + 1)
                    dve.scalar_tensor_tensor(hid[:, r, :], ps[:, Q_U[r], :], q_col[:, r, 5:6], sil[:, r, :],
                                             ALU.mult, ALU.mult).then_inc(hid_ready, 1)
                    dve.wait_ge(hid_ready, i.t + 1)
                    dve.tensor_reduce(q_col[:, r, 6:7], hid[:, r, :], AX.X, ALU.max, apply_absolute_value=True).then_inc(q_link, 1)
                    dve.wait_ge(q_link, base_link(i, 2, 1))
                    dve.tensor_scalar(q_col[:, r, 7:8], q_col[:, r, 6:7], EPS, None, ALU.max).then_inc(q_link, 1)
                    dve.wait_ge(q_link, base_link(i, 2, 2))
                    dve.reciprocal(q_col[:, r, 8:9], q_col[:, r, 7:8]).then_inc(q_link, 1)
                    dve.wait_ge(q_link, base_link(i, 2, 3))
                    dve.tensor_scalar(q_col[:, r, 9:10], q_col[:, r, 8:9], 127.0, None, ALU.mult).then_inc(hs_ready, 1)
                    dve.tensor_scalar(q_col[:, r, 10:11], q_col[:, r, 7:8], q_mean[:, 6:7], None, ALU.mult).then_inc(hs_ready, 1)
                if (i := at(0)) is not None:
                    r = i.par
                    norm_tile(dve, 1, i)
                    dve.wait_ge(xn_ready, base + i.t + 1)
                    dve.tensor_reduce(q_col[:, r, 0:1], xn[:, r, :], AX.X, ALU.max, apply_absolute_value=True).then_inc(xq_link[0], 1)
                    dve.wait_ge(xq_link[0], i.t + 1)
                    dve.tensor_scalar(q_col[:, r, 1:2], q_col[:, r, 0:1], EPS, None, ALU.max).then_inc(xq_link[1], 1)
                    dve.wait_ge(xq_link[1], i.t + 1)
                    dve.reciprocal(q_col[:, r, 2:3], q_col[:, r, 1:2]).then_inc(xq_link[2], 1)
                    dve.wait_ge(xq_link[2], i.t + 1)
                    dve.tensor_scalar(q_col[:, r, 3:4], q_col[:, r, 2:3], 127.0, None, ALU.mult).then_inc(xq_link[3], 1)
                    free_again(dve, hid_ready, 0, i, 2)
                    dve.wait_ge(xq_link[3], i.t + 1)
                    dve.tensor_scalar(xq_t[:, r, :], xn[:, r, :], q_col[:, r, 3:4], ROUND, ALU.mult, ALU.add).then_inc(xq_link[4], 1)
                    dve.tensor_scalar(q_col[:, r, 4:6], q_mean[:, 4:6], q_col[:, r, 1:2], None, ALU.mult)
                    free_again(dve, xq_turned, 0, i, 2)
                    dve.wait_ge(xq_link[4], i.t + 1)
                    dve.tensor_scalar(xq[:, r, :], xq_t[:, r, :], -ROUND, None, ALU.add).then_inc(xq_ready, 1)
            tile_steps(dve, body, QFF_DEPTH)

        def base_link(i, lag, n):
            return 3 * i.t + n

        xq_link = [sem(f"xq_link{n}") for n in range(5)]

        def qff_scalar(act):
            for n in range(3):
                act.wait_ge(qw_turned, n + 2)
                act.copy(qw[:, n, :], p16[:, 1024 * (n % 2):1024 * (n % 2) + 512]).then_inc(qw_copied, 1)

            def body(at):
                if (i := at(3)) is not None:
                    act.wait_ge(hq_turned, i.t + 1)
                    free_again(act, q_down, 0, i, 2)
                    act.copy(hqT[:, i.par, :, :], p_hq.rearrange("p (c q) -> p c q", q=P)).then_inc(hq_copied, 1)
                if (i := at(1)) is not None:
                    act.wait_ge(xq_turned, i.t + 1)
                    free_again(act, gu_ready, 0, i, 2)
                    act.copy(xqT[:, i.par, :], p_xq).then_inc(xq_copied, 1)
                if (i := at(2)) is not None:
                    r = i.par
                    act.wait_ge(gu_ready, i.t + 1)
                    free_again(act, hid_ready, 0, i, 2)
                    act.activation(sil[:, r, :], ps[:, Q_G[r], :], ACT.Silu, scale=q_col[:, r, 4:5]).then_inc(silu_done, 1)
                if (i := at(2)) is not None:
                    r = i.par
                    act.wait_ge(hs_ready, 2 * i.t + 2)
                    free_again(act, hq_ready, 0, i, 2)
                    act.activation(hq_t[:, r, :], hid[:, r, :], ACT.Identity, bias=round_col[:, 0:1], scale=q_col[:, r, 9:10]).then_inc(hq_scaled, 1)
            tile_steps(act, body, QFF_DEPTH)

        round_col = sb("round_col", [P, 1])

        def qff_tensor(pe):
            x_ready(pe, 1)
            pe.wait_ge(qw_step, 1)
            pe.wait_ge(setup_zero, 2)
            pe.matmul(ps[:, 7, 0:4], ones[:, :], q_sum[:, 0:4], start=True, stop=True).then_inc(qw_turned, 1)
            for n in range(3):
                pe.wait_ge(qw_step, 3 + 3 * n + 3)
                if n == 2:
                    pe.wait_ge(qw_copied, 1)
                for c in range(4):
                    src = q_int[:, n, P * c:P * c + P]
                    last = pe.transpose(p16[:, 1024 * (n % 2) + P * c:1024 * (n % 2) + P * c + P], src, ident16[:, :])
                last.then_inc(qw_turned, 1)
            pe.wait_ge(qw_copied, 3)

            def body(at):
                if (i := at(1)) is not None:
                    pe.wait_ge(xq_ready, i.t + 1)
                    free_again(pe, xq_copied, 0, i, 1)
                    pe.transpose(p_xq, xq[:, i.par, :], ident16[:, :]).then_inc(xq_turned, 1)
                if (i := at(3)) is not None:
                    pe.wait_ge(hq_ready, i.t + 1)
                    free_again(pe, hq_copied, 0, i, 1)
                    for c in range(4):
                        last = pe.transpose(p_hq[:, P * c:P * c + P], hq[:, i.par, P * c:P * c + P], ident16[:, :])
                    last.then_inc(hq_turned, 1)
                if (i := at(2)) is not None:
                    r = i.par
                    pe.wait_ge(xq_copied, i.t + 1)
                    free_again(pe, hid_ready, 0, i, 2)
                    pe.matmul(ps[:, Q_G[r], :], xqT[:, r, :], qw[:, 0, :], start=True, stop=True)
                    pe.matmul(ps[:, Q_U[r], :], xqT[:, r, :], qw[:, 1, :], start=True, stop=True).then_inc(gu_ready, 1)
                if (i := at(4)) is not None:
                    r = i.par
                    pe.wait_ge(hq_copied, i.t + 1)
                    free_again(pe, x_done, 16, i, 2)
                    for c in range(4):
                        last = pe.matmul(ps[:, Q_Y + r, 0:P], hqT[:, r, c, :], qw[:, 2, P * c:P * c + P], start=(c == 0), stop=(c == 3))
                    last.then_inc(q_down, 1)
            tile_steps(pe, body, QFF_DEPTH)

        BANK_T, BANK_G, BANK_U, BANK_Y = 0, (2, 3), (4, 5), (6, 7)

        class Pass:

            def __init__(self, n, par, half, least):
                self.n, self.par, self.half, self.least = n, par, half, least

            def next(self):
                return Pass(self.n + 1, 1 - self.par, self.half + self.par, self.least + 1)

        def expert_passes(eng, M, body):
            def fixed(n):
                body(Pass(n, n % 2, n // 2, n), n + 1 < M.passes)
            fixed(0)
            fixed(1)
            ends = (M.passes - 1) // 2
            with eng.Fori(1, ends) as pair:
                for r in range(2):
                    body(Pass(pair * 2 + r, r, pair, 2 + r), True)
            for n in range(2 * ends, M.passes):
                fixed(n)

        def weights_sync(sp, M, n, more=True):
            L, r = M.layer, n.par
            if L == 2:
                wait_free(sp, moe_y, 4 * base_passes[L], 4, n)
                for k, name in enumerate(("L2_ffn_w1", "L2_ffn_w3")):
                    sp.dma_start(w_up[:, r, k, 0:256], a[name][n.n]).then_inc(w_loaded[r], 16)
                sp.dma_start(w_dn[:, r, 0:2, :], a["L2_ffn_w2"][n.n].rearrange("(c p) d -> p c d", p=P)).then_inc(w_loaded[r], 16)
                return
            if L == 3 and n.least >= 2:
                wait_free(sp, w_turned2, 0, 1, n)
            else:
                wait_free(sp, w_turned, base_turned[L], 1, n)
            if L == 1:
                if isinstance(n.n, int) and n.n == 0:
                    gu = a["L1_ffn_shared_gu"]
                    sp.dma_start(w_nat[:, r, 0, 0:P], gu[0:P, :]).then_inc(w_loaded[r], 16)
                    sp.dma_start(w_nat[:, r, 1, 0:P], gu[P:2 * P, :]).then_inc(w_loaded[r], 16)
                    sp.dma_start(w_nat[:, r, 2, 0:P], a["L1_ffn_shared_down"]).then_inc(w_loaded[r], 16)
                else:
                    sp.dma_start(w_nat[:, r, 0, 0:P], a["L1_ffn_w1"][n.n - 1]).then_inc(w_loaded[r], 16)
                    sp.dma_start(w_nat[:, r, 2, 0:P], a["L1_ffn_w2"][n.n - 1]).then_inc(w_loaded[r], 16)
                return
            for k, name in enumerate(("L3_ffn_W1", "L3_ffn_W2")):
                for c, (off, size) in enumerate(M.pieces):
                    sp.dma_start(w_nat[0:size, r, k, P * c:P * c + P], a[name][n.n, off:off + size, :]).then_inc(w_loaded[r], 16)
            sp.dma_start(w_nat[:, r, 2, 0:352], a["L3_ffn_W3"][n.n]).then_inc(w_loaded[r], 16)

        def wait_free(eng, s, base, per, n, lag=2):
            if base + per * (n.least - lag + 1) > 0:
                eng.wait_ge(s, base + per * (n.n - lag + 1))

        def moe_sync(sp, M):
            L = M.layer
            if L == 2:
                sp.wait_ge(moe_y, 4 * base_passes[2])
                sp.wait_ge(w_copied, base_turned[2])
            expert_passes(sp, M, lambda n, more: weights_sync(sp, M, n))

        def turn_weights(pe, M, n):
            L, r = M.layer, n.par
            if not M.turned:
                return
            pe.wait_ge(w_loaded[r], 16 * loads_until(L, n, n.half))
            wait_free(pe, w_copied, base_turned[L], 1, n, 1)
            shared = L == 1 and isinstance(n.n, int) and n.n == 0
            if L == 3:
                for k in range(2):
                    for c, (off, size) in enumerate(M.pieces):
                        pe.transpose(ps[:, BANK_T + k, off:off + size], w_nat[0:size, r, k, P * c:P * c + P], ident[0:size, 0:size])
                last = pe.transpose(ps[:, BANK_T, 352:480], w_nat[:, r, 2, 0:P], ident)
                last = pe.transpose(ps[:, BANK_T + 1, 352:480], w_nat[:, r, 2, P:2 * P], ident)
                last.then_inc(w_turned, 1)
            else:
                last = pe.transpose(ps[:, BANK_T, 0:P], w_nat[:, r, 0, 0:P], ident)
                if shared:
                    last = pe.transpose(ps[:, BANK_T, P:2 * P], w_nat[:, r, 1, 0:P], ident)
                last = pe.transpose(ps[:, BANK_T + 1, 0:P], w_nat[:, r, 2, 0:P], ident)
                last.then_inc(w_turned, 1)

        def moe_tensor(pe, M):
            L, nc_ = M.layer, len(M.pieces)
            ub, yb, sub = base_units[L], 4 * base_passes[L], 2 * L + 1
            x_ready(pe, sub)
            if L != 2:
                k = 0 if L == 1 else 1
                pe.wait_ge(setup_loaded, SETUP)
                pe.transpose(ps[:, 7, 0:16], gate_nat[:, k, :], ident[0:16, 0:16]).then_inc(gate_turned, 1)
                pe.wait_ge(gate_copied, k + 1)

            def route(at):
                if (i := at(1)) is not None:
                    pe.wait_ge(xn_ready, xn_base[sub] + i.t + 1)
                    free_again(pe, x_copied, 16 * (L - 1), i, 2)
                    pe.transpose(ps[:, BANK_G[i.par], 0:P], xn[:, i.par, :], ident).then_inc(x_turned, 1)
                if (i := at(2)) is not None:
                    pe.wait_ge(x_copied, 16 * (L - 1) + i.t + 1)
                    free_again(pe, logits_copied, 16 * (L - 1), i, 2)
                    pe.matmul(ps[:, BANK_Y[i.par], 0:16], xTs[:, i.par, :], gate_w[:, L - 1, :], start=True, stop=True).then_inc(logits_done, 1)
            tile_steps(pe, route, ROUTE_DEPTH)
            turn_weights(pe, M, Pass(0, 0, 0, 0))
            pe.wait_ge(logits_copied, 16 * L)

            def body(n, more):
                r = n.par
                if M.turned:
                    pe.wait_ge(w_copied, base_turned[L] + n.n + 1)
                else:
                    pe.wait_ge(w_loaded[r], 16 * loads_until(L, n, n.half))
                up = L != 1 or (isinstance(n.n, int) and n.n == 0)

                def down(g):
                    pe.wait_ge(units_h, ub + M.units * n.n + nc_ * (g + 1))
                    wait_free_group(pe, moe_used, yb, n, g, 2)
                    for j in range(4):
                        for c, (off, size) in enumerate(M.pieces):
                            last = pe.matmul(ps[:, BANK_Y[g % 2], P * j:P * j + P], h[0:size, g % 2, c, P * j:P * j + P],
                                             w_dn[0:size, r, c, :], start=(c == 0), stop=(c == nc_ - 1))
                    last.then_inc(moe_y, 1)

                for g in range(4):
                    for c, (off, size) in enumerate(M.pieces):
                        k = g * nc_ + c
                        if ub + M.units * n.least + k - 1 > ub:
                            pe.wait_ge(units_h, ub + M.units * n.n + k - 1)
                        s = k % 2
                        rhs = xT[:, 4 * g:4 * g + 4, :].rearrange("p t q -> p (t q)")
                        last = pe.matmul(ps[0:size, BANK_G[s], :], w_up[:, r, 0, off:off + size], rhs, start=True, stop=True)
                        if up:
                            last = pe.matmul(ps[0:size, BANK_U[s], :], w_up[:, r, 1, off:off + size], rhs, start=True, stop=True)
                        last.then_inc(units_up, 1)
                    if g:
                        down(g - 1)
                if more:
                    turn_weights(pe, M, n.next())
                down(3)
            expert_passes(pe, M, body)

        def wait_free_group(eng, s, base, n, g, lag):
            if base + 4 * n.least + g - lag + 1 > 0:
                eng.wait_ge(s, base + 4 * n.n + g - lag + 1)

        def moe_scalar(act, M):
            L, nc_ = M.layer, len(M.pieces)
            ub, yb = base_units[L], 4 * base_passes[L]
            if L != 2:
                k = 0 if L == 1 else 1
                act.wait_ge(gate_turned, k + 1)
                act.copy(gate_w[:, L - 1, :], ps[:, 7, 0:16]).then_inc(gate_copied, 1)

            def route(at):
                if (i := at(1)) is not None:
                    act.wait_ge(x_turned, 16 * (L - 1) + i.t + 1)
                    free_again(act, logits_done, 16 * (L - 1), i, 2)
                    act.copy(xT[:, i.t, :], ps[:, BANK_G[i.par], 0:P])
                    act.copy(xTs[:, i.par, :], ps[:, BANK_G[i.par], 0:P]).then_inc(x_copied, 1)
                if (i := at(2)) is not None:
                    act.wait_ge(logits_done, 16 * (L - 1) + i.t + 1)
                    act.copy(logit[:, i.t, :], ps[:, BANK_Y[i.par], 0:16]).then_inc(logits_copied, 1)
            tile_steps(act, route, ROUTE_DEPTH)
            copy_weights(act, M, Pass(0, 0, 0, 0))
            if L < 3:
                act.wait_ge(route_asked, L)
                if L == 1:
                    act.activation(ex[:, :, :], cent[:, :, :], ACT.Exp).then_inc(route_exp, 1)
                else:
                    act.activation(rz[:, :], rmax[:, :], ACT.Tanh, scale=0.5).then_inc(route_exp, 1)

            def body(n, more):
                r = n.par
                up = L != 1 or (isinstance(n.n, int) and n.n == 0)
                for g in range(4):
                    for c, (off, size) in enumerate(M.pieces):
                        k = g * nc_ + c
                        act.wait_ge(units_up, ub + M.units * n.n + k + 1)
                        if up:
                            if ub + M.units * n.least + k - 1 > 0:
                                act.wait_ge(units_h, ub + M.units * n.n + k - 1)
                            act.activation(sg[0:size, k % 2, :], ps[0:size, BANK_G[k % 2], :], ACT.Silu).then_inc(units_silu, 1)
                        else:
                            wait_free_group(act, moe_y, yb, n, g, 2)
                            act.activation(h[0:size, g % 2, c, :], ps[0:size, BANK_G[k % 2], :], ACT.Silu).then_inc(units_h, 1)
                if more:
                    copy_weights(act, M, n.next())
            expert_passes(act, M, body)

        def copy_weights(act, M, n):
            L, r = M.layer, n.par
            if not M.turned:
                return
            act.wait_ge(w_turned, base_turned[L] + n.n + 1)
            wait_free(act, moe_y, 4 * base_passes[L], 4, n)
            if L == 3:
                act.copy(w_up[:, r, 0, 0:352], ps[:, BANK_T, 0:352])
                act.copy(w_up[:, r, 1, 0:352], ps[:, BANK_T + 1, 0:352])
                act.copy(w_dn[:, r, 0:2, :], ps[:, BANK_T:BANK_T + 2, 352:480]).then_inc(w_part, 1)
                act.wait_ge(w_turned2, n.n + 1)
                act.copy(w_dn[0:96, r, 2, :], ps[0:96, BANK_T, 0:P]).then_inc(w_copied, 1)
            else:
                wide = 256 if isinstance(n.n, int) and n.n == 0 else 128
                if wide == 256:
                    act.copy(w_up[:, r, 0:2, 0:P], ps[:, BANK_T, 0:256].rearrange("p (k q) -> p k q", k=2))
                else:
                    act.copy(w_up[:, r, 0, 0:P], ps[:, BANK_T, 0:P])
                act.copy(w_dn[:, r, 0, :], ps[:, BANK_T + 1, 0:P]).then_inc(w_copied, 1)

        w_part, w_turned2 = sem("w_part"), sem("w_turned2")

        plain_turn = turn_weights

        def turn_weights(pe, M, n):
            plain_turn(pe, M, n)
            if M.layer == 3:
                pe.wait_ge(w_part, n.n + 1)
                pe.transpose(ps[0:96, BANK_T, 0:P], w_nat[:, n.par, 2, 256:352], ident).then_inc(w_turned2, 1)

        def moe_vector(dve, M):
            L, nc_ = M.layer, len(M.pieces)
            ub, yb, sub = base_units[L], 4 * base_passes[L], 2 * L + 1
            K, E = {1: 4, 2: 2, 3: 2}[L], M.experts

            x_ready(dve, sub)
            norm_stats(dve, x, 0)

            def norm(at):
                if (i := at(0)) is not None:
                    free_again(dve, x_turned, 16 * (L - 1), i, 2)
                    norm_tile(dve, sub, i)
            tile_steps(dve, norm, 0)

            link = [link_base[L]]

            def linked(ins):
                link[0] += 1
                ins.then_inc(route_link, 1)
                dve.wait_ge(route_link, link[0])
            dve.wait_ge(logits_copied, 16 * L)
            wide = lambda col, n: col.unsqueeze(2).broadcast_to([P, TILES, n])
            if L == 1:
                linked(dve.tensor_reduce(rmax[:, :], logit[:, :, :], AX.X, ALU.max))
                dve.tensor_tensor(cent[:, :, :], logit[:, :, :], wide(rmax[:, :], 16), ALU.subtract).then_inc(route_asked, 1)
                dve.wait_ge(route_exp, 1)
                linked(dve.tensor_reduce(rz[:, :], ex[:, :, :], AX.X, ALU.add))
                linked(dve.reciprocal(rzi[:, :], rz[:, :]))
                linked(dve.tensor_tensor(logit[:, :, :], ex[:, :, :], wide(rzi[:, :], 16), ALU.mult))
            for t in range(TILES):
                ins = dve.max(best[:, t, :], logit[:, t, 0:E])
            linked(ins)
            for t in range(TILES):
                ins = dve.max_index(besti[:, t, :], best[:, t, :], logit[:, t, 0:E])
            linked(ins)
            linked(dve.tensor_copy(bestf[:, :, :], besti[:, :, :]))
            gate = gates[:, 4 + L:5 + L]
            if L == 1:
                linked(dve.tensor_reduce(rz[:, :], best[:, :, 0:4], AX.X, ALU.add))
                linked(dve.reciprocal(rzi[:, :], rz[:, :]))
                linked(dve.tensor_scalar(rz[:, :], rzi[:, :], gate, None, ALU.mult))
                linked(dve.tensor_tensor(wk[:, :, :], best[:, :, 0:4], wide(rz[:, :], 4), ALU.mult))
            elif L == 2:
                dve.tensor_tensor(rmax[:, :], best[:, :, 0], best[:, :, 1], ALU.subtract).then_inc(route_asked, 1)
                dve.wait_ge(route_exp, 2)
                linked(dve.tensor_scalar(wk[:, :, 0], rz[:, :], 0.5, 0.5, ALU.mult, ALU.add))
                linked(dve.tensor_scalar(wk[:, :, 1], rz[:, :], -0.5, 0.5, ALU.mult, ALU.add))
                linked(dve.tensor_scalar(wk[:, :, 0:2], wk[:, :, 0:2], gate, None, ALU.mult))
            else:
                linked(dve.tensor_scalar(wk[:, :, 0:2], best[:, :, 0:2], gate, None, ALU.mult))
            first = M.shared
            dst = ew[:, :, first:first + E]
            for k in range(K):
                number = iota[:, 0:E].unsqueeze(1).broadcast_to([P, TILES, E])
                linked(dve.tensor_tensor(hit[:, :, 0:E], number, wide(bestf[:, :, k], E), ALU.is_equal))
                if k == 0:
                    linked(dve.tensor_tensor(dst, hit[:, :, 0:E], wide(wk[:, :, k], E), ALU.mult))
                else:
                    linked(dve.tensor_tensor(hitw[:, :, 0:E], hit[:, :, 0:E], wide(wk[:, :, k], E), ALU.mult))
                    linked(dve.tensor_tensor(dst, dst, hitw[:, :, 0:E], ALU.add))
            if M.shared:
                linked(dve.tensor_scalar(ew[:, :, 0], ew[:, :, 1], 0.0, gate, ALU.mult, ALU.add))
            link_base[L + 1] = link[0]

            def body(n, more):
                up = L != 1 or (isinstance(n.n, int) and n.n == 0)

                def add(g):
                    dve.wait_ge(moe_y, yb + 4 * n.n + g + 1)
                    wait_free(dve, moe_used, yb + g, 4, n, 1) if n.least else None
                    for j in range(4):
                        t = 4 * g + j
                        last = dve.scalar_tensor_tensor(x[:, t, :], ps[:, BANK_Y[g % 2], P * j:P * j + P], ew[:, t, bass.ds(n.n, 1)],
                                                        x[:, t, :], ALU.mult, ALU.add)
                    last.then_inc(moe_used, 1)

                for g in range(4):
                    for c, (off, size) in enumerate(M.pieces):
                        k = g * nc_ + c
                        if up:
                            dve.wait_ge(units_silu, sb_[L] + M.units * n.n + k + 1)
                            wait_free_group(dve, moe_y, yb, n, g, 2)
                            dve.tensor_tensor(h[0:size, g % 2, c, :], sg[0:size, k % 2, :], ps[0:size, BANK_U[k % 2], :],
                                              ALU.mult).then_inc(units_h, 1)
                    if g:
                        add(g - 1)
                add(3)
            expert_passes(dve, M, body)

        link_base = {1: 0}
        sb_ = {1: 0, 2: 4, 3: 4 + 8 * 8}

        NAMES = {0: ("L0_xattn_Wq", "L0_xattn_Wk", "L0_xattn_Wv", None),
                 1: ("L1_xattn_Wq", "L1_xattn_Wk", "L1_xattn_Wv", "L1_xattn_Wo"),
                 2: ("L2_xattn_Wq", "L2_xattn_Wk", "L2_xattn_Wv", "L2_xattn_Wo"),
                 3: ("L3_xattn_w_q", "L3_xattn_w_k", "L3_xattn_w_v", "L3_xattn_w_o")}
        COLS = [(0, 0, "L0_xattn_bq"), (0, 1, "L0_xattn_bk"), (1, 0, "L1_xattn_bq"), (1, 1, "L1_xattn_bk"),
                (3, 0, "L3_xattn_b_q"), (3, 1, "L3_xattn_b_k")]
        ROWS = [(0, 0, "L0_xattn_bv"), (1, 0, "L1_xattn_bv"), (1, 1, "L1_xattn_bo"), (2, 1, "L2_xattn_bo"),
                (3, 0, "L3_xattn_b_v"), (3, 1, "L3_xattn_b_o")]
        SETUP = 16 * (3 + 2 + 15 + len(COLS) + len(ROWS) + 4 + 3 + 3)

        def column(name):
            return a[name].rearrange("(p n) -> p n", n=1)

        def row(name):
            return a[name].rearrange("(n p) -> n p", n=1)

        def setup_sync(sp):
            n = [0]

            def load(to, src):
                n[0] += 16
                sp.dma_start(to, src).then_inc(setup_loaded, 16)
            load(x[:, :, :], a["x"].rearrange("(t b) s d -> (b s) t d", b=2))
            load(const[:, :], a["const"])
            load(ctx_all[:, :, :], a["ctx_768"].rearrange("(t b) s d -> (b s) t d", b=2))
            load(gates[:, 0:4], row("g_xattn").broadcast_to([P, 4]))
            load(gates[:, 4:8], row("g_ffn").broadcast_to([P, 4]))
            sp.wait_ge(setup_zero, 3)
            for L in range(4):
                for k, name in enumerate(NAMES[L]):
                    if name:
                        rows = P if k in (0, 3) else CTX
                        load(att_w[0:rows, L, k, :], a[name])
            for L, k, name in COLS:
                load(att_col[:, L, k:k + 1], column(name))
            for L, k, name in ROWS:
                load(att_row[0:1, L, k, :], row(name))
            load(ln_col[:, 0:1], column("L1_xattn_ln1_g"))
            load(ln_col[:, 1:2], column("L1_xattn_ln1_b"))
            load(ln_col[0:CTX, 2:3], column("L1_xattn_ln2_g"))
            load(ln_col[0:CTX, 3:4], column("L1_xattn_ln2_b"))
            load(q_nat[:, 0, :].rearrange("p (c d) -> p c d", d=P), a["L0_ffn_w_gate"].rearrange("(c p) d -> p c d", p=P))
            load(q_nat[:, 1, :].rearrange("p (c d) -> p c d", d=P), a["L0_ffn_w_up"].rearrange("(c p) d -> p c d", p=P))
            load(q_nat[:, 2, :], a["L0_ffn_w_down"])
            load(gate_nat[:, 0, :], a["L1_ffn_gate_w"])
            load(gate_nat[0:8, 1, :], a["L3_ffn_Wg"])
            load(gate_w[:, 1, 0:8], a["L2_ffn_w_gate"])
            assert n[0] == SETUP, n

        def setup_pool(pool):
            pool.memset(att_w[:, :, :, :], 0.0)
            pool.memset(att_col[:, :, :], 0.0)
            pool.memset(ones[:, :], 1.0)
            pool.memset(ln_col[:, :], 0.0)
            pool.memset(gate_nat[:, :, :], 0.0)
            pool.memset(gate_w[:, :, :], 0.0).then_inc(setup_zero, 3)
            pool.memset(ctx_nat[:, :, :], 0.0)
            pool.memset(ctx_norm[:, :, :], 0.0)
            pool.memset(round_col[:, :], ROUND)
            pool.memset(q_sum[:, :], 0.0)
            pool.memset(vx[:, :, :, :, :], 0.0).then_inc(setup_pad, 1)

        def setup_vector(dve):
            dve.wait_ge(setup_loaded, SETUP)
            dve.wait_ge(setup_pad, 1)
            dve.tensor_copy(ident16[:, :], ident)
            for r in range(2):
                for b in range(2):
                    dve.tensor_copy(vx[:, r, b, :, 16:18], value_mask.rearrange("p (m j e) -> p m j e", j=2, e=HEAD)[:, :, :, 0])
            for L in range(2, 4):
                ins = dve.tensor_scalar(key_bias4[:, L, :], head_mask, att_col[:, L, 1:2], None, ALU.mult)
            ins.then_inc(setup_done, 1)

        block = ctx.enter_context(nc.Block())

        @block.sync
        def _(sp):
            setup_sync(sp)
            sp.wait_ge(setup_pad, 1)
            for L in range(4):
                if 2 * L < stop_after:
                    att_sync(sp, ATT[L])
                if L and 2 * L + 1 < stop_after:
                    moe_sync(sp, MOES[L])
            for g in range(4):
                if stop_after == 8:
                    sp.wait_ge(moe_used, 4 * (base_passes[3] + 7) + g + 1)
                else:
                    x_ready(sp, stop_after)
                sp.dma_start(out_d[:, 4 * g:4 * g + 4, :], x[:, 4 * g:4 * g + 4, :]).then_inc(stored, 16)
            sp.wait_ge(stored, 64)

        @block.gpsimd
        def _(pool):
            setup_pool(pool)

        @block.scalar
        def _(act):
            act.wait_ge(setup_loaded, SETUP)
            act.wait_ge(setup_done, 1)
            act.activation(gates[:, :], gates[:, :], ACT.Tanh).then_inc(gates_done, 1)
            for L in range(4):
                if 2 * L < stop_after:
                    att_scalar(act, ATT[L])
                if 2 * L + 1 < stop_after:
                    qff_scalar(act) if L == 0 else moe_scalar(act, MOES[L])

        @block.tensor
        def _(pe):
            pe.wait_ge(setup_loaded, SETUP)
            pe.wait_ge(setup_done, 1)
            for L in range(4):
                if 2 * L < stop_after:
                    att_tensor(pe, ATT[L])
                if 2 * L + 1 < stop_after:
                    qff_tensor(pe) if L == 0 else moe_tensor(pe, MOES[L])

        @block.vector
        def _(dve):
            setup_vector(dve)
            dve.wait_ge(gates_done, 1)
            for L in range(4):
                if 2 * L < stop_after:
                    att_vector(dve, ATT[L])
                if 2 * L + 1 < stop_after:
                    qff_vector(dve) if L == 0 else moe_vector(dve, MOES[L])


_INS = ["x", "ctx_768", "g_xattn", "g_ffn",
        "L0_xattn_Wq", "L0_xattn_bq", "L0_xattn_Wk", "L0_xattn_bk", "L0_xattn_Wv", "L0_xattn_bv",
        "L0_ffn_w_gate", "L0_ffn_w_up", "L0_ffn_w_down",
        "L1_xattn_ln1_g", "L1_xattn_ln1_b", "L1_xattn_ln2_g", "L1_xattn_ln2_b",
        "L1_xattn_Wq", "L1_xattn_bq", "L1_xattn_Wk", "L1_xattn_bk", "L1_xattn_Wv", "L1_xattn_bv",
        "L1_xattn_Wo", "L1_xattn_bo",
        "L1_ffn_gate_w", "L1_ffn_w1", "L1_ffn_w2", "L1_ffn_shared_gu", "L1_ffn_shared_down",
        "L2_xattn_Wq", "L2_xattn_Wk", "L2_xattn_Wv", "L2_xattn_Wo", "L2_xattn_bo",
        "L2_ffn_w_gate", "L2_ffn_w1", "L2_ffn_w3", "L2_ffn_w2",
        "L3_xattn_w_q", "L3_xattn_b_q", "L3_xattn_w_k", "L3_xattn_b_k", "L3_xattn_w_v", "L3_xattn_b_v",
        "L3_xattn_w_o", "L3_xattn_b_o",
        "L3_ffn_Wg", "L3_ffn_W1", "L3_ffn_W2", "L3_ffn_W3"]
STOP = 8


def kernel(**inputs):
    import numpy as _np
    import concourse.bacc as _bacc
    from concourse import mybir as _mybir
    from concourse.bass_utils import run_bass_kernel_spmd as _run

    nc = _bacc.Bacc("TRN2", target_bir_lowering=False, num_devices=1)
    arrays, aps = {}, {}
    for name in _INS + ["const"]:
        a = constants() if name == "const" else _np.ascontiguousarray(inputs[name])
        arrays[f"in_{name}_dram"] = a
        aps[name] = nc.dram_tensor(f"in_{name}_dram", a.shape, _mybir.dt.from_np(a.dtype), kind="ExternalInput").ap()
    out = nc.dram_tensor("out_0_dram", (SEQS, LEN, DIM), F32, kind="ExternalOutput").ap()
    build(nc, aps, out, STOP)
    r = _run(nc, [arrays], core_ids=[0])
    return r.results[0]["out_0_dram"]
```

```python
from contextlib import ExitStack

import numpy as np

import concourse.bass as bass
from concourse import mybir

F32 = mybir.dt.float32
BF16 = mybir.dt.bfloat16
U32 = mybir.dt.uint32
I32 = mybir.dt.int32
ALU = mybir.AluOpType
ACT = mybir.ActivationFunctionType
AX = mybir.AxisListType

P = 128
SEQS, LEN, DIM = 32, 64, 128
CTX = 96
TILES = SEQS * LEN // P
GROUPS = TILES // 4
EPS = 1e-5
HEADS, HEAD = 16, 8
INNER = 512
ROUND = 1.5 * 2.0 ** 23
FAR = -1.0e30
ATT_DEPTH = 8
QFF_DEPTH = 5

C_IDENT, C_HEAD, C_VALUE, C_SEQ, C_IOTA, C_END = 0, 128, 132, 260, 388, 404


def constants():
    c = np.zeros((P, C_END), np.float32)
    row = np.arange(P)
    c[:, C_IDENT:C_HEAD] = np.eye(P)
    c[:, C_HEAD:C_VALUE] = (row[:, None] // HEAD) % 4 == np.arange(4)[None, :]
    c[:, C_VALUE:C_SEQ] = (row[:, None] // LEN) == (row[None, :] // HEAD) % 2
    c[:, C_SEQ:C_IOTA] = np.where(row[:, None] // LEN == row[None, :] // LEN, 0.0, FAR)
    c[:, C_IOTA:C_END] = np.arange(16)[None, :]
    return c


class Tile:

    def __init__(self, pair, r, least_pair):
        self.t = pair * 2 + r
        self.par = r % 2
        self.half = pair + r // 2
        self.least = least_pair * 2 + r


def tile_steps(eng, body, depth):
    def steps(pair, least, ends):
        for r in range(2):
            def at(d, r=r):
                tile = Tile(pair, r - d, least)
                if ends and not 0 <= tile.t < TILES:
                    return None
                return tile
            body(at)

    first = (depth + 3) // 2
    for pair in range(first):
        steps(pair, pair, True)
    with eng.Fori(first, TILES // 2) as pair:
        steps(pair, first, False)
    for pair in range(TILES // 2, (TILES + depth + 1) // 2):
        steps(pair, pair, True)


def build(nc, a, out, stop_after=8):
    with ExitStack() as ctx:
        def sb(name, shape, dt=F32):
            return ctx.enter_context(nc.sbuf_tensor(name, shape, dt))

        def sem(name):
            return ctx.enter_context(nc.semaphore(name))

        x = sb("x", [P, TILES, DIM])
        const = sb("const", [P, C_END])
        ident = const[:, C_IDENT:C_HEAD]
        head_mask = const[:, C_HEAD:C_VALUE]
        value_mask = const[:, C_VALUE:C_SEQ]
        seq_mask = const[:, C_SEQ:C_IOTA]
        iota = const[:, C_IOTA:C_END]
        ident16 = sb("ident16", [P, P], BF16)
        ones = sb("ones", [P, P])
        gates = sb("gates", [P, 8])
        att_w = sb("att_w", [P, 4, 4, P])
        att_col = sb("att_col", [P, 4, 2])
        att_row = sb("att_row", [1, 4, 2, P])
        ln_col = sb("ln_col", [P, 4])
        key_bias4 = sb("key_bias4", [P, 4, 4])
        ctx_nat = sb("ctx_nat", [P, 2, P])
        ctx_norm = sb("ctx_norm", [P, 2, P])
        ctx_all = sb("ctx_all", [P, TILES, CTX])
        xn_all = sb("xn_all", [P, TILES, P])
        stats = sb("stats", [P, TILES, 6])
        moments = sb("moments", [P, 3, TILES, 2])
        rstd = sb("rstd", [P, 3, TILES])
        nr_a = sb("nr_a", [P, TILES])
        nr_i = sb("nr_i", [P, TILES], I32)
        nr_t = sb("nr_t", [P, TILES])
        xn = sb("xn", [P, 2, P])
        xnn = sb("xnn", [P, 2, P])
        inT = sb("inT", [P, 2, 2, P])
        ctx2 = sb("ctx2", [P, 2, 2, 2, LEN])
        qT = sb("qT", [P, 2, P])
        qz = sb("qz", [P, 2, 4, P])
        kT = sb("kT", [P, 2, P])
        kx = sb("kx", [P, 2, 2, 4, LEN])
        vx = sb("vx", [P, TILES, 2, 8, 18])
        top = sb("top", [P, 2, HEADS])
        prob = sb("prob", [P, 2, HEADS * LEN])
        probT = sb("probT", [P, 2, 8, P])
        rsum = sb("rsum", [P, 2, HEADS])
        rinv = sb("rinv", [P, 2, HEADS])
        rgate = sb("rgate", [P, 2])
        on = sb("on", [P, 2, P])
        oT = sb("oT", [P, 2, P])
        bias_row = sb("bias_row", [P, P])
        value_col = sb("value_col", [P, 4])
        value_bias = sb("value_bias", [P, 4, P])
        q_nat = sb("q_nat", [P, 3, INNER])
        q_tmp = sb("q_tmp", [P, 3, INNER])
        q_int = sb("q_int", [P, 3, INNER], BF16)
        qw = sb("qw", [P, 3, INNER], BF16)
        q_sum = sb("q_sum", [P, 8])
        q_mean = sb("q_mean", [P, 8])
        q_scale = sb("q_scale", [P, 8])
        q_top = sb("q_top", [P, 3, TILES])
        q_gu = sb("q_gu", [P, TILES, 2])
        hs_col = sb("hs_col", [P, 2, 2])
        hs_inv = sb("hs_inv", [P, 2])
        hs_down = sb("hs_down", [P, TILES])
        xq = sb("xq", [P, TILES, P], BF16)
        xqT = sb("xqT", [P, TILES, P], BF16)
        sil = sb("sil", [P, 2, INNER])
        hid = sb("hid", [P, 2, INNER])
        hq_t = sb("hq_t", [P, 2, INNER])
        hq = sb("hq", [P, 2, INNER], BF16)
        hqT = sb("hqT", [P, 2, 4, P], BF16)
        xT = sb("xT", [P, TILES, P])
        v1 = xT
        gate_nat = sb("gate_nat", [16, 2, P])
        gate_w = sb("gate_w", [P, 3, 16])
        logit = sb("logit", [P, TILES, 16])
        cent = sb("cent", [P, TILES, 16])
        ex = sb("ex", [P, TILES, 16])
        rmax = sb("rmax", [P, TILES])
        rz = sb("rz", [P, TILES])
        rzi = sb("rzi", [P, TILES])
        best = sb("best", [P, TILES, 8])
        besti = sb("besti", [P, TILES, 8], U32)
        bestf = sb("bestf", [P, TILES, 8])
        wk = sb("wk", [P, TILES, 4])
        hit = sb("hit", [P, TILES, 16])
        hitw = sb("hitw", [P, TILES, 16])
        ew = sb("ew", [P, TILES, 17])
        w_nat = sb("w_nat", [P, 2, 3, 384])
        w_up = sb("w_up", [P, 2, 2, 384])
        w_dn = sb("w_dn", [P, 2, 3, P])
        sg = sb("sg", [P, 2, 512])
        h = sb("h", [P, 2, 3, 512])

        ps = ctx.enter_context(nc.psum_tensor("ps", [P, 8, 512], F32))
        p_score = ps[:, 0:4, 0:256]
        p_oT = ps[:, 4, 0:P]
        p_o = ps[:, 5, 0:288].rearrange("p (m b c) -> p m b c", m=8, b=2)
        p_in = ps[:, 6, 0:256]
        p_qk = ps[:, 6, 0:256]
        p_v = ps[:, 7, 0:256]
        p_y = ps[:, 7, 0:P]

        setup_loaded, later_loaded = sem("setup_loaded"), sem("later_loaded")
        setup_const = sem("setup_const")
        setup_zero = sem("setup_zero")
        setup_pad = sem("setup_pad")
        setup_done, later_done = sem("setup_done"), sem("later_done")
        gates_done = sem("gates_done")
        ctx_loaded = [sem("ctx_loaded0"), sem("ctx_loaded1")]
        ln_link = sem("ln_link")
        xn_ready = sem("xn_ready")
        xnn_ready = sem("xnn_ready")
        xn_all_ready = sem("xn_all_ready")
        row_done, row_copied, x_biased = sem("row_done"), sem("row_copied"), sem("x_biased")
        x_stats, moe_stats = sem("x_stats"), sem("moe_stats")
        in_turned, in_copied = sem("in_turned"), sem("in_copied")
        qk_projected, v_projected = sem("qk_projected"), sem("v_projected")
        qk_copied, v_copied = sem("qk_copied"), sem("v_copied")
        scored, top_ready, centered, exped = sem("scored"), sem("top_ready"), sem("centered"), sem("exped")
        p_turned, p_copied_act, p_copied_dve = sem("p_turned"), sem("p_copied_act"), sem("p_copied_dve")
        attended, sum_inverted, normed = sem("attended"), sem("sum_inverted"), sem("normed")
        o_turned, o_copied, y_done = sem("o_turned"), sem("o_copied"), sem("y_done")
        x_done = sem("x_done")
        qw_step, qw_turned, qw_copied = sem("qw_step"), sem("qw_turned"), sem("qw_copied")
        q_gu_ready, hs_top, hs_floor, q_stats = sem("q_gu_ready"), sem("hs_top"), sem("hs_floor"), sem("q_stats")
        q_down = sem("q_down")
        xq_ready, xq_turned, xq_copied = sem("xq_ready"), sem("xq_turned"), sem("xq_copied")
        gu_ready, silu_done, hid_ready = sem("gu_ready"), sem("silu_done"), sem("hid_ready")
        hs_ready, hq_scaled, hq_ready = sem("hs_ready"), sem("hq_scaled"), sem("hq_ready")
        hq_turned, hq_copied = sem("hq_turned"), sem("hq_copied")
        moe_xn, x_turned, x_copied = sem("moe_xn"), sem("x_turned"), sem("x_copied")
        gate_turned, gate_copied = sem("gate_turned"), sem("gate_copied")
        logits_done, logits_copied = sem("logits_done"), sem("logits_copied")
        route_link, route_asked, route_exp = sem("route_link"), sem("route_asked"), sem("route_exp")
        w_loaded = [sem("w_loaded0"), sem("w_loaded1")]
        w_turned, w_copied = sem("w_turned"), sem("w_copied")
        units_up, units_silu, units_h = sem("units_up"), sem("units_silu"), sem("units_h")
        moe_y, moe_used = sem("moe_y"), sem("moe_used")
        stored = sem("stored")

        x_d = a["x"].rearrange("(t b) s d -> t (b s) d", b=2)
        ctx_d = a["ctx_768"].rearrange("(t b) s d -> t (b s) d", b=2)
        out_d = out.rearrange("(t b) s d -> (b s) t d", b=2)

        class Moe:
            def __init__(self, layer, experts, shared, pieces, turned):
                self.layer, self.experts, self.shared = layer, experts, shared
                self.pieces, self.turned = pieces, turned
                self.passes = experts + shared
                self.units = 4 * len(pieces)
        MOES = {1: Moe(1, 16, 1, [(0, 128)], True),
                2: Moe(2, 8, 0, [(0, 128), (128, 128)], False),
                3: Moe(3, 8, 0, [(0, 128), (128, 128), (256, 96)], True)}
        base_units, base_passes, base_turned, base_loads = {}, {}, {}, {}
        u = p_ = tn = 0
        for L, m in MOES.items():
            base_units[L], base_passes[L], base_turned[L] = u, p_, tn
            u += m.units * m.passes
            p_ += m.passes
            tn += m.passes if m.turned else 0
        LOADS = {1: 2, 2: 3, 3: 7}
        def loads_of(L, n):
            return 3 if L == 1 and n == 0 else LOADS[L]
        for par in range(2):
            c = 0
            for L, m in MOES.items():
                base_loads[L, par] = c
                c += sum(loads_of(L, n) for n in range(par, m.passes, 2))

        def loads_until(L, n, half):
            extra = 1 if L == 1 and n.par == 0 else 0
            return (half + 1) * LOADS[L] + base_loads[L, n.par] + extra

        def x_ready(eng, sub, tile=None):
            if sub == 0:
                return
            L = (sub - 1) // 2
            if sub % 2 == 0 and L >= 1:
                eng.wait_ge(moe_used, 4 * (base_passes[L] + MOES[L].passes))
            else:
                base = {1: 0, 2: 16, 3: 32, 5: 48, 7: 64}[sub]
                eng.wait_ge(x_done, base + (TILES if tile is None else tile.t + 1))
        xn_base = {0: 0, 4: 16, 6: 32}
        x_done_base = {0: 0, 1: 16, 2: 32, 4: 48, 6: 64}

        class Att:
            def __init__(self, L):
                self.L, self.sub, self.base = L, 2 * L, 16 * L
                self.multi = L >= 2
                self.mbase = 16 * (L - 2)
                self.obase = 16 * (L - 1)
                self.scale = [1.0, P ** -0.5, HEAD ** -0.5, HEAD ** -0.5][L]
                self.p_oT, self.p_y, self.p_qk = (p_oT, p_y, p_qk) if self.multi else (ps[:, 1, 0:P], ps[:, 2, 0:P], ps[:, 3, 0:256])
        ATT = [Att(L) for L in range(4)]

        def free_again(eng, s, base, tile, lag, per=1):
            if base + per * (tile.least - lag + 1) > 0:
                eng.wait_ge(s, base + per * (tile.t - lag + 1))

        def att_sync(sp, A, later=None):
            if later:
                later()
            def body(at):
                if (i := at(0)) is not None:
                    free_again(sp, in_turned, A.base, i, 2)
                    sp.dma_start(ctx_nat[:, i.par, 0:CTX], ctx_d[i.t]).then_inc(ctx_loaded[i.par], 16)
            if A.L != 1:
                tile_steps(sp, body, 0)

        def att_vector(dve, A):
            x_ready(dve, A.sub)
            if A.L == 0:
                all_stats(dve, ctx_all)
                norm_roots(dve, 2)
                all_stats(dve, x)
            elif A.L == 1:
                dve.wait_ge(q_stats, TILES)
            else:
                dve.wait_ge(moe_stats, 4 * (A.L - 1))
            norm_roots(dve, 0)
            dve.wait_ge(row_done, A.L + 1)
            dve.tensor_scalar(bias_row[:, :], ps[:, 7, 0:P], gates[:, A.L:A.L + 1], None, ALU.mult).then_inc(row_copied, 1)
            dve.wait_ge(row_copied, A.L + 1)
            if A.L == 1:
                for t in range(TILES):
                    ins = dve.tensor_scalar(xn_all[:, t, :], x[:, t, :], moments[:, 0, t, 0:1], rstd[:, 0, t:t + 1],
                                            ALU.subtract, ALU.mult)
                ins.then_inc(xn_all_ready, 1)
                dve.wait_ge(xn_all_ready, 1)
                all_stats(dve, xn_all)
                norm_roots(dve, 1)

            def body(at):
                if A.multi and (i := at(5)) is not None:
                    dve.wait_ge(p_turned, A.base + i.t + 1)
                    free_again(dve, attended, A.base, i, 2)
                    dve.tensor_copy(probT[:, i.par, 4:8, :], ps[:, 5, :].rearrange("p (m q) -> p m q", q=P)).then_inc(p_copied_dve, 1)
                if A.L >= 1 and (i := at(7)) is not None:
                    dve.wait_ge(y_done, A.obase + i.t + 1)
                    dve.wait_ge(x_biased, A.base + i.t + 1)
                    dve.scalar_tensor_tensor(x[:, i.t, :], A.p_y, gates[:, A.L:A.L + 1], x[:, i.t, :],
                                             ALU.mult, ALU.add).then_inc(x_done, 1)
                if (i := at(0)) is not None:
                    free_again(dve, in_turned, A.base, i, 2)
                    if A.L != 1:
                        norm_tile(dve, A.sub, i)
                    else:
                        r = i.par
                        dve.tensor_scalar(xnn[:, r, :], xn_all[:, i.t, :], moments[:, 1, i.t, 0:1], rstd[:, 1, bass.ds(i.t, 1)],
                                          ALU.subtract, ALU.mult)
                        dve.tensor_scalar(ctx_norm[:, r, 0:CTX], ctx_all[:, i.t, :], moments[:, 2, i.t, 0:1],
                                          rstd[:, 2, bass.ds(i.t, 1)], ALU.subtract, ALU.mult).then_inc(xnn_ready, 1)
                if (i := at(4)) is not None:
                    r = i.par
                    dve.wait_ge(scored, A.base + i.t + 1)
                    free_again(dve, p_turned, A.base, i, 2)
                    if A.multi:
                        sc = p_score.rearrange("p g (n k) -> p g n k", k=LEN)
                        tp = top[:, r, :].rearrange("p (g n) -> p g n", g=4)
                        dve.tensor_reduce(tp, sc, AX.X, ALU.max).then_inc(top_ready, 1)
                        dve.wait_ge(top_ready, A.base + i.t + 1)
                        dve.tensor_tensor(prob[:, r, :].rearrange("p (g n k) -> p g n k", g=4, k=LEN), sc,
                                          tp.unsqueeze(3).broadcast_to([P, 4, 4, LEN]), ALU.subtract).then_inc(centered, 1)
                    else:
                        dve.scalar_tensor_tensor(prob[:, r, 0:P], ps[:, 0, 0:P], A.scale, seq_mask, ALU.mult, ALU.add).then_inc(top_ready, 1)
                        dve.wait_ge(top_ready, A.base + i.t + 1)
                        dve.tensor_reduce(top[:, r, 0:1], prob[:, r, 0:P], AX.X, ALU.max, negate=True).then_inc(centered, 1)
                if (i := at(5)) is not None:
                    r = i.par
                    dve.wait_ge(attended, A.base + i.t + 1)
                    if A.multi:
                        for b in range(2):
                            rows = slice(LEN * b, LEN * b + LEN)
                            last = dve.reciprocal(rinv[rows, r, :].rearrange("p (m j) -> p m j", j=2), p_o[rows, :, b, 16:18])
                        last.then_inc(sum_inverted, 1)
                        free_again(dve, o_turned, A.obase, i, 2)
                        dve.wait_ge(sum_inverted, A.base + i.t + 1)
                        for b in range(2):
                            rows = slice(LEN * b, LEN * b + LEN)
                            last = dve.tensor_tensor(on[rows, r, :].rearrange("p (m j e) -> p m j e", j=2, e=HEAD),
                                                     p_o[rows, :, b, 0:16].rearrange("p m (j e) -> p m j e", j=2),
                                                     rinv[rows, r, :].rearrange("p (m j) -> p m j", j=2).unsqueeze(3)
                                                     .broadcast_to([LEN, 8, 2, HEAD]), ALU.mult)
                        last.then_inc(normed, 1)
                    else:
                        dve.reciprocal(rinv[:, r, 0:1], rsum[:, r, 0:1]).then_inc(sum_inverted, 1)
                        dve.wait_ge(sum_inverted, A.base + i.t + 1)
                        if A.L == 0:
                            dve.tensor_scalar(rgate[:, r:r + 1], rinv[:, r, 0:1], gates[:, 0:1], None, ALU.mult).then_inc(normed, 1)
                            dve.wait_ge(normed, A.base + i.t + 1)
                            dve.wait_ge(x_biased, A.base + i.t + 1)
                            dve.scalar_tensor_tensor(x[:, i.t, :], ps[:, 5, 0:P], rgate[:, r:r + 1], x[:, i.t, :],
                                                     ALU.mult, ALU.add).then_inc(x_done, 1)
                        else:
                            free_again(dve, o_turned, A.obase, i, 2)
                            dve.tensor_scalar(on[:, r, :], ps[:, 5, 0:P], rinv[:, r, 0:1], None, ALU.mult).then_inc(normed, 1)
                if (i := at(2)) is not None:
                    r = i.par
                    dve.wait_ge(v_projected, A.base + i.t + 1)
                    if A.multi:
                        for b in range(2):
                            last = dve.tensor_tensor(vx[:, i.t, b, :, 0:16], p_v[:, P * b:P * b + P].rearrange("p (m c) -> p m c", c=16),
                                                     value_mask.rearrange("p (m c) -> p m c", c=16), ALU.mult)
                        last.then_inc(v_copied, 1)
                    else:
                        dve.tensor_copy(v1[:, i.t, :], p_v[:, 0:P]).then_inc(v_copied, 1)
                if (i := at(2)) is not None:
                    dve.wait_ge(in_turned, A.base + i.t + 1)
                    dve.tensor_tensor(x[:, i.t, :], x[:, i.t, :], bias_row[:, :], ALU.add).then_inc(x_biased, 1)
                if (i := at(8)) is not None:
                    dve.wait_ge(x_done, x_done_base[A.sub] + i.t + 1)
                    tile_stats(dve, i, A.base)
            tile_steps(dve, body, ATT_DEPTH)

        ln_links = [0]

        def linked_ln(dve, ins):
            ln_links[0] += 1
            ins.then_inc(ln_link, 1)
            dve.wait_ge(ln_link, ln_links[0])

        def tile_stats(dve, i, base):
            dve.bn_stats(stats[:, i.t, :], x[:, i.t, :]).then_inc(x_stats, 1)

        def all_stats(dve, src):
            for t in range(TILES):
                ins = dve.bn_stats(stats[:, t, :], src[:, t, :])
            linked_ln(dve, ins)

        def norm_roots(dve, which):
            def linked(ins):
                linked_ln(dve, ins)
            for t in range(TILES):
                ins = dve.bn_aggr(moments[:, which, t, :], stats[:, t, :])
            linked(ins)
            root = rstd[:, which, :]
            linked(dve.tensor_scalar(nr_a[:, :], moments[:, which, :, 1], EPS, None, ALU.add))
            linked(dve.tensor_scalar(nr_i[:, :], nr_a[:, :].bitcast(I32), 1, None, ALU.arith_shift_right))
            linked(dve.tensor_scalar(root.bitcast(I32), nr_i[:, :], -1.0, float(0x5F3759DF), ALU.mult, ALU.add))
            for _ in range(3):
                linked(dve.tensor_tensor(nr_t[:, :], nr_a[:, :], root, ALU.mult))
                linked(dve.scalar_tensor_tensor(nr_t[:, :], nr_t[:, :], -0.5, root, ALU.mult, ALU.mult))
                linked(dve.scalar_tensor_tensor(root, nr_t[:, :], 1.5, root, ALU.add, ALU.mult))

        def norm_tile(dve, sub, i):
            dve.tensor_scalar(xn[:, i.par, :], x[:, i.t, :], moments[:, 0, i.t, 0:1], rstd[:, 0, bass.ds(i.t, 1)],
                              ALU.subtract, ALU.mult).then_inc(xn_ready, 1)

        def att_scalar(act, A):
            def body(at):
                if (i := at(5)) is not None:
                    act.wait_ge(p_turned, A.base + i.t + 1)
                    free_again(act, attended, A.base, i, 2)
                    if A.multi:
                        act.copy(probT[:, i.par, 0:4, :], ps[:, 4, :].rearrange("p (m q) -> p m q", q=P)).then_inc(p_copied_act, 1)
                    else:
                        act.copy(probT[:, i.par, 0, :], ps[:, 4, 0:P]).then_inc(p_copied_act, 1)
                if (i := at(1)) is not None:
                    r = i.par
                    act.wait_ge(in_turned, A.base + i.t + 1)
                    free_again(act, v_projected, A.base, i, 2)
                    if A.L == 1:
                        act.activation(inT[:, r, 0, :], p_in[:, 0:P], ACT.Identity, bias=ln_col[:, 1:2], scale=ln_col[:, 0:1])
                        act.activation(inT[:, r, 1, :], p_in[:, P:2 * P], ACT.Identity, bias=ln_col[:, 3:4],
                                       scale=ln_col[:, 2:3]).then_inc(in_copied, 1)
                    elif A.multi:
                        act.copy(inT[:, r, 0, :], p_in[:, 0:P])
                        act.copy(ctx2[:, r, :, :, :], p_in[:, P:2 * P].rearrange("p (b k) -> p b k", b=2).unsqueeze(2)
                                 .broadcast_to([P, 2, 2, LEN])).then_inc(in_copied, 1)
                    else:
                        act.copy(inT[:, r, :, :], p_in.rearrange("p (a q) -> p a q", a=2)).then_inc(in_copied, 1)
                if A.L >= 1 and (i := at(6)) is not None:
                    act.wait_ge(o_turned, A.obase + i.t + 1)
                    free_again(act, y_done, A.obase, i, 2)
                    act.copy(oT[:, i.par, :], A.p_oT).then_inc(o_copied, 1)
                if (i := at(4)) is not None:
                    r = i.par
                    act.wait_ge(centered, A.base + i.t + 1)
                    if A.multi:
                        act.activation(prob[:, r, :], prob[:, r, :], ACT.Exp, scale=A.scale).then_inc(exped, 1)
                    else:
                        free_again(act, sum_inverted, A.base, i, 2)
                        act.activation(prob[:, r, 0:P], prob[:, r, 0:P], ACT.Exp, bias=top[:, r, 0:1],
                                       accum_out=rsum[:, r, 0:1]).then_inc(exped, 1)
                if (i := at(2)) is not None:
                    r = i.par
                    act.wait_ge(qk_projected, A.base + i.t + 1)
                    free_again(act, scored, A.base, i, 2)
                    if not A.multi:
                        act.activation(qT[:, r, :], A.p_qk[:, 0:P], ACT.Identity, bias=att_col[:, A.L, 0:1])
                    if A.multi:
                        for g in range(4):
                            rows = slice(32 * g, 32 * g + 32)
                            act.activation(qz[rows, r, g, :], A.p_qk[rows, 0:P], ACT.Identity, bias=att_col[rows, A.L, 0:1])
                        for n in range(4):
                            last = act.activation(kx[:, r, :, n, :], A.p_qk[:, P:2 * P].rearrange("p (b k) -> p b k", b=2),
                                                  ACT.Identity, bias=key_bias4[:, A.L, n:n + 1], scale=head_mask[:, n:n + 1])
                        last.then_inc(qk_copied, 1)
                    else:
                        act.activation(kT[:, r, :], A.p_qk[:, P:2 * P], ACT.Identity, bias=att_col[:, A.L, 1:2]).then_inc(qk_copied, 1)
            tile_steps(act, body, ATT_DEPTH)

        def att_tensor(pe, A):
            wq, wk_, wv, wo = (att_w[:, A.L, n, :] for n in range(4))

            def body(at):
                if (i := at(5)) is not None:
                    r = i.par
                    pe.wait_ge(exped, A.base + i.t + 1)
                    free_again(pe, p_copied_act, A.base, i, 1)
                    if A.multi:
                        free_again(pe, o_copied, A.obase, i, 2)
                        free_again(pe, normed, A.base, i, 1)
                        for m in range(8):
                            last = pe.transpose(ps[:, 4 + m // 4, P * (m % 4):P * (m % 4) + P], prob[:, r, P * m:P * m + P], ident)
                    else:
                        last = pe.transpose(ps[:, 4, 0:P], prob[:, r, 0:P], ident)
                    last.then_inc(p_turned, 1)
                if A.L >= 1 and (i := at(7)) is not None:
                    pe.wait_ge(o_copied, A.obase + i.t + 1)
                    if A.multi:
                        v = at(3)
                        pe.wait_ge(v_copied, A.base + (v.t + 1 if v is not None else TILES))
                    free_again(pe, x_done, x_done_base[A.sub], i, 1)
                    pe.matmul(A.p_y, oT[:, i.par, :], wo, start=True, stop=True).then_inc(y_done, 1)
                if (i := at(1)) is not None:
                    r = i.par
                    if A.L == 1:
                        pe.wait_ge(xnn_ready, i.t + 1)
                    else:
                        pe.wait_ge(xn_ready, xn_base[A.sub] + i.t + 1)
                        pe.wait_ge(ctx_loaded[r], 16 * (8 * (A.L - (A.L > 1)) + i.half + 1))
                    if A.multi:
                        free_again(pe, qk_copied, A.base, i, 2)
                    free_again(pe, in_copied, A.base, i, 1)
                    pe.transpose(p_in[:, 0:P], (xnn if A.L == 1 else xn)[:, r, :], ident)
                    pe.transpose(p_in[:, P:2 * P], (ctx_norm if A.L == 1 else ctx_nat)[:, r, :], ident).then_inc(in_turned, 1)
                if A.L >= 1 and (i := at(6)) is not None:
                    pe.wait_ge(normed, A.base + i.t + 1)
                    if A.multi:
                        p = at(5)
                        pe.wait_ge(p_copied_act, A.base + (p.t + 1 if p is not None else TILES))
                    free_again(pe, o_copied, A.obase, i, 1)
                    pe.transpose(A.p_oT, on[:, i.par, :], ident).then_inc(o_turned, 1)

                def project(i):
                    r = i.par
                    n = at(1) if A.multi else i
                    pe.wait_ge(in_copied, A.base + (n.t + 1 if n is not None else TILES))
                    free_again(pe, qk_copied, A.base, i, 1)
                    pe.matmul(A.p_qk[:, 0:P], wq, inT[:, r, 0, :], start=True, stop=True)
                    keys = ctx2[:, r, :, 0, :] if A.multi else inT[:, r, 1, :]
                    pe.matmul(A.p_qk[:, P:2 * P], wk_, keys, start=True, stop=True).then_inc(qk_projected, 1)
                if not A.multi and (i := at(2)) is not None:
                    project(i)
                if (i := at(5)) is not None:
                    r = i.par
                    pe.wait_ge(p_copied_act, A.base + i.t + 1)
                    pe.wait_ge(v_copied, A.base + i.t + 1)
                    if A.multi:
                        pe.wait_ge(p_copied_dve, A.mbase + i.t + 1)
                        for m in range(8):
                            last = pe.matmul(p_o[:, m, :, :], probT[:, r, m, :], vx[:, i.t, :, m, :], start=True, stop=True)
                    else:
                        free_again(pe, x_done if A.L == 0 else normed, A.base, i, 1)
                        last = pe.matmul(ps[:, 5, 0:P], probT[:, r, 0, :], v1[:, i.t, :], start=True, stop=True)
                    last.then_inc(attended, 1)
                if A.multi and (i := at(2)) is not None:
                    project(i)
                if (i := at(2)) is not None:
                    r = i.par
                    free_again(pe, v_copied, A.base, i, 1)
                    if A.multi:
                        free_again(pe, x_done, x_done_base[A.sub], i, 5)
                    for b in range(2 if A.multi else 1):
                        keys = ctx2[:, r, b, :, :].rearrange("p j k -> p (j k)") if A.multi else inT[:, r, 1, :]
                        last = pe.matmul(p_v[:, P * b:P * b + P], keys, wv, start=True, stop=True)
                    last.then_inc(v_projected, 1)
                if (i := at(3)) is not None:
                    r = i.par
                    pe.wait_ge(qk_copied, A.base + i.t + 1)
                    free_again(pe, centered if A.multi else top_ready, A.base, i, 1)
                    if A.multi:
                        for b in range(2):
                            for g in range(4):
                                last = pe.matmul(ps[LEN * b:LEN * b + LEN, g, 0:256], qz[:, r, g, LEN * b:LEN * b + LEN],
                                                 kx[:, r, b, :, :].rearrange("p n k -> p (n k)"), start=True, stop=True)
                    else:
                        last = pe.matmul(ps[:, 0, 0:P], qT[:, r, :], kT[:, r, :], start=True, stop=True)
                    last.then_inc(scored, 1)
            x_ready(pe, A.sub)
            if A.L == 0:
                pe.matmul(ps[:, 7, 0:P], ones[0:1, :], att_row[0:1, 0, 0, :], start=True, stop=True).then_inc(row_done, 1)
            else:
                if A.L != 2:
                    pe.matmul(ps[:, 7, 0:P], value_bias[:, A.L, :], wo, start=True, stop=False)
                pe.matmul(ps[:, 7, 0:P], ones[0:1, :], att_row[0:1, A.L, 1, :], start=A.L == 2, stop=True).then_inc(row_done, 1)
            pe.wait_ge(row_copied, A.L + 1)

            tile_steps(pe, body, ATT_DEPTH)

        Q_G, Q_U, Q_T, Q_Y = (0, 1), (2, 3), 4, 6
        p16 = ps[:, 4:6, :].rearrange("p b n -> p (b n)").bitcast(BF16)
        p_xq = p16[:, 0:P]
        p_hq = p16[:, 1024:1024 + 512]

        def qff_prepare_vector(dve):
            link = [0]

            def linked(ins):
                link[0] += 1
                ins.then_inc(qw_step, 1)
                dve.wait_ge(qw_step, link[0])
            dve.wait_ge(later_loaded, LATER)
            linked(dve.tensor_reduce(q_sum[:, 0:3], q_nat[:, :, :], AX.X, ALU.add, apply_absolute_value=True))
            dve.wait_ge(qw_turned, 1)
            linked(dve.tensor_scalar(q_mean[:, 0:3], ps[:, 7, 0:3], 1.0 / (INNER * DIM), EPS, ALU.mult, ALU.max))
            linked(dve.reciprocal(q_scale[:, 0:3], q_mean[:, 0:3]))
            for n in range(3):
                linked(dve.tensor_scalar(q_tmp[:, n, :], q_nat[:, n, :], q_scale[:, n:n + 1], 1.0, ALU.mult, ALU.min))
                linked(dve.tensor_scalar(q_tmp[:, n, :], q_tmp[:, n, :], -1.0, ROUND, ALU.max, ALU.add))
                linked(dve.tensor_scalar(q_int[:, n, :], q_tmp[:, n, :], -ROUND, None, ALU.add))
            linked(dve.tensor_scalar(q_mean[:, 6:7], q_mean[:, 2:3], gates[:, 4:5], None, ALU.mult))
            assert link[0] == QW_LINKS

        QW_LINKS = 13

        def qff_vector(dve):
            dve.wait_ge(x_stats, TILES)
            norm_roots(dve, 0)
            for t in range(TILES):
                ins = dve.tensor_scalar(xn_all[:, t, :], x[:, t, :], moments[:, 0, t, 0:1], rstd[:, 0, t:t + 1],
                                        ALU.subtract, ALU.mult)
            linked_ln(dve, ins)
            linked_ln(dve, dve.tensor_reduce(q_top[:, 0, :], xn_all[:, :, :], AX.X, ALU.max, apply_absolute_value=True))
            linked_ln(dve, dve.tensor_scalar(q_top[:, 1, :], q_top[:, 0, :], EPS, 1.0 / 127.0, ALU.max, ALU.mult))
            linked_ln(dve, dve.reciprocal(q_top[:, 2, :], q_top[:, 1, :]))
            for t in range(TILES):
                ins = dve.tensor_scalar(xn_all[:, t, :], xn_all[:, t, :], q_top[:, 2, t:t + 1], ROUND, ALU.mult, ALU.add)
            linked_ln(dve, ins)
            for g in range(4):
                dve.tensor_scalar(xq[:, 4 * g:4 * g + 4, :], xn_all[:, 4 * g:4 * g + 4, :], -ROUND, None, ALU.add).then_inc(xq_ready, 1)
            for k in range(2):
                ins = dve.tensor_scalar(q_gu[:, :, k], q_top[:, 1, :], q_mean[:, k:k + 1], None, ALU.mult)
            ins.then_inc(q_gu_ready, 1)
            dve.wait_ge(q_gu_ready, 1)

            def body(at):
                if (i := at(3)) is not None:
                    r = i.par
                    dve.wait_ge(hq_scaled, i.t + 1)
                    free_again(dve, hq_turned, 0, i, 2)
                    dve.tensor_scalar(hq[:, r, :], hq_t[:, r, :], -ROUND, None, ALU.add).then_inc(hq_ready, 1)
                if (i := at(1)) is not None:
                    r = i.par
                    dve.wait_ge(silu_done, i.t + 1)
                    free_again(dve, hq_scaled, 0, i, 2)
                    dve.scalar_tensor_tensor(hid[:, r, :], ps[:, Q_U[r], :], q_gu[:, i.t, 1:2], sil[:, r, :],
                                             ALU.mult, ALU.mult).then_inc(hid_ready, 1)
                if (i := at(4)) is not None:
                    dve.wait_ge(q_down, i.t + 1)
                    dve.wait_ge(hs_ready, 2 * i.t + 2)
                    dve.scalar_tensor_tensor(x[:, i.t, :], ps[:, Q_Y + i.par, 0:P], hs_down[:, bass.ds(i.t, 1)], x[:, i.t, :],
                                             ALU.mult, ALU.add).then_inc(x_done, 1)
                if (i := at(1)) is not None:
                    r = i.par
                    dve.wait_ge(hid_ready, i.t + 1)
                    dve.tensor_reduce(hs_col[:, r, 0:1], hid[:, r, :], AX.X, ALU.max, apply_absolute_value=True).then_inc(hs_top, 1)
                if (i := at(5)) is not None:
                    dve.wait_ge(x_done, 16 + i.t + 1)
                    dve.bn_stats(stats[:, i.t, :], x[:, i.t, :]).then_inc(q_stats, 1)
                if (i := at(1)) is not None:
                    r = i.par
                    dve.wait_ge(hs_top, i.t + 1)
                    dve.tensor_scalar(hs_col[:, r, 1:2], hs_col[:, r, 0:1], EPS, 1.0 / 127.0, ALU.max, ALU.mult).then_inc(hs_floor, 1)
                if (i := at(1)) is not None:
                    r = i.par
                    dve.wait_ge(hs_floor, i.t + 1)
                    dve.reciprocal(hs_inv[:, r:r + 1], hs_col[:, r, 1:2]).then_inc(hs_ready, 1)
                    dve.tensor_scalar(hs_down[:, bass.ds(i.t, 1)], hs_col[:, r, 1:2], q_mean[:, 6:7], None, ALU.mult).then_inc(hs_ready, 1)
            tile_steps(dve, body, QFF_DEPTH)

        def qff_turn_weights(act):
            for n in range(3):
                act.wait_ge(qw_turned, n + 2)
                act.copy(qw[:, n, :], p16[:, 1024 * (n % 2):1024 * (n % 2) + 512]).then_inc(qw_copied, 1)

        def qff_scalar(act):
            for g in range(4):
                act.wait_ge(xq_turned, g + 1)
                act.copy(xqT[:, 4 * g:4 * g + 4, :], p16[:, 1024 * (g % 2):1024 * (g % 2) + 512].rearrange("p (t q) -> p t q", q=P)).then_inc(xq_copied, 1)
            act.wait_ge(q_gu_ready, 1)

            def body(at):
                if (i := at(2)) is not None:
                    r = i.par
                    act.wait_ge(hs_ready, 2 * i.t + 2)
                    free_again(act, hq_ready, 0, i, 2)
                    act.activation(hq_t[:, r, :], hid[:, r, :], ACT.Identity, bias=round_col[:, 0:1], scale=hs_inv[:, r:r + 1]).then_inc(hq_scaled, 1)
                if (i := at(0)) is not None:
                    r = i.par
                    act.wait_ge(gu_ready, i.t + 1)
                    free_again(act, hid_ready, 0, i, 2)
                    act.activation(sil[:, r, :], ps[:, Q_G[r], :], ACT.Silu, scale=q_gu[:, i.t, 0:1]).then_inc(silu_done, 1)
                if (i := at(3)) is not None:
                    act.wait_ge(hq_turned, i.t + 1)
                    free_again(act, q_down, 0, i, 2)
                    act.copy(hqT[:, i.par, :, :], p_hq.rearrange("p (c q) -> p c q", q=P)).then_inc(hq_copied, 1)
            tile_steps(act, body, QFF_DEPTH)

        round_col = sb("round_col", [P, 1])

        def qff_prepare_tensor(pe):
            pe.wait_ge(qw_step, 1)
            pe.wait_ge(setup_zero, 2)
            pe.matmul(ps[:, 7, 0:4], ones[:, :], q_sum[:, 0:4], start=True, stop=True).then_inc(qw_turned, 1)
            for n in range(3):
                pe.wait_ge(qw_step, 3 + 3 * n + 3)
                if n == 2:
                    pe.wait_ge(qw_copied, 1)
                for c in range(4):
                    src = q_int[:, n, P * c:P * c + P]
                    last = pe.transpose(p16[:, 1024 * (n % 2) + P * c:1024 * (n % 2) + P * c + P], src, ident16[:, :])
                last.then_inc(qw_turned, 1)

        def qff_tensor(pe):
            x_ready(pe, 1)
            pe.wait_ge(qw_copied, 3)
            for g in range(4):
                pe.wait_ge(xq_ready, g + 1)
                if g >= 2:
                    pe.wait_ge(xq_copied, g - 1)
                for j in range(4):
                    last = pe.transpose(p16[:, 1024 * (g % 2) + P * j:1024 * (g % 2) + P * j + P], xq[:, 4 * g + j, :], ident16[:, :])
                last.then_inc(xq_turned, 1)
            pe.wait_ge(xq_copied, 4)

            def body(at):
                if (i := at(3)) is not None:
                    pe.wait_ge(hq_ready, i.t + 1)
                    free_again(pe, hq_copied, 0, i, 1)
                    for c in range(4):
                        last = pe.transpose(p_hq[:, P * c:P * c + P], hq[:, i.par, P * c:P * c + P], ident16[:, :])
                    last.then_inc(hq_turned, 1)
                if (i := at(0)) is not None:
                    r = i.par
                    free_again(pe, hid_ready, 0, i, 2)
                    pe.matmul(ps[:, Q_G[r], :], xqT[:, i.t, :], qw[:, 0, :], start=True, stop=True)
                    pe.matmul(ps[:, Q_U[r], :], xqT[:, i.t, :], qw[:, 1, :], start=True, stop=True).then_inc(gu_ready, 1)
                if (i := at(4)) is not None:
                    r = i.par
                    pe.wait_ge(hq_copied, i.t + 1)
                    free_again(pe, x_done, 16, i, 2)
                    for c in range(4):
                        last = pe.matmul(ps[:, Q_Y + r, 0:P], hqT[:, r, c, :], qw[:, 2, P * c:P * c + P], start=(c == 0), stop=(c == 3))
                    last.then_inc(q_down, 1)
            tile_steps(pe, body, QFF_DEPTH)

        BANK_T, BANK_G, BANK_U, BANK_Y = 0, (2, 3), (4, 5), (6, 7)

        class Pass:

            def __init__(self, n, par, half, least):
                self.n, self.par, self.half, self.least = n, par, half, least

            def next(self):
                return Pass(self.n + 1, 1 - self.par, self.half + self.par, self.least + 1)

        def expert_passes(eng, M, body):
            def fixed(n):
                body(Pass(n, n % 2, n // 2, n), n + 1 < M.passes)
            fixed(0)
            fixed(1)
            ends = (M.passes - 1) // 2
            with eng.Fori(1, ends) as pair:
                for r in range(2):
                    body(Pass(pair * 2 + r, r, pair, 2 + r), True)
            for n in range(2 * ends, M.passes):
                fixed(n)

        def weights_sync(sp, M, n, more=True):
            L, r = M.layer, n.par
            if L == 2:
                wait_free(sp, moe_y, 4 * base_passes[L], 4, n)
                for k, name in enumerate(("L2_ffn_w1", "L2_ffn_w3")):
                    sp.dma_start(w_up[:, r, k, 0:256], a[name][n.n]).then_inc(w_loaded[r], 16)
                sp.dma_start(w_dn[:, r, 0:2, :], a["L2_ffn_w2"][n.n].rearrange("(c p) d -> p c d", p=P)).then_inc(w_loaded[r], 16)
                return
            if L == 3 and n.least >= 2:
                wait_free(sp, w_turned2, 0, 1, n)
            else:
                wait_free(sp, w_turned, base_turned[L], 1, n)
            if L == 1:
                if isinstance(n.n, int) and n.n == 0:
                    gu = a["L1_ffn_shared_gu"]
                    sp.dma_start(w_nat[:, r, 0, 0:P], gu[0:P, :]).then_inc(w_loaded[r], 16)
                    sp.dma_start(w_nat[:, r, 1, 0:P], gu[P:2 * P, :]).then_inc(w_loaded[r], 16)
                    sp.dma_start(w_nat[:, r, 2, 0:P], a["L1_ffn_shared_down"]).then_inc(w_loaded[r], 16)
                else:
                    sp.dma_start(w_nat[:, r, 0, 0:P], a["L1_ffn_w1"][n.n - 1]).then_inc(w_loaded[r], 16)
                    sp.dma_start(w_nat[:, r, 2, 0:P], a["L1_ffn_w2"][n.n - 1]).then_inc(w_loaded[r], 16)
                return
            for k, name in enumerate(("L3_ffn_W1", "L3_ffn_W2")):
                for c, (off, size) in enumerate(M.pieces):
                    sp.dma_start(w_nat[0:size, r, k, P * c:P * c + P], a[name][n.n, off:off + size, :]).then_inc(w_loaded[r], 16)
            sp.dma_start(w_nat[:, r, 2, 0:352], a["L3_ffn_W3"][n.n]).then_inc(w_loaded[r], 16)

        def wait_free(eng, s, base, per, n, lag=2):
            if base + per * (n.least - lag + 1) > 0:
                eng.wait_ge(s, base + per * (n.n - lag + 1))

        def moe_sync(sp, M):
            L = M.layer
            if L == 2:
                sp.wait_ge(moe_y, 4 * base_passes[2])
                sp.wait_ge(w_copied, base_turned[2])
            expert_passes(sp, M, lambda n, more: weights_sync(sp, M, n))

        def turn_weights(pe, M, n):
            L, r = M.layer, n.par
            if not M.turned:
                return
            pe.wait_ge(w_loaded[r], 16 * loads_until(L, n, n.half))
            wait_free(pe, w_copied, base_turned[L], 1, n, 1)
            shared = L == 1 and isinstance(n.n, int) and n.n == 0
            if L == 3:
                for k in range(2):
                    for c, (off, size) in enumerate(M.pieces):
                        pe.transpose(ps[:, BANK_T + k, off:off + size], w_nat[0:size, r, k, P * c:P * c + P], ident[0:size, 0:size])
                last = pe.transpose(ps[:, BANK_T, 352:480], w_nat[:, r, 2, 0:P], ident)
                last = pe.transpose(ps[:, BANK_T + 1, 352:480], w_nat[:, r, 2, P:2 * P], ident)
                last.then_inc(w_turned, 1)
            else:
                last = pe.transpose(ps[:, BANK_T, 0:P], w_nat[:, r, 0, 0:P], ident)
                if shared:
                    last = pe.transpose(ps[:, BANK_T, P:2 * P], w_nat[:, r, 1, 0:P], ident)
                last = pe.transpose(ps[:, BANK_T + 1, 0:P], w_nat[:, r, 2, 0:P], ident)
                last.then_inc(w_turned, 1)

        def moe_tensor(pe, M):
            L, nc_ = M.layer, len(M.pieces)
            ub, yb, sub = base_units[L], 4 * base_passes[L], 2 * L + 1
            x_ready(pe, sub)
            if L != 2:
                k = 0 if L == 1 else 1
                pe.transpose(ps[:, 7, 0:16], gate_nat[:, k, :], ident[0:16, 0:16]).then_inc(gate_turned, 1)
                pe.wait_ge(gate_copied, k + 1)

            for g in range(4):
                pe.wait_ge(moe_xn, 4 * (L - 1) + g + 1)
                if g >= 2:
                    pe.wait_ge(x_copied, 4 * (L - 1) + g - 1)
                for j in range(4):
                    last = pe.transpose(ps[:, BANK_G[g % 2], P * j:P * j + P], xn_all[:, 4 * g + j, :], ident)
                last.then_inc(x_turned, 1)
            for g in range(4):
                pe.wait_ge(x_copied, 4 * (L - 1) + g + 1)
                for t in range(4 * g, 4 * g + 4):
                    last = pe.matmul(ps[:, BANK_Y[1], 16 * t:16 * t + 16], xT[:, t, :], gate_w[:, L - 1, :], start=True, stop=True)
            last.then_inc(logits_done, 1)
            turn_weights(pe, M, Pass(0, 0, 0, 0))

            def body(n, more):
                r = n.par
                if M.turned:
                    pe.wait_ge(w_copied, base_turned[L] + n.n + 1)
                else:
                    pe.wait_ge(w_loaded[r], 16 * loads_until(L, n, n.half))
                up = L != 1 or (isinstance(n.n, int) and n.n == 0)

                def down(g):
                    pe.wait_ge(units_h, ub + M.units * n.n + nc_ * (g + 1))
                    if g == 1 and isinstance(n.n, int) and n.n == 0:
                        pe.wait_ge(logits_copied, L)
                    wait_free_group(pe, moe_used, yb, n, g, 2)
                    for j in range(4):
                        for c, (off, size) in enumerate(M.pieces):
                            last = pe.matmul(ps[:, BANK_Y[g % 2], P * j:P * j + P], h[0:size, g % 2, c, P * j:P * j + P],
                                             w_dn[0:size, r, c, :], start=(c == 0), stop=(c == nc_ - 1))
                    last.then_inc(moe_y, 1)

                for g in range(4):
                    for c, (off, size) in enumerate(M.pieces):
                        k = g * nc_ + c
                        if ub + M.units * n.least + k - 1 > ub:
                            pe.wait_ge(units_h, ub + M.units * n.n + k - 1)
                        s = k % 2
                        rhs = xT[:, 4 * g:4 * g + 4, :].rearrange("p t q -> p (t q)")
                        last = pe.matmul(ps[0:size, BANK_G[s], :], w_up[:, r, 0, off:off + size], rhs, start=True, stop=True)
                        if up:
                            last = pe.matmul(ps[0:size, BANK_U[s], :], w_up[:, r, 1, off:off + size], rhs, start=True, stop=True)
                        last.then_inc(units_up, 1)
                    if g:
                        down(g - 1)
                if more:
                    turn_weights(pe, M, n.next())
                down(3)
            expert_passes(pe, M, body)

        def wait_free_group(eng, s, base, n, g, lag):
            if base + 4 * n.least + g - lag + 1 > 0:
                eng.wait_ge(s, base + 4 * n.n + g - lag + 1)

        def moe_scalar(act, M):
            L, nc_ = M.layer, len(M.pieces)
            ub, yb = base_units[L], 4 * base_passes[L]
            if L != 2:
                k = 0 if L == 1 else 1
                act.wait_ge(gate_turned, k + 1)
                act.copy(gate_w[:, L - 1, :], ps[:, 7, 0:16]).then_inc(gate_copied, 1)

            for g in range(4):
                act.wait_ge(x_turned, 4 * (L - 1) + g + 1)
                act.copy(xT[:, 4 * g:4 * g + 4, :], ps[:, BANK_G[g % 2], :].rearrange("p (t q) -> p t q", q=P)).then_inc(x_copied, 1)
            act.wait_ge(logits_done, L)
            act.copy(logit[:, :, :], ps[:, BANK_Y[1], 0:256].rearrange("p (t e) -> p t e", e=16)).then_inc(logits_copied, 1)
            copy_weights(act, M, Pass(0, 0, 0, 0))
            if L < 3:
                act.wait_ge(route_asked, L)
                if L == 1:
                    act.activation(ex[:, :, :], cent[:, :, :], ACT.Exp).then_inc(route_exp, 1)
                else:
                    act.activation(rz[:, :], rmax[:, :], ACT.Tanh, scale=0.5).then_inc(route_exp, 1)

            def body(n, more):
                r = n.par
                up = L != 1 or (isinstance(n.n, int) and n.n == 0)
                for g in range(4):
                    for c, (off, size) in enumerate(M.pieces):
                        k = g * nc_ + c
                        act.wait_ge(units_up, ub + M.units * n.n + k + 1)
                        if up:
                            if ub + M.units * n.least + k - 1 > 0:
                                act.wait_ge(units_h, ub + M.units * n.n + k - 1)
                            act.activation(sg[0:size, k % 2, :], ps[0:size, BANK_G[k % 2], :], ACT.Silu).then_inc(units_silu, 1)
                        else:
                            wait_free_group(act, moe_y, yb, n, g, 2)
                            act.activation(h[0:size, g % 2, c, :], ps[0:size, BANK_G[k % 2], :], ACT.Silu).then_inc(units_h, 1)
                if more:
                    copy_weights(act, M, n.next())
            expert_passes(act, M, body)

        def copy_weights(act, M, n):
            L, r = M.layer, n.par
            if not M.turned:
                return
            act.wait_ge(w_turned, base_turned[L] + n.n + 1)
            wait_free(act, moe_y, 4 * base_passes[L], 4, n)
            if L == 3:
                act.copy(w_up[:, r, 0, 0:352], ps[:, BANK_T, 0:352])
                act.copy(w_up[:, r, 1, 0:352], ps[:, BANK_T + 1, 0:352])
                act.copy(w_dn[:, r, 0:2, :], ps[:, BANK_T:BANK_T + 2, 352:480]).then_inc(w_part, 1)
                act.wait_ge(w_turned2, n.n + 1)
                act.copy(w_dn[0:96, r, 2, :], ps[0:96, BANK_T, 0:P]).then_inc(w_copied, 1)
            else:
                wide = 256 if isinstance(n.n, int) and n.n == 0 else 128
                if wide == 256:
                    act.copy(w_up[:, r, 0:2, 0:P], ps[:, BANK_T, 0:256].rearrange("p (k q) -> p k q", k=2))
                else:
                    act.copy(w_up[:, r, 0, 0:P], ps[:, BANK_T, 0:P])
                act.copy(w_dn[:, r, 0, :], ps[:, BANK_T + 1, 0:P]).then_inc(w_copied, 1)

        w_part, w_turned2 = sem("w_part"), sem("w_turned2")

        plain_turn = turn_weights

        def turn_weights(pe, M, n):
            plain_turn(pe, M, n)
            if M.layer == 3:
                pe.wait_ge(w_part, n.n + 1)
                pe.transpose(ps[0:96, BANK_T, 0:P], w_nat[:, n.par, 2, 256:352], ident).then_inc(w_turned2, 1)

        def moe_vector(dve, M):
            L, nc_ = M.layer, len(M.pieces)
            ub, yb, sub = base_units[L], 4 * base_passes[L], 2 * L + 1
            K, E = {1: 4, 2: 2, 3: 2}[L], M.experts

            dve.wait_ge(x_stats, 16 * (L + 1))
            norm_roots(dve, 0)
            for g in range(4):
                for t in range(4 * g, 4 * g + 4):
                    ins = dve.tensor_scalar(xn_all[:, t, :], x[:, t, :], moments[:, 0, t, 0:1], rstd[:, 0, t:t + 1],
                                            ALU.subtract, ALU.mult)
                ins.then_inc(moe_xn, 1)

            link = [link_base[L]]

            def linked(ins):
                link[0] += 1
                ins.then_inc(route_link, 1)
                dve.wait_ge(route_link, link[0])
            dve.wait_ge(logits_copied, L)
            wide = lambda col, n: col.unsqueeze(2).broadcast_to([P, TILES, n])
            if L == 1:
                linked(dve.tensor_reduce(rmax[:, :], logit[:, :, :], AX.X, ALU.max))
                dve.tensor_tensor(cent[:, :, :], logit[:, :, :], wide(rmax[:, :], 16), ALU.subtract).then_inc(route_asked, 1)
                dve.wait_ge(route_exp, 1)
                linked(dve.tensor_reduce(rz[:, :], ex[:, :, :], AX.X, ALU.add))
                linked(dve.reciprocal(rzi[:, :], rz[:, :]))
                linked(dve.tensor_tensor(logit[:, :, :], ex[:, :, :], wide(rzi[:, :], 16), ALU.mult))
            for t in range(TILES):
                ins = dve.max(best[:, t, :], logit[:, t, 0:E])
            linked(ins)
            for t in range(TILES):
                ins = dve.max_index(besti[:, t, :], best[:, t, :], logit[:, t, 0:E])
            linked(ins)
            linked(dve.tensor_copy(bestf[:, :, :], besti[:, :, :]))
            gate = gates[:, 4 + L:5 + L]
            if L == 1:
                linked(dve.tensor_reduce(rz[:, :], best[:, :, 0:4], AX.X, ALU.add))
                linked(dve.reciprocal(rzi[:, :], rz[:, :]))
                linked(dve.tensor_scalar(rz[:, :], rzi[:, :], gate, None, ALU.mult))
                linked(dve.tensor_tensor(wk[:, :, :], best[:, :, 0:4], wide(rz[:, :], 4), ALU.mult))
            elif L == 2:
                dve.tensor_tensor(rmax[:, :], best[:, :, 0], best[:, :, 1], ALU.subtract).then_inc(route_asked, 1)
                dve.wait_ge(route_exp, 2)
                linked(dve.tensor_scalar(wk[:, :, 0], rz[:, :], 0.5, 0.5, ALU.mult, ALU.add))
                linked(dve.tensor_scalar(wk[:, :, 1], rz[:, :], -0.5, 0.5, ALU.mult, ALU.add))
                linked(dve.tensor_scalar(wk[:, :, 0:2], wk[:, :, 0:2], gate, None, ALU.mult))
            else:
                linked(dve.tensor_scalar(wk[:, :, 0:2], best[:, :, 0:2], gate, None, ALU.mult))
            first = M.shared
            dst = ew[:, :, first:first + E]
            for k in range(K):
                number = iota[:, 0:E].unsqueeze(1).broadcast_to([P, TILES, E])
                linked(dve.tensor_tensor(hit[:, :, 0:E], number, wide(bestf[:, :, k], E), ALU.is_equal))
                if k == 0:
                    linked(dve.tensor_tensor(dst, hit[:, :, 0:E], wide(wk[:, :, k], E), ALU.mult))
                else:
                    linked(dve.tensor_tensor(hitw[:, :, 0:E], hit[:, :, 0:E], wide(wk[:, :, k], E), ALU.mult))
                    linked(dve.tensor_tensor(dst, dst, hitw[:, :, 0:E], ALU.add))
            if M.shared:
                linked(dve.tensor_scalar(ew[:, :, 0], ew[:, :, 1], 0.0, gate, ALU.mult, ALU.add))
            link_base[L + 1] = link[0]

            def body(n, more):
                up = L != 1 or (isinstance(n.n, int) and n.n == 0)

                def add(g):
                    dve.wait_ge(moe_y, yb + 4 * n.n + g + 1)
                    wait_free(dve, moe_used, yb + g, 4, n, 1) if n.least else None
                    for j in range(4):
                        t = 4 * g + j
                        last = dve.scalar_tensor_tensor(x[:, t, :], ps[:, BANK_Y[g % 2], P * j:P * j + P], ew[:, t, bass.ds(n.n, 1)],
                                                        x[:, t, :], ALU.mult, ALU.add)
                    last.then_inc(moe_used, 1)
                    if not more and L < 3:
                        dve.wait_ge(moe_used, yb + 4 * n.n + g + 1)
                        for t in range(4 * g, 4 * g + 4):
                            last = dve.bn_stats(stats[:, t, :], x[:, t, :])
                        last.then_inc(moe_stats, 1)

                for g in range(4):
                    for c, (off, size) in enumerate(M.pieces):
                        k = g * nc_ + c
                        if up:
                            dve.wait_ge(units_silu, sb_[L] + M.units * n.n + k + 1)
                            wait_free_group(dve, moe_y, yb, n, g, 2)
                            dve.tensor_tensor(h[0:size, g % 2, c, :], sg[0:size, k % 2, :], ps[0:size, BANK_U[k % 2], :],
                                              ALU.mult).then_inc(units_h, 1)
                    if g:
                        add(g - 1)
                add(3)
            expert_passes(dve, M, body)

        link_base = {1: 0}
        sb_ = {1: 0, 2: 4, 3: 4 + 8 * 8}

        NAMES = {0: ("L0_xattn_Wq", "L0_xattn_Wk", "L0_xattn_Wv", None),
                 1: ("L1_xattn_Wq", "L1_xattn_Wk", "L1_xattn_Wv", "L1_xattn_Wo"),
                 2: ("L2_xattn_Wq", "L2_xattn_Wk", "L2_xattn_Wv", "L2_xattn_Wo"),
                 3: ("L3_xattn_w_q", "L3_xattn_w_k", "L3_xattn_w_v", "L3_xattn_w_o")}
        COLS = [(0, 0, "L0_xattn_bq"), (0, 1, "L0_xattn_bk"), (1, 0, "L1_xattn_bq"), (1, 1, "L1_xattn_bk"),
                (3, 0, "L3_xattn_b_q"), (3, 1, "L3_xattn_b_k")]
        ROWS = [(0, 0, "L0_xattn_bv"), (1, 0, "L1_xattn_bv"), (1, 1, "L1_xattn_bo"), (2, 1, "L2_xattn_bo"),
                (3, 0, "L3_xattn_b_v"), (3, 1, "L3_xattn_b_o")]
        SETUP = 16 * (5 + 3 + 3)
        LATER = 16 * (12 + 4 + 5 + 4 + 3 + 3 + 3)

        def column(name):
            return a[name].rearrange("(p n) -> p n", n=1)

        def row(name):
            return a[name].rearrange("(n p) -> n p", n=1)

        def setup_sync(sp):
            n = [0]
            signal = [setup_loaded]

            def load(to, src):
                n[0] += 16
                sp.dma_start(to, src).then_inc(signal[0], 16)

            def weights(L):
                for k, name in enumerate(NAMES[L]):
                    if name:
                        rows = P if k in (0, 3) else CTX
                        load(att_w[0:rows, L, k, :], a[name])
                for l, k, name in COLS:
                    if l == L:
                        load(att_col[:, L, k:k + 1], column(name))
                for l, k, name in ROWS:
                    if l == L:
                        load(att_row[0:1, L, k, :], row(name))
            load(x[:, :, :], a["x"].rearrange("(t b) s d -> (b s) t d", b=2))
            load(const[:, :], a["const"])
            load(ctx_all[:, :, :], a["ctx_768"].rearrange("(t b) s d -> (b s) t d", b=2))
            load(gates[:, 0:4], row("g_xattn").broadcast_to([P, 4]))
            load(gates[:, 4:8], row("g_ffn").broadcast_to([P, 4]))
            sp.wait_ge(setup_zero, 3)
            weights(0)
            assert n[0] == SETUP, n
            n[0], signal[0] = 0, later_loaded

            def later():
                load(q_nat[:, 0, :].rearrange("p (c d) -> p c d", d=P), a["L0_ffn_w_gate"].rearrange("(c p) d -> p c d", p=P))
                load(q_nat[:, 1, :].rearrange("p (c d) -> p c d", d=P), a["L0_ffn_w_up"].rearrange("(c p) d -> p c d", p=P))
                load(q_nat[:, 2, :], a["L0_ffn_w_down"])
                for L in range(1, 4):
                    weights(L)
                for L, name in ((1, "L1_xattn_bv"), (3, "L3_xattn_b_v"), (0, "L0_xattn_bv")):
                    load(value_col[:, L:L + 1], column(name))
                load(ln_col[:, 0:1], column("L1_xattn_ln1_g"))
                load(ln_col[:, 1:2], column("L1_xattn_ln1_b"))
                load(ln_col[0:CTX, 2:3], column("L1_xattn_ln2_g"))
                load(ln_col[0:CTX, 3:4], column("L1_xattn_ln2_b"))
                load(gate_nat[:, 0, :], a["L1_ffn_gate_w"])
                load(gate_nat[0:8, 1, :], a["L3_ffn_Wg"])
                load(gate_w[:, 1, 0:8], a["L2_ffn_w_gate"])
                assert n[0] == LATER, (n, LATER)
            return later

        def setup_pool(pool):
            pool.memset(att_w[:, :, :, :], 0.0)
            pool.memset(att_col[:, :, :], 0.0)
            pool.memset(ones[:, :], 1.0)
            pool.memset(ln_col[:, :], 0.0)
            pool.memset(gate_nat[:, :, :], 0.0)
            pool.memset(gate_w[:, :, :], 0.0).then_inc(setup_zero, 3)
            pool.memset(ctx_nat[:, :, :], 0.0)
            pool.memset(ctx_norm[:, :, :], 0.0)
            pool.memset(round_col[:, :], ROUND)
            pool.memset(q_sum[:, :], 0.0)
            pool.memset(qz[:, :, :, :], 0.0)
            pool.memset(vx[:, :, :, :, :], 0.0).then_inc(setup_pad, 1)

        def setup_vector(dve):
            dve.wait_ge(setup_loaded, SETUP)
            dve.wait_ge(setup_pad, 1)
            dve.tensor_copy(ident16[:, :], ident).then_inc(setup_done, 1)
            for t in range(TILES):
                for b in range(2):
                    ins = dve.tensor_copy(vx[:, t, b, :, 16:18], value_mask.rearrange("p (m j e) -> p m j e", j=2, e=HEAD)[:, :, :, 0])

        def later_vector(dve):
            dve.wait_ge(later_loaded, LATER)
            for L in range(2, 4):
                dve.tensor_scalar(key_bias4[:, L, :], head_mask, att_col[:, L, 1:2], None, ALU.mult)
            for L in (1, 3):
                ins = dve.tensor_scalar(value_bias[:, L, :], ones[:, :], value_col[:, L:L + 1], None, ALU.mult)
            ins.then_inc(later_done, 1)
            qff_prepare_vector(dve)

        block = ctx.enter_context(nc.Block())

        @block.sync
        def _(sp):
            later = setup_sync(sp)
            sp.wait_ge(setup_pad, 1)
            for L in range(4):
                if 2 * L < stop_after:
                    att_sync(sp, ATT[L], later if L == 0 else None)
                if L and 2 * L + 1 < stop_after:
                    moe_sync(sp, MOES[L])
            for g in range(4):
                if stop_after == 8:
                    sp.wait_ge(moe_used, 4 * (base_passes[3] + 7) + g + 1)
                else:
                    x_ready(sp, stop_after)
                sp.dma_start(out_d[:, 4 * g:4 * g + 4, :], x[:, 4 * g:4 * g + 4, :]).then_inc(stored, 16)
            sp.wait_ge(stored, 64)

        @block.gpsimd
        def _(pool):
            setup_pool(pool)

        @block.scalar
        def _(act):
            act.wait_ge(setup_loaded, SETUP)
            act.wait_ge(setup_done, 1)
            act.activation(gates[:, :], gates[:, :], ACT.Tanh).then_inc(gates_done, 1)
            for L in range(4):
                if 2 * L < stop_after:
                    att_scalar(act, ATT[L])
                if L == 0:
                    act.wait_ge(later_loaded, LATER)
                    act.wait_ge(later_done, 1)
                    qff_turn_weights(act)
                if 2 * L + 1 < stop_after:
                    qff_scalar(act) if L == 0 else moe_scalar(act, MOES[L])

        @block.tensor
        def _(pe):
            pe.wait_ge(setup_loaded, SETUP)
            pe.wait_ge(setup_done, 1)
            for L in range(4):
                if 2 * L < stop_after:
                    att_tensor(pe, ATT[L])
                if L == 0:
                    x_ready(pe, 1)
                    pe.wait_ge(later_loaded, LATER)
                    pe.wait_ge(later_done, 1)
                    qff_prepare_tensor(pe)
                if 2 * L + 1 < stop_after:
                    qff_tensor(pe) if L == 0 else moe_tensor(pe, MOES[L])

        @block.vector
        def _(dve):
            setup_vector(dve)
            dve.wait_ge(gates_done, 1)
            for L in range(4):
                if 2 * L < stop_after:
                    att_vector(dve, ATT[L])
                if L == 0:
                    later_vector(dve)
                if 2 * L + 1 < stop_after:
                    qff_vector(dve) if L == 0 else moe_vector(dve, MOES[L])


_INS = ["x", "ctx_768", "g_xattn", "g_ffn",
        "L0_xattn_Wq", "L0_xattn_bq", "L0_xattn_Wk", "L0_xattn_bk", "L0_xattn_Wv", "L0_xattn_bv",
        "L0_ffn_w_gate", "L0_ffn_w_up", "L0_ffn_w_down",
        "L1_xattn_ln1_g", "L1_xattn_ln1_b", "L1_xattn_ln2_g", "L1_xattn_ln2_b",
        "L1_xattn_Wq", "L1_xattn_bq", "L1_xattn_Wk", "L1_xattn_bk", "L1_xattn_Wv", "L1_xattn_bv",
        "L1_xattn_Wo", "L1_xattn_bo",
        "L1_ffn_gate_w", "L1_ffn_w1", "L1_ffn_w2", "L1_ffn_shared_gu", "L1_ffn_shared_down",
        "L2_xattn_Wq", "L2_xattn_Wk", "L2_xattn_Wv", "L2_xattn_Wo", "L2_xattn_bo",
        "L2_ffn_w_gate", "L2_ffn_w1", "L2_ffn_w3", "L2_ffn_w2",
        "L3_xattn_w_q", "L3_xattn_b_q", "L3_xattn_w_k", "L3_xattn_b_k", "L3_xattn_w_v", "L3_xattn_b_v",
        "L3_xattn_w_o", "L3_xattn_b_o",
        "L3_ffn_Wg", "L3_ffn_W1", "L3_ffn_W2", "L3_ffn_W3"]
STOP = 8


def kernel(**inputs):
    import numpy as _np
    import concourse.bacc as _bacc
    from concourse import mybir as _mybir
    from concourse.bass_utils import run_bass_kernel_spmd as _run

    nc = _bacc.Bacc("TRN2", target_bir_lowering=False, num_devices=1)
    arrays, aps = {}, {}
    for name in _INS + ["const"]:
        a = constants() if name == "const" else _np.ascontiguousarray(inputs[name])
        arrays[f"in_{name}_dram"] = a
        aps[name] = nc.dram_tensor(f"in_{name}_dram", a.shape, _mybir.dt.from_np(a.dtype), kind="ExternalInput").ap()
    out = nc.dram_tensor("out_0_dram", (SEQS, LEN, DIM), F32, kind="ExternalOutput").ap()
    build(nc, aps, out, STOP)
    r = _run(nc, [arrays], core_ids=[0])
    return r.results[0]["out_0_dram"]
```

```python
from contextlib import ExitStack

import numpy as np

import concourse.bass as bass
from concourse import mybir

F32 = mybir.dt.float32
BF16 = mybir.dt.bfloat16
F32R = mybir.dt.float32r
U32 = mybir.dt.uint32
I32 = mybir.dt.int32
ALU = mybir.AluOpType
ACT = mybir.ActivationFunctionType
AX = mybir.AxisListType

P = 128
SEQS, LEN, DIM = 32, 64, 128
CTX = 96
TILES = SEQS * LEN // P
EPS = 1e-5
HEADS, HEAD = 16, 8
INNER = 512
ROUND = 1.5 * 2.0 ** 23
FAR = -1.0e30
HIGH_BITS = 0xFFFFF000
ATT_DEPTH = 8
QFF_DEPTH = 6

C_IDENT, C_HEAD, C_VALUE, C_SEQ, C_IOTA, C_END = 0, 128, 132, 260, 388, 404


def constants():
    c = np.zeros((P, C_END), np.float32)
    row = np.arange(P)
    c[:, C_IDENT:C_HEAD] = np.eye(P)
    c[:, C_HEAD:C_VALUE] = (row[:, None] // HEAD) % 4 == np.arange(4)[None, :]
    c[:, C_VALUE:C_SEQ] = (row[:, None] // LEN) == (row[None, :] // HEAD) % 2
    c[:, C_SEQ:C_IOTA] = np.where(row[:, None] // LEN == row[None, :] // LEN, 0.0, FAR)
    c[:, C_IOTA:C_END] = np.arange(16)[None, :]
    return c


class Tile:

    def __init__(self, pair, r, least_pair):
        self.t = pair * 2 + r
        self.par = r % 2
        self.half = pair + r // 2
        self.least = least_pair * 2 + r


def tile_steps(eng, body, depth):
    def steps(pair, least, ends):
        for r in range(2):
            def at(d, r=r):
                tile = Tile(pair, r - d, least)
                if ends and not 0 <= tile.t < TILES:
                    return None
                return tile
            body(at)

    first = (depth + 3) // 2
    for pair in range(first):
        steps(pair, pair, True)
    with eng.Fori(first, TILES // 2) as pair:
        steps(pair, first, False)
    for pair in range(TILES // 2, (TILES + depth + 1) // 2):
        steps(pair, pair, True)


def build(nc, a, out):
    with ExitStack() as ctx:
        def sb(name, shape, dt=F32):
            return ctx.enter_context(nc.sbuf_tensor(name, shape, dt))

        def sem(name):
            return ctx.enter_context(nc.semaphore(name))

        x = sb("x", [P, TILES, DIM])
        const = sb("const", [P, C_END])
        ident = const[:, C_IDENT:C_HEAD]
        head_mask = const[:, C_HEAD:C_VALUE]
        value_mask = const[:, C_VALUE:C_SEQ]
        seq_mask = const[:, C_SEQ:C_IOTA]
        iota = const[:, C_IOTA:C_END]
        ident16 = sb("ident16", [P, P], BF16)
        ones = sb("ones", [P, P])
        gates = sb("gates", [P, 8])
        att_w = sb("att_w", [P, 4, 4, P])
        att_col = sb("att_col", [P, 4, 2])
        att_row = sb("att_row", [1, 4, 2, P])
        ln_col = sb("ln_col", [P, 4])
        key_bias4 = sb("key_bias4", [P, 4, 4])
        ctx_nat = sb("ctx_nat", [P, 2, P])
        ctx_norm = sb("ctx_norm", [P, 2, P])
        ctx_all = sb("ctx_all", [P, TILES, CTX])
        xn_all = sb("xn_all", [P, TILES, P])
        stats = sb("stats", [P, 2, TILES, 6])
        moments = sb("moments", [P, 3, TILES, 2])
        rstd = sb("rstd", [P, 3, TILES])
        nr_a = sb("nr_a", [P, 3, TILES])
        nr_i = sb("nr_i", [P, 3, TILES], I32)
        nr_t = sb("nr_t", [P, 3, TILES])
        xn = sb("xn", [P, 2, P])
        xnn = sb("xnn", [P, 2, P])
        inT = sb("inT", [P, 2, 2, P])
        ctx2 = sb("ctx2", [P, 2, 2, 2, LEN])
        qT = sb("qT", [P, 2, P])
        qz = sb("qz", [P, 2, 4, P])
        kT = sb("kT", [P, 2, P])
        kx = sb("kx", [P, 2, 2, 4, LEN])
        vx = sb("vx", [P, TILES, 2, 8, 18])
        top = sb("top", [P, 2, HEADS])
        prob = sb("prob", [P, 2, HEADS * LEN])
        probT = sb("probT", [P, 2, 8, P])
        rsum = sb("rsum", [P, 2, HEADS])
        rinv = sb("rinv", [P, 2, HEADS])
        rgate = sb("rgate", [P, 2])
        on = sb("on", [P, 2, P])
        oT = sb("oT", [P, 2, P])
        bias_row = sb("bias_row", [P, P])
        value_col = sb("value_col", [P, 4])
        value_bias = sb("value_bias", [P, 4, P])
        space = sb("space", [P, 6144])
        q_nat = space[:, 0:1536].rearrange("p (n c) -> p n c", n=3)
        q_tmp = space[:, 1536:3072].rearrange("p (n c) -> p n c", n=3)
        q_int = sb("q_int", [P, 3, INNER], BF16)
        qw = sb("qw", [P, 3, INNER], BF16)
        q_sum = sb("q_sum", [P, 8])
        q_mean = sb("q_mean", [P, 8])
        q_scale = sb("q_scale", [P, 8])
        q_top = sb("q_top", [P, 3, TILES])
        q_gu = sb("q_gu", [P, TILES, 2])
        hs_col = sb("hs_col", [P, 2, 2])
        hs_inv = sb("hs_inv", [P, 2])
        hs_down = sb("hs_down", [P, TILES])
        xq = sb("xq", [P, TILES, P], BF16)
        xqT = sb("xqT", [P, TILES, P], BF16)
        sil = space[:, 3072:4096].rearrange("p (r c) -> p r c", r=2)
        hid = space[:, 4096:5120].rearrange("p (r c) -> p r c", r=2)
        hq_t = space[:, 5120:6144].rearrange("p (r c) -> p r c", r=2)
        hq = sb("hq", [P, 2, INNER], BF16)
        hqT = sb("hqT", [P, 2, 4, P], BF16)
        xT = sb("xT", [P, TILES, P])
        v1 = xT
        gate_nat = sb("gate_nat", [16, 2, P])
        gate_w = sb("gate_w", [P, 3, 16])
        logit = sb("logit", [P, TILES, 16])
        cent = sb("cent", [P, TILES, 16])
        ex = sb("ex", [P, TILES, 16])
        rmax = sb("rmax", [P, TILES])
        rz = sb("rz", [P, TILES])
        rzi = sb("rzi", [P, TILES])
        best = sb("best", [P, TILES, 8])
        besti = sb("besti", [P, TILES, 8], U32)
        bestf = sb("bestf", [P, TILES, 8])
        wk = sb("wk", [P, TILES, 4])
        hit = sb("hit", [P, TILES, 16])
        hitw = sb("hitw", [P, TILES, 16])
        ew = sb("ew", [P, TILES, 17])
        w_nat = space[:, 3072:5376].rearrange("p (r k c) -> p r k c", r=2, k=3)
        w_raw = space[:, 5376:6144].rearrange("p (k c) -> p k c", k=2)
        w_mask = sb("w_mask", [P, 2, 384])
        x_hi, x_lo = sb("x_hi", [P, TILES, P], F32R), sb("x_lo", [P, TILES, P], F32R)
        w_hi, w_lo = sb("w_hi", [P, 2, 2, 384], F32R), sb("w_lo", [P, 2, 2, 384], F32R)
        w_dn = sb("w_dn", [P, 2, 3, P])
        sg = sb("sg", [P, 2, 512])
        h = space[:, 0:3072].rearrange("p (r c q) -> p r c q", r=2, c=3)

        ps = ctx.enter_context(nc.psum_tensor("ps", [P, 8, 512], F32))
        p_score = ps[:, 0:4, 0:256]
        p_oT = ps[:, 4, 0:P]
        p_o = ps[:, 5, 0:288].rearrange("p (m b c) -> p m b c", m=8, b=2)
        p_in = ps[:, 6, 0:256]
        p_qk = ps[:, 6, 0:256]
        p_v = ps[:, 7, 0:256]
        p_y = ps[:, 7, 0:P]

        setup_loaded, later_loaded = sem("setup_loaded"), sem("later_loaded")
        x_loaded, ctx_all_loaded, q_loaded = sem("x_loaded"), sem("ctx_all_loaded"), sem("q_loaded")
        setup_zero = sem("setup_zero")
        setup_pad = sem("setup_pad")
        setup_done, later_done = sem("setup_done"), sem("later_done")
        gates_done = sem("gates_done")
        ctx_loaded = [sem("ctx_loaded0"), sem("ctx_loaded1")]
        ctx_placed = sem("ctx_placed")
        ln_link = sem("ln_link")
        xn_ready = sem("xn_ready")
        xnn_ready = sem("xnn_ready")
        row_done, row_copied, x_biased = sem("row_done"), sem("row_copied"), sem("x_biased")
        x_stats, ctx_stats, moe_stats = sem("x_stats"), sem("ctx_stats"), sem("moe_stats")
        in_turned, in_copied = sem("in_turned"), sem("in_copied")
        qk_projected, v_projected = sem("qk_projected"), sem("v_projected")
        qk_copied, v_copied = sem("qk_copied"), sem("v_copied")
        scored, top_ready, centered, exped = sem("scored"), sem("top_ready"), sem("centered"), sem("exped")
        p_turned, p_copied_act, p_copied_dve = sem("p_turned"), sem("p_copied_act"), sem("p_copied_dve")
        attended, sum_inverted, normed = sem("attended"), sem("sum_inverted"), sem("normed")
        o_turned, o_copied, y_done = sem("o_turned"), sem("o_copied"), sem("y_done")
        x_done = sem("x_done")
        qw_step, qw_rounded, qw_turned, qw_copied = sem("qw_step"), sem("qw_rounded"), sem("qw_turned"), sem("qw_copied")
        q_gu_ready, hs_top, hs_floor, q_stats = sem("q_gu_ready"), sem("hs_top"), sem("hs_floor"), sem("q_stats")
        q_down = sem("q_down")
        xq_ready, xq_turned, xq_copied = sem("xq_ready"), sem("xq_turned"), sem("xq_copied")
        gu_ready, silu_done, hid_ready = sem("gu_ready"), sem("silu_done"), sem("hid_ready")
        hs_ready, hq_scaled, hq_ready = sem("hs_ready"), sem("hq_scaled"), sem("hq_ready")
        hq_turned, hq_copied = sem("hq_turned"), sem("hq_copied")
        moe_xn, x_turned, x_copied = sem("moe_xn"), sem("x_turned"), sem("x_copied")
        gate_turned, gate_copied = sem("gate_turned"), sem("gate_copied")
        logits_done, logits_copied = sem("logits_done"), sem("logits_copied")
        route_link, route_asked, route_exp = sem("route_link"), sem("route_asked"), sem("route_exp")
        w_loaded = [sem("w_loaded0"), sem("w_loaded1")]
        w_turned, w_copied = sem("w_turned"), sem("w_copied")
        w_part, w_turned2 = sem("w_part"), sem("w_turned2")
        units_up, units_silu, units_h = sem("units_up"), sem("units_silu"), sem("units_h")
        moe_y, moe_used = sem("moe_y"), sem("moe_used")
        x_masked, x_low, x_high = sem("x_masked"), sem("x_low"), sem("x_high")
        w_masked, w_low, w_high = sem("w_masked"), sem("w_low"), sem("w_high")
        stored = sem("stored")

        ctx_d = a["ctx_768"].rearrange("(t b) s d -> t (b s) d", b=2)
        out_d = out.rearrange("(t b) s d -> (b s) t d", b=2)

        class Moe:
            def __init__(self, layer, experts, shared, pieces, turned):
                self.layer, self.experts, self.shared = layer, experts, shared
                self.pieces, self.turned = pieces, turned
                self.passes = experts + shared
                self.units = 4 * len(pieces)
        MOES = {1: Moe(1, 16, 1, [(0, 128)], True),
                2: Moe(2, 8, 0, [(0, 128), (128, 128)], False),
                3: Moe(3, 8, 0, [(0, 128), (128, 128), (256, 96)], True)}
        base_units, base_passes, base_turned, base_loads = {}, {}, {}, {}
        u = p_ = tn = 0
        for L, m in MOES.items():
            base_units[L], base_passes[L], base_turned[L] = u, p_, tn
            u += m.units * m.passes
            p_ += m.passes
            tn += m.passes if m.turned else 0
        LOADS = {1: 2, 2: 3, 3: 7}
        def loads_of(L, n):
            return 3 if L == 1 and n == 0 else LOADS[L]
        for par in range(2):
            c = 0
            for L, m in MOES.items():
                base_loads[L, par] = c
                c += sum(loads_of(L, n) for n in range(par, m.passes, 2))

        def loads_until(L, n, half):
            extra = 1 if L == 1 and n.par == 0 else 0
            return (half + 1) * LOADS[L] + base_loads[L, n.par] + extra

        def x_ready(eng, sub, tile=None):
            if sub == 0:
                return
            L = (sub - 1) // 2
            if sub % 2 == 0 and L >= 1:
                eng.wait_ge(moe_used, 4 * (base_passes[L] + MOES[L].passes))
            else:
                base = {1: 0, 2: 16, 3: 32, 5: 48, 7: 64}[sub]
                eng.wait_ge(x_done, base + (TILES if tile is None else tile.t + 1))
        xn_base = {0: 0, 4: 16, 6: 32}
        x_done_base = {0: 0, 1: 16, 2: 32, 4: 48, 6: 64}

        class Att:
            def __init__(self, L):
                self.L, self.sub, self.base = L, 2 * L, 16 * L
                self.multi = L >= 2
                self.mbase = 16 * (L - 2)
                self.obase = 16 * (L - 1)
                self.scale = [1.0, P ** -0.5, HEAD ** -0.5, HEAD ** -0.5][L]
                self.p_oT, self.p_y, self.p_qk = (p_oT, p_y, p_qk) if self.multi else (ps[:, 1, 0:P], ps[:, 2, 0:P], ps[:, 3, 0:256])
        ATT = [Att(L) for L in range(4)]

        def free_again(eng, s, base, tile, lag, per=1):
            if base + per * (tile.least - lag + 1) > 0:
                eng.wait_ge(s, base + per * (tile.t - lag + 1))

        def att_sync(sp, A):
            def body(at):
                if (i := at(0)) is not None:
                    free_again(sp, in_turned, A.base, i, 2)
                    sp.dma_start(ctx_nat[:, i.par, 0:CTX], ctx_d[i.t]).then_inc(ctx_loaded[i.par], 16)
            tile_steps(sp, body, 0)

        def att_pool(pool, A):
            def body(at):
                if (i := at(0)) is not None:
                    free_again(pool, in_turned, A.base, i, 2)
                    pool.tensor_copy(ctx_nat[:, i.par, 0:CTX], ctx_all[:, i.t, :]).then_inc(ctx_placed, 1)
            tile_steps(pool, body, 0)

        def att_vector(dve, A):
            x_ready(dve, A.sub)
            if A.L == 0:
                qff_scales(dve)
                dve.wait_ge(ctx_all_loaded, 16)
            else:
                if A.L == 1:
                    dve.wait_ge(q_stats, TILES)
                else:
                    dve.wait_ge(moe_stats, 4 * (A.L - 1))
                norm_roots(dve, 0)
            dve.wait_ge(row_done, A.L + 1)
            dve.tensor_scalar(bias_row[:, :], ps[:, 7, 0:P], gates[:, A.L:A.L + 1], None, ALU.mult).then_inc(row_copied, 1)
            dve.wait_ge(row_copied, A.L + 1)
            if A.L == 1:
                second = moments[:, 2, :, 1]
                linked_ln(dve, dve.tensor_tensor(second, moments[:, 0, :, 1], rstd[:, 0, :], ALU.mult))
                linked_ln(dve, dve.tensor_tensor(second, second, rstd[:, 0, :], ALU.mult))
                norm_roots(dve, 2)
                linked_ln(dve, dve.tensor_tensor(rstd[:, 2, :], rstd[:, 2, :], rstd[:, 0, :], ALU.mult))

            def body(at):
                if A.multi and (i := at(5)) is not None:
                    dve.wait_ge(p_turned, A.base + i.t + 1)
                    free_again(dve, attended, A.base, i, 2)
                    dve.tensor_copy(probT[:, i.par, 4:8, :], ps[:, 5, :].rearrange("p (m q) -> p m q", q=P)).then_inc(p_copied_dve, 1)
                if A.L >= 1 and (i := at(7)) is not None:
                    dve.wait_ge(y_done, A.obase + i.t + 1)
                    dve.wait_ge(x_biased, A.base + i.t + 1)
                    dve.scalar_tensor_tensor(x[:, i.t, :], A.p_y, gates[:, A.L:A.L + 1], x[:, i.t, :],
                                             ALU.mult, ALU.add).then_inc(x_done, 1)
                if (i := at(0)) is not None:
                    free_again(dve, in_turned, A.base, i, 2)
                    if A.L != 1:
                        norm_tile(dve, A.sub, i)
                    else:
                        r = i.par
                        dve.tensor_scalar(xnn[:, r, :], x[:, i.t, :], moments[:, 0, i.t, 0:1], rstd[:, 2, bass.ds(i.t, 1)],
                                          ALU.subtract, ALU.mult)
                        dve.tensor_scalar(ctx_norm[:, r, 0:CTX], ctx_all[:, i.t, :], moments[:, 1, i.t, 0:1],
                                          rstd[:, 1, bass.ds(i.t, 1)], ALU.subtract, ALU.mult).then_inc(xnn_ready, 1)
                i, o = at(4), at(5)
                if not A.multi:
                    if i is not None:
                        dve.wait_ge(scored, A.base + i.t + 1)
                        free_again(dve, p_turned, A.base, i, 2)
                        dve.scalar_tensor_tensor(prob[:, i.par, 0:P], ps[:, 0, 0:P], A.scale, seq_mask, ALU.mult, ALU.add).then_inc(top_ready, 1)
                    if o is not None:
                        dve.wait_ge(exped, A.base + o.t + 1)
                        dve.reciprocal(rinv[:, o.par, 0:1], rsum[:, o.par, 0:1]).then_inc(sum_inverted, 1)
                    if i is not None:
                        dve.wait_ge(top_ready, A.base + i.t + 1)
                        dve.tensor_reduce(top[:, i.par, 0:1], prob[:, i.par, 0:P], AX.X, ALU.max, negate=True).then_inc(centered, 1)
                    if o is not None:
                        dve.wait_ge(sum_inverted, A.base + o.t + 1)
                        if A.L == 0:
                            dve.tensor_scalar(rgate[:, o.par:o.par + 1], rinv[:, o.par, 0:1], gates[:, 0:1], None, ALU.mult).then_inc(normed, 1)
                elif i is not None:
                    r = i.par
                    dve.wait_ge(scored, A.base + i.t + 1)
                    free_again(dve, p_turned, A.base, i, 2)
                    sc = p_score.rearrange("p g (n k) -> p g n k", k=LEN)
                    tp = top[:, r, :].rearrange("p (g n) -> p g n", g=4)
                    dve.tensor_reduce(tp, sc, AX.X, ALU.max).then_inc(top_ready, 1)
                    dve.wait_ge(top_ready, A.base + i.t + 1)
                    dve.tensor_tensor(prob[:, r, :].rearrange("p (g n k) -> p g n k", g=4, k=LEN), sc,
                                      tp.unsqueeze(3).broadcast_to([P, 4, 4, LEN]), ALU.subtract).then_inc(centered, 1)
                if (i := at(5)) is not None:
                    r = i.par
                    dve.wait_ge(attended, A.base + i.t + 1)
                    if A.multi:
                        for b in range(2):
                            rows = slice(LEN * b, LEN * b + LEN)
                            last = dve.reciprocal(rinv[rows, r, :].rearrange("p (m j) -> p m j", j=2), p_o[rows, :, b, 16:18])
                        last.then_inc(sum_inverted, 1)
                        free_again(dve, o_turned, A.obase, i, 2)
                        dve.wait_ge(sum_inverted, A.base + i.t + 1)
                        for b in range(2):
                            rows = slice(LEN * b, LEN * b + LEN)
                            last = dve.tensor_tensor(on[rows, r, :].rearrange("p (m j e) -> p m j e", j=2, e=HEAD),
                                                     p_o[rows, :, b, 0:16].rearrange("p m (j e) -> p m j e", j=2),
                                                     rinv[rows, r, :].rearrange("p (m j) -> p m j", j=2).unsqueeze(3)
                                                     .broadcast_to([LEN, 8, 2, HEAD]), ALU.mult)
                        last.then_inc(normed, 1)
                    else:
                        if A.L == 0:
                            dve.wait_ge(normed, A.base + i.t + 1)
                            dve.wait_ge(x_biased, A.base + i.t + 1)
                            dve.scalar_tensor_tensor(x[:, i.t, :], ps[:, 5, 0:P], rgate[:, r:r + 1], x[:, i.t, :],
                                                     ALU.mult, ALU.add).then_inc(x_done, 1)
                        else:
                            free_again(dve, o_turned, A.obase, i, 2)
                            dve.tensor_scalar(on[:, r, :], ps[:, 5, 0:P], rinv[:, r, 0:1], None, ALU.mult).then_inc(normed, 1)
                if (i := at(2)) is not None:
                    r = i.par
                    dve.wait_ge(v_projected, A.base + i.t + 1)
                    if A.multi:
                        for b in range(2):
                            last = dve.tensor_tensor(vx[:, i.t, b, :, 0:16], p_v[:, P * b:P * b + P].rearrange("p (m c) -> p m c", c=16),
                                                     value_mask.rearrange("p (m c) -> p m c", c=16), ALU.mult)
                        last.then_inc(v_copied, 1)
                    else:
                        dve.tensor_copy(v1[:, i.t, :], p_v[:, 0:P]).then_inc(v_copied, 1)
                if (i := at(2)) is not None:
                    dve.wait_ge(in_turned, A.base + i.t + 1)
                    dve.tensor_tensor(x[:, i.t, :], x[:, i.t, :], bias_row[:, :], ALU.add).then_inc(x_biased, 1)
                if A.L == 0 and (i := at(0)) is not None:
                    dve.bn_stats(stats[:, 1, i.t, :], ctx_all[:, i.t, :]).then_inc(ctx_stats, 1)
                if (i := at(8)) is not None:
                    dve.wait_ge(x_done, x_done_base[A.sub] + i.t + 1)
                    tile_stats(dve, i, A.base)
            tile_steps(dve, body, ATT_DEPTH)

        ln_links = [0]

        def linked_ln(dve, ins):
            ln_links[0] += 1
            ins.then_inc(ln_link, 1)
            dve.wait_ge(ln_link, ln_links[0])

        def tile_stats(dve, i, base):
            dve.bn_stats(stats[:, 0, i.t, :], x[:, i.t, :]).then_inc(x_stats, 1)

        def all_stats(dve, src):
            for t in range(TILES):
                ins = dve.bn_stats(stats[:, 0, t, :], src[:, t, :])
            linked_ln(dve, ins)

        def norm_roots(dve, first, last=None):
            last = first if last is None else last

            def linked(ins):
                linked_ln(dve, ins)
            for n in range(first, min(last, 1) + 1):
                for t in range(TILES):
                    ins = dve.bn_aggr(moments[:, n, t, :], stats[:, n, t, :])
            if first < 2:
                linked(ins)
            some = slice(first, last + 1)
            root, var, half, guess = rstd[:, some, :], nr_a[:, some, :], nr_t[:, some, :], nr_i[:, some, :]
            linked(dve.tensor_scalar(var, moments[:, some, :, 1], EPS, None, ALU.add))
            linked(dve.tensor_scalar(guess, var.bitcast(I32), 1, None, ALU.arith_shift_right))
            linked(dve.tensor_scalar(root.bitcast(I32), guess, -1.0, float(0x5F3759DF), ALU.mult, ALU.add))
            for _ in range(3):
                linked(dve.tensor_tensor(half, var, root, ALU.mult))
                linked(dve.scalar_tensor_tensor(half, half, -0.5, root, ALU.mult, ALU.mult))
                linked(dve.scalar_tensor_tensor(root, half, 1.5, root, ALU.add, ALU.mult))

        def norm_tile(dve, sub, i):
            dve.tensor_scalar(xn[:, i.par, :], x[:, i.t, :], moments[:, 0, i.t, 0:1], rstd[:, 0, bass.ds(i.t, 1)],
                              ALU.subtract, ALU.mult).then_inc(xn_ready, 1)

        def att_scalar(act, A):
            def body(at):
                if (i := at(5)) is not None:
                    act.wait_ge(p_turned, A.base + i.t + 1)
                    free_again(act, attended, A.base, i, 2)
                    if A.multi:
                        act.copy(probT[:, i.par, 0:4, :], ps[:, 4, :].rearrange("p (m q) -> p m q", q=P)).then_inc(p_copied_act, 1)
                    else:
                        act.copy(probT[:, i.par, 0, :], ps[:, 4, 0:P]).then_inc(p_copied_act, 1)
                if (i := at(1)) is not None:
                    r = i.par
                    act.wait_ge(in_turned, A.base + i.t + 1)
                    free_again(act, v_projected, A.base, i, 2)
                    if A.L == 1:
                        act.activation(inT[:, r, 0, :], p_in[:, 0:P], ACT.Identity, bias=ln_col[:, 1:2], scale=ln_col[:, 0:1])
                        act.activation(inT[:, r, 1, :], p_in[:, P:2 * P], ACT.Identity, bias=ln_col[:, 3:4],
                                       scale=ln_col[:, 2:3]).then_inc(in_copied, 1)
                    elif A.multi:
                        act.copy(inT[:, r, 0, :], p_in[:, 0:P])
                        act.copy(ctx2[:, r, :, :, :], p_in[:, P:2 * P].rearrange("p (b k) -> p b k", b=2).unsqueeze(2)
                                 .broadcast_to([P, 2, 2, LEN])).then_inc(in_copied, 1)
                    else:
                        act.copy(inT[:, r, :, :], p_in.rearrange("p (a q) -> p a q", a=2)).then_inc(in_copied, 1)
                if A.L >= 1 and (i := at(6)) is not None:
                    act.wait_ge(o_turned, A.obase + i.t + 1)
                    free_again(act, y_done, A.obase, i, 2)
                    act.copy(oT[:, i.par, :], A.p_oT).then_inc(o_copied, 1)
                if (i := at(4)) is not None:
                    r = i.par
                    act.wait_ge(centered, A.base + i.t + 1)
                    if A.multi:
                        act.activation(prob[:, r, :], prob[:, r, :], ACT.Exp, scale=A.scale).then_inc(exped, 1)
                    else:
                        free_again(act, sum_inverted, A.base, i, 2)
                        act.activation(prob[:, r, 0:P], prob[:, r, 0:P], ACT.Exp, bias=top[:, r, 0:1],
                                       accum_out=rsum[:, r, 0:1]).then_inc(exped, 1)
                if (i := at(2)) is not None:
                    r = i.par
                    act.wait_ge(qk_projected, A.base + i.t + 1)
                    free_again(act, scored, A.base, i, 2)
                    if not A.multi:
                        act.activation(qT[:, r, :], A.p_qk[:, 0:P], ACT.Identity, bias=att_col[:, A.L, 0:1])
                    if A.multi:
                        for g in range(4):
                            rows = slice(32 * g, 32 * g + 32)
                            act.activation(qz[rows, r, g, :], A.p_qk[rows, 0:P], ACT.Identity, bias=att_col[rows, A.L, 0:1])
                        for n in range(4):
                            last = act.activation(kx[:, r, :, n, :], A.p_qk[:, P:2 * P].rearrange("p (b k) -> p b k", b=2),
                                                  ACT.Identity, bias=key_bias4[:, A.L, n:n + 1], scale=head_mask[:, n:n + 1])
                        last.then_inc(qk_copied, 1)
                    else:
                        act.activation(kT[:, r, :], A.p_qk[:, P:2 * P], ACT.Identity, bias=att_col[:, A.L, 1:2]).then_inc(qk_copied, 1)
            tile_steps(act, body, ATT_DEPTH)

        def att_tensor(pe, A):
            wq, wk_, wv, wo = (att_w[:, A.L, n, :] for n in range(4))

            def body(at):
                if (i := at(5)) is not None:
                    r = i.par
                    pe.wait_ge(exped, A.base + i.t + 1)
                    free_again(pe, p_copied_act, A.base, i, 1)
                    if A.multi:
                        free_again(pe, o_copied, A.obase, i, 2)
                        free_again(pe, normed, A.base, i, 1)
                        for m in range(8):
                            last = pe.transpose(ps[:, 4 + m // 4, P * (m % 4):P * (m % 4) + P], prob[:, r, P * m:P * m + P], ident)
                    else:
                        last = pe.transpose(ps[:, 4, 0:P], prob[:, r, 0:P], ident)
                    last.then_inc(p_turned, 1)
                if A.L >= 1 and (i := at(7)) is not None:
                    pe.wait_ge(o_copied, A.obase + i.t + 1)
                    if A.multi:
                        v = at(3)
                        pe.wait_ge(v_copied, A.base + (v.t + 1 if v is not None else TILES))
                    free_again(pe, x_done, x_done_base[A.sub], i, 1)
                    pe.matmul(A.p_y, oT[:, i.par, :], wo, start=True, stop=True).then_inc(y_done, 1)
                if (i := at(1)) is not None:
                    r = i.par
                    if A.L == 1:
                        pe.wait_ge(xnn_ready, i.t + 1)
                    else:
                        pe.wait_ge(xn_ready, xn_base[A.sub] + i.t + 1)
                        if A.L == 0:
                            pe.wait_ge(ctx_loaded[r], 16 * (i.half + 1))
                        else:
                            pe.wait_ge(ctx_placed, A.mbase + i.t + 1)
                    if A.multi:
                        free_again(pe, qk_copied, A.base, i, 2)
                    free_again(pe, in_copied, A.base, i, 1)
                    pe.transpose(p_in[:, 0:P], (xnn if A.L == 1 else xn)[:, r, :], ident)
                    pe.transpose(p_in[:, P:2 * P], (ctx_norm if A.L == 1 else ctx_nat)[:, r, :], ident).then_inc(in_turned, 1)
                if A.L >= 1 and (i := at(6)) is not None:
                    pe.wait_ge(normed, A.base + i.t + 1)
                    if A.multi:
                        p = at(5)
                        pe.wait_ge(p_copied_act, A.base + (p.t + 1 if p is not None else TILES))
                    free_again(pe, o_copied, A.obase, i, 1)
                    pe.transpose(A.p_oT, on[:, i.par, :], ident).then_inc(o_turned, 1)

                def project(i):
                    r = i.par
                    n = at(1) if A.multi else i
                    pe.wait_ge(in_copied, A.base + (n.t + 1 if n is not None else TILES))
                    free_again(pe, qk_copied, A.base, i, 1)
                    pe.matmul(A.p_qk[:, 0:P], wq, inT[:, r, 0, :], start=True, stop=True)
                    keys = ctx2[:, r, :, 0, :] if A.multi else inT[:, r, 1, :]
                    pe.matmul(A.p_qk[:, P:2 * P], wk_, keys, start=True, stop=True).then_inc(qk_projected, 1)
                if not A.multi and (i := at(2)) is not None:
                    project(i)
                if (i := at(5)) is not None:
                    r = i.par
                    pe.wait_ge(p_copied_act, A.base + i.t + 1)
                    pe.wait_ge(v_copied, A.base + i.t + 1)
                    if A.multi:
                        pe.wait_ge(p_copied_dve, A.mbase + i.t + 1)
                        for m in range(8):
                            last = pe.matmul(p_o[:, m, :, :], probT[:, r, m, :], vx[:, i.t, :, m, :], start=True, stop=True)
                    else:
                        free_again(pe, x_done if A.L == 0 else normed, A.base, i, 1)
                        last = pe.matmul(ps[:, 5, 0:P], probT[:, r, 0, :], v1[:, i.t, :], start=True, stop=True)
                    last.then_inc(attended, 1)
                if A.multi and (i := at(2)) is not None:
                    project(i)
                if (i := at(2)) is not None:
                    r = i.par
                    free_again(pe, v_copied, A.base, i, 1)
                    if A.multi:
                        free_again(pe, x_done, x_done_base[A.sub], i, 5)
                    for b in range(2 if A.multi else 1):
                        keys = ctx2[:, r, b, :, :].rearrange("p j k -> p (j k)") if A.multi else inT[:, r, 1, :]
                        last = pe.matmul(p_v[:, P * b:P * b + P], keys, wv, start=True, stop=True)
                    last.then_inc(v_projected, 1)
                if (i := at(3)) is not None:
                    r = i.par
                    pe.wait_ge(qk_copied, A.base + i.t + 1)
                    free_again(pe, centered if A.multi else top_ready, A.base, i, 1)
                    if A.multi:
                        for b in range(2):
                            for g in range(4):
                                last = pe.matmul(ps[LEN * b:LEN * b + LEN, g, 0:256], qz[:, r, g, LEN * b:LEN * b + LEN],
                                                 kx[:, r, b, :, :].rearrange("p n k -> p (n k)"), start=True, stop=True)
                    else:
                        last = pe.matmul(ps[:, 0, 0:P], qT[:, r, :], kT[:, r, :], start=True, stop=True)
                    last.then_inc(scored, 1)
            x_ready(pe, A.sub)
            if A.L == 0:
                pe.matmul(ps[:, 7, 0:P], ones[0:1, :], att_row[0:1, 0, 0, :], start=True, stop=True).then_inc(row_done, 1)
                qff_sum_tensor(pe)
            else:
                if A.L != 2:
                    pe.matmul(ps[:, 7, 0:P], value_bias[:, A.L, :], wo, start=True, stop=False)
                pe.matmul(ps[:, 7, 0:P], ones[0:1, :], att_row[0:1, A.L, 1, :], start=A.L == 2, stop=True).then_inc(row_done, 1)
            pe.wait_ge(row_copied, A.L + 1)

            tile_steps(pe, body, ATT_DEPTH)

        Q_G, Q_U, Q_T, Q_Y = (0, 1), (2, 3), 4, 6
        p16 = ps[:, 4:6, :].rearrange("p b n -> p (b n)").bitcast(BF16)
        p_xq = p16[:, 0:P]
        p_hq = p16[:, 1024:1024 + 512]

        def qff_scales(dve):
            link = [0]

            def linked(ins):
                link[0] += 1
                ins.then_inc(qw_step, 1)
                dve.wait_ge(qw_step, link[0])
            dve.wait_ge(q_loaded, 48)
            linked(dve.tensor_reduce(q_sum[:, 0:3], q_nat[:, :, :], AX.X, ALU.add, apply_absolute_value=True))
            dve.wait_ge(qw_turned, 1)
            linked(dve.tensor_scalar(q_mean[:, 0:3], ps[:, 3, 0:3], 1.0 / (INNER * DIM), EPS, ALU.mult, ALU.max))
            linked(dve.reciprocal(q_scale[:, 0:3], q_mean[:, 0:3]))
            linked(dve.tensor_scalar(q_mean[:, 6:7], q_mean[:, 2:3], gates[:, 4:5], None, ALU.mult))

        def qff_round_weights(pool):
            link = [0]

            def linked(ins):
                link[0] += 1
                ins.then_inc(qw_rounded, 1)
                pool.wait_ge(qw_rounded, link[0])
            pool.wait_ge(qw_step, 3)
            for n in range(3):
                linked(pool.tensor_scalar(q_tmp[:, n, :], q_nat[:, n, :], q_scale[:, n:n + 1], 1.0, ALU.mult, ALU.min))
                linked(pool.tensor_scalar(q_tmp[:, n, :], q_tmp[:, n, :], -1.0, ROUND, ALU.max, ALU.add))
                linked(pool.tensor_scalar(q_int[:, n, :], q_tmp[:, n, :], -ROUND, None, ALU.add))

        def qff_vector(dve):
            dve.wait_ge(x_stats, TILES)
            dve.wait_ge(ctx_stats, TILES)
            norm_roots(dve, 0, 1)
            for t in range(TILES):
                ins = dve.tensor_scalar(xn_all[:, t, :], x[:, t, :], moments[:, 0, t, 0:1], rstd[:, 0, t:t + 1],
                                        ALU.subtract, ALU.mult)
            linked_ln(dve, ins)
            linked_ln(dve, dve.tensor_reduce(q_top[:, 0, :], xn_all[:, :, :], AX.X, ALU.max, apply_absolute_value=True))
            linked_ln(dve, dve.tensor_scalar(q_top[:, 1, :], q_top[:, 0, :], EPS, 1.0 / 127.0, ALU.max, ALU.mult))
            linked_ln(dve, dve.reciprocal(q_top[:, 2, :], q_top[:, 1, :]))
            for t in range(TILES):
                ins = dve.tensor_scalar(xn_all[:, t, :], xn_all[:, t, :], q_top[:, 2, t:t + 1], ROUND, ALU.mult, ALU.add)
            linked_ln(dve, ins)
            for g in range(4):
                dve.tensor_scalar(xq[:, 4 * g:4 * g + 4, :], xn_all[:, 4 * g:4 * g + 4, :], -ROUND, None, ALU.add).then_inc(xq_ready, 1)
            for k in range(2):
                ins = dve.tensor_scalar(q_gu[:, :, k], q_top[:, 1, :], q_mean[:, k:k + 1], None, ALU.mult)
            ins.then_inc(q_gu_ready, 1)
            dve.wait_ge(q_gu_ready, 1)

            def body(at):
                if (i := at(5)) is not None:
                    dve.wait_ge(q_down, i.t + 1)
                    dve.wait_ge(hs_ready, 2 * i.t + 2)
                    dve.scalar_tensor_tensor(x[:, i.t, :], ps[:, Q_Y + i.par, 0:P], hs_down[:, bass.ds(i.t, 1)], x[:, i.t, :],
                                             ALU.mult, ALU.add).then_inc(x_done, 1)
                if (i := at(3)) is not None:
                    r = i.par
                    dve.wait_ge(hq_scaled, i.t + 1)
                    free_again(dve, hq_turned, 0, i, 2)
                    dve.tensor_scalar(hq[:, r, :], hq_t[:, r, :], -ROUND, None, ALU.add).then_inc(hq_ready, 1)
                if (i := at(1)) is not None:
                    r = i.par
                    dve.wait_ge(silu_done, i.t + 1)
                    free_again(dve, hq_scaled, 0, i, 2)
                    dve.scalar_tensor_tensor(hid[:, r, :], ps[:, Q_U[r], :], q_gu[:, i.t, 1:2], sil[:, r, :],
                                             ALU.mult, ALU.mult).then_inc(hid_ready, 1)
                if (i := at(1)) is not None:
                    r = i.par
                    dve.wait_ge(hid_ready, i.t + 1)
                    dve.tensor_reduce(hs_col[:, r, 0:1], hid[:, r, :], AX.X, ALU.max, apply_absolute_value=True).then_inc(hs_top, 1)
                if (i := at(6)) is not None:
                    dve.wait_ge(x_done, 16 + i.t + 1)
                    dve.bn_stats(stats[:, 0, i.t, :], x[:, i.t, :]).then_inc(q_stats, 1)
                if (i := at(1)) is not None:
                    r = i.par
                    dve.wait_ge(hs_top, i.t + 1)
                    dve.tensor_scalar(hs_col[:, r, 1:2], hs_col[:, r, 0:1], EPS, 1.0 / 127.0, ALU.max, ALU.mult).then_inc(hs_floor, 1)
                if (i := at(1)) is not None:
                    r = i.par
                    dve.wait_ge(hs_floor, i.t + 1)
                    dve.reciprocal(hs_inv[:, r:r + 1], hs_col[:, r, 1:2]).then_inc(hs_ready, 1)
                    dve.tensor_scalar(hs_down[:, bass.ds(i.t, 1)], hs_col[:, r, 1:2], q_mean[:, 6:7], None, ALU.mult).then_inc(hs_ready, 1)
            tile_steps(dve, body, QFF_DEPTH)

        def qff_turn_weights(act):
            for n in range(3):
                act.wait_ge(qw_turned, n + 2)
                act.copy(qw[:, n, :], p16[:, 1024 * (n % 2):1024 * (n % 2) + 512]).then_inc(qw_copied, 1)

        def qff_scalar(act):
            for g in range(4):
                act.wait_ge(xq_turned, g + 1)
                act.copy(xqT[:, 4 * g:4 * g + 4, :], p16[:, 1024 * (g % 2):1024 * (g % 2) + 512].rearrange("p (t q) -> p t q", q=P)).then_inc(xq_copied, 1)
            act.wait_ge(q_gu_ready, 1)

            def body(at):
                if (i := at(2)) is not None:
                    r = i.par
                    act.wait_ge(hs_ready, 2 * i.t + 2)
                    free_again(act, hq_ready, 0, i, 2)
                    act.activation(hq_t[:, r, :], hid[:, r, :], ACT.Identity, bias=round_col[:, 0:1], scale=hs_inv[:, r:r + 1]).then_inc(hq_scaled, 1)
                if (i := at(0)) is not None:
                    r = i.par
                    act.wait_ge(gu_ready, i.t + 1)
                    free_again(act, hid_ready, 0, i, 2)
                    act.activation(sil[:, r, :], ps[:, Q_G[r], :], ACT.Silu, scale=q_gu[:, i.t, 0:1]).then_inc(silu_done, 1)
                if (i := at(3)) is not None:
                    act.wait_ge(hq_turned, i.t + 1)
                    free_again(act, q_down, 0, i, 2)
                    act.copy(hqT[:, i.par, :, :], p_hq.rearrange("p (c q) -> p c q", q=P)).then_inc(hq_copied, 1)
            tile_steps(act, body, QFF_DEPTH)

        round_col = sb("round_col", [P, 1])

        def qff_sum_tensor(pe):
            pe.wait_ge(qw_step, 1)
            pe.matmul(ps[:, 3, 0:4], ones[:, :], q_sum[:, 0:4], start=True, stop=True).then_inc(qw_turned, 1)

        def qff_prepare_tensor(pe):
            for n in range(3):
                pe.wait_ge(qw_rounded, 3 * n + 3)
                if n == 2:
                    pe.wait_ge(qw_copied, 1)
                for c in range(4):
                    src = q_int[:, n, P * c:P * c + P]
                    last = pe.transpose(p16[:, 1024 * (n % 2) + P * c:1024 * (n % 2) + P * c + P], src, ident16[:, :])
                last.then_inc(qw_turned, 1)

        def qff_tensor(pe):
            x_ready(pe, 1)
            pe.wait_ge(qw_copied, 3)
            for g in range(4):
                pe.wait_ge(xq_ready, g + 1)
                if g >= 2:
                    pe.wait_ge(xq_copied, g - 1)
                for j in range(4):
                    last = pe.transpose(p16[:, 1024 * (g % 2) + P * j:1024 * (g % 2) + P * j + P], xq[:, 4 * g + j, :], ident16[:, :])
                last.then_inc(xq_turned, 1)
            pe.wait_ge(xq_copied, 4)

            def body(at):
                if (i := at(0)) is not None:
                    r = i.par
                    free_again(pe, hid_ready, 0, i, 2)
                    pe.matmul(ps[:, Q_G[r], :], xqT[:, i.t, :], qw[:, 0, :], start=True, stop=True)
                    pe.matmul(ps[:, Q_U[r], :], xqT[:, i.t, :], qw[:, 1, :], start=True, stop=True).then_inc(gu_ready, 1)
                if (i := at(4)) is not None:
                    r = i.par
                    pe.wait_ge(hq_copied, i.t + 1)
                    free_again(pe, x_done, 16, i, 2)
                    for c in range(4):
                        last = pe.matmul(ps[:, Q_Y + r, 0:P], hqT[:, r, c, :], qw[:, 2, P * c:P * c + P], start=(c == 0), stop=(c == 3))
                    last.then_inc(q_down, 1)
                if (i := at(3)) is not None:
                    pe.wait_ge(hq_ready, i.t + 1)
                    free_again(pe, hq_copied, 0, i, 1)
                    for c in range(4):
                        last = pe.transpose(p_hq[:, P * c:P * c + P], hq[:, i.par, P * c:P * c + P], ident16[:, :])
                    last.then_inc(hq_turned, 1)
            tile_steps(pe, body, QFF_DEPTH)

        BANK_T, BANK_G, BANK_U, BANK_Y = 0, (2, 3), (4, 5), (6, 7)

        class Pass:

            def __init__(self, n, par, half, least):
                self.n, self.par, self.half, self.least = n, par, half, least

            def next(self):
                return Pass(self.n + 1, 1 - self.par, self.half + self.par, self.least + 1)

        def expert_passes(eng, M, body):
            def fixed(n):
                body(Pass(n, n % 2, n // 2, n), n + 1 < M.passes)
            fixed(0)
            fixed(1)
            ends = (M.passes - 1) // 2
            with eng.Fori(1, ends) as pair:
                for r in range(2):
                    body(Pass(pair * 2 + r, r, pair, 2 + r), True)
            for n in range(2 * ends, M.passes):
                fixed(n)

        def weights_sync(sp, M, n, more=True):
            L, r = M.layer, n.par
            if L == 2:
                wait_free(sp, moe_y, 4 * base_passes[L], 4, n)
                for k, name in enumerate(("L2_ffn_w1", "L2_ffn_w3")):
                    sp.dma_start(w_nat[:, r, k, 0:256], a[name][n.n]).then_inc(w_loaded[r], 16)
                sp.dma_start(w_dn[:, r, 0:2, :], a["L2_ffn_w2"][n.n].rearrange("(c p) d -> p c d", p=P)).then_inc(w_loaded[r], 16)
                return
            if L == 3 and n.least >= 2:
                wait_free(sp, w_turned2, 0, 1, n)
            else:
                wait_free(sp, w_turned, base_turned[L], 1, n)
            if L == 1:
                if isinstance(n.n, int) and n.n == 0:
                    gu = a["L1_ffn_shared_gu"]
                    sp.dma_start(w_nat[:, r, 0, 0:P], gu[0:P, :]).then_inc(w_loaded[r], 16)
                    sp.dma_start(w_nat[:, r, 1, 0:P], gu[P:2 * P, :]).then_inc(w_loaded[r], 16)
                    sp.dma_start(w_nat[:, r, 2, 0:P], a["L1_ffn_shared_down"]).then_inc(w_loaded[r], 16)
                else:
                    sp.dma_start(w_nat[:, r, 0, 0:P], a["L1_ffn_w1"][n.n - 1]).then_inc(w_loaded[r], 16)
                    sp.dma_start(w_nat[:, r, 2, 0:P], a["L1_ffn_w2"][n.n - 1]).then_inc(w_loaded[r], 16)
                return
            for k, name in enumerate(("L3_ffn_W1", "L3_ffn_W2")):
                for c, (off, size) in enumerate(M.pieces):
                    sp.dma_start(w_nat[0:size, r, k, P * c:P * c + P], a[name][n.n, off:off + size, :]).then_inc(w_loaded[r], 16)
            sp.dma_start(w_nat[:, r, 2, 0:352], a["L3_ffn_W3"][n.n]).then_inc(w_loaded[r], 16)

        def wait_free(eng, s, base, per, n, lag=2):
            if base + per * (n.least - lag + 1) > 0:
                eng.wait_ge(s, base + per * (n.n - lag + 1))

        def moe_sync(sp, M):
            L = M.layer
            if L == 1:
                sp.wait_ge(x_done, 32)
            if L == 2:
                sp.wait_ge(moe_y, 4 * base_passes[2])
                sp.wait_ge(w_copied, base_turned[2])
            if L == 3:
                sp.wait_ge(moe_y, 4 * base_passes[3])
            expert_passes(sp, M, lambda n, more: weights_sync(sp, M, n))

        def turn_weights(pe, M, n):
            L, r = M.layer, n.par
            if not M.turned:
                return
            pe.wait_ge(w_loaded[r], 16 * loads_until(L, n, n.half))
            wait_free(pe, w_copied, base_turned[L], 1, n, 1)
            shared = L == 1 and isinstance(n.n, int) and n.n == 0
            if L == 3:
                for k in range(2):
                    for c, (off, size) in enumerate(M.pieces):
                        pe.transpose(ps[:, BANK_T + k, off:off + size], w_nat[0:size, r, k, P * c:P * c + P], ident[0:size, 0:size])
                last = pe.transpose(ps[:, BANK_T, 352:480], w_nat[:, r, 2, 0:P], ident)
                last = pe.transpose(ps[:, BANK_T + 1, 352:480], w_nat[:, r, 2, P:2 * P], ident)
                last.then_inc(w_turned, 1)
            else:
                last = pe.transpose(ps[:, BANK_T, 0:P], w_nat[:, r, 0, 0:P], ident)
                if shared:
                    last = pe.transpose(ps[:, BANK_T, P:2 * P], w_nat[:, r, 1, 0:P], ident)
                last = pe.transpose(ps[:, BANK_T + 1, 0:P], w_nat[:, r, 2, 0:P], ident)
                last.then_inc(w_turned, 1)

        def moe_tensor(pe, M):
            L, nc_ = M.layer, len(M.pieces)
            ub, yb, sub = base_units[L], 4 * base_passes[L], 2 * L + 1
            x_ready(pe, sub)
            if L != 2:
                k = 0 if L == 1 else 1
                pe.transpose(ps[:, 7, 0:16], gate_nat[:, k, :], ident[0:16, 0:16]).then_inc(gate_turned, 1)
                pe.wait_ge(gate_copied, k + 1)

            turn_weights(pe, M, Pass(0, 0, 0, 0))
            turn_rest(pe, M, Pass(0, 0, 0, 0))
            for g in range(4):
                pe.wait_ge(moe_xn, 4 * (L - 1) + g + 1)
                if g >= 2:
                    pe.wait_ge(x_copied, 4 * (L - 1) + g - 1)
                for j in range(4):
                    last = pe.transpose(ps[:, BANK_G[g % 2], P * j:P * j + P], xn_all[:, 4 * g + j, :], ident)
                last.then_inc(x_turned, 1)
            for g in range(4):
                pe.wait_ge(x_copied, 4 * (L - 1) + g + 1)
                for t in range(4 * g, 4 * g + 4):
                    last = pe.matmul(ps[:, BANK_Y[1], 16 * t:16 * t + 16], xT[:, t, :], gate_w[:, L - 1, :], start=True, stop=True)
            last.then_inc(logits_done, 1)
            pe.wait_ge(x_high, 4 * L)
            pe.wait_ge(x_low, 4 * L)

            def body(n, more):
                r = n.par
                if M.turned:
                    pe.wait_ge(w_copied, base_turned[L] + n.n + 1)
                else:
                    pe.wait_ge(w_loaded[r], 16 * loads_until(L, n, n.half))
                pe.wait_ge(w_high, base_passes[L] + n.n + 1)
                pe.wait_ge(w_low, base_passes[L] + n.n + 1)
                up = L != 1 or (isinstance(n.n, int) and n.n == 0)

                def down(g):
                    pe.wait_ge(units_h, ub + M.units * n.n + nc_ * (g + 1))
                    if g == 1 and isinstance(n.n, int) and n.n == 0:
                        pe.wait_ge(logits_copied, L)
                    wait_free_group(pe, moe_used, yb, n, g, 2)
                    for j in range(4):
                        for c, (off, size) in enumerate(M.pieces):
                            last = pe.matmul(ps[:, BANK_Y[g % 2], P * j:P * j + P], h[0:size, g % 2, c, P * j:P * j + P],
                                             w_dn[0:size, r, c, :], start=(c == 0), stop=(c == nc_ - 1))
                    last.then_inc(moe_y, 1)

                for g in range(4):
                    for c, (off, size) in enumerate(M.pieces):
                        k = g * nc_ + c
                        if ub + M.units * n.least + k - 1 > ub:
                            pe.wait_ge(units_h, ub + M.units * n.n + k - 1)
                        s = k % 2
                        high = x_hi[:, 4 * g:4 * g + 4, :].rearrange("p t q -> p (t q)")
                        low = x_lo[:, 4 * g:4 * g + 4, :].rearrange("p t q -> p (t q)")
                        for kind, bank in enumerate((BANK_G, BANK_U)[:2 if up else 1]):
                            p_unit = ps[0:size, bank[s], :]
                            pe.matmul(p_unit, w_hi[:, r, kind, off:off + size], high, start=True, stop=False)
                            pe.matmul(p_unit, w_hi[:, r, kind, off:off + size], low, start=False, stop=False)
                            last = pe.matmul(p_unit, w_lo[:, r, kind, off:off + size], high, start=False, stop=True)
                        last.then_inc(units_up, 1)
                    if more and g == 1:
                        turn_weights(pe, M, n.next())
                    if g:
                        down(g - 1)
                    if more and g == 1:
                        turn_rest(pe, M, n.next())
                down(3)
            expert_passes(pe, M, body)

        def wait_free_group(eng, s, base, n, g, lag):
            if base + 4 * n.least + g - lag + 1 > 0:
                eng.wait_ge(s, base + 4 * n.n + g - lag + 1)

        def moe_scalar(act, M):
            L, nc_ = M.layer, len(M.pieces)
            ub, yb = base_units[L], 4 * base_passes[L]
            if L != 2:
                k = 0 if L == 1 else 1
                act.wait_ge(gate_turned, k + 1)
                act.copy(gate_w[:, L - 1, :], ps[:, 7, 0:16]).then_inc(gate_copied, 1)
            copy_weights(act, M, Pass(0, 0, 0, 0))
            copy_rest(act, M, Pass(0, 0, 0, 0))

            for g in range(4):
                act.wait_ge(x_turned, 4 * (L - 1) + g + 1)
                act.copy(xT[:, 4 * g:4 * g + 4, :], ps[:, BANK_G[g % 2], :].rearrange("p (t q) -> p t q", q=P)).then_inc(x_copied, 1)
            split_scalar(act, M, Pass(0, 0, 0, 0))
            for g in range(4):
                act.wait_ge(x_masked, 4 * (L - 1) + g + 1)
                act.copy(x_hi[:, 4 * g:4 * g + 4, :], xn_all[:, 4 * g:4 * g + 4, :]).then_inc(x_high, 1)
            act.wait_ge(logits_done, L)
            act.copy(logit[:, :, :], ps[:, BANK_Y[1], 0:256].rearrange("p (t e) -> p t e", e=16)).then_inc(logits_copied, 1)
            if L < 3:
                act.wait_ge(route_asked, L)
                if L == 1:
                    act.activation(ex[:, :, :], cent[:, :, :], ACT.Exp).then_inc(route_exp, 1)
                else:
                    act.activation(rz[:, :], rmax[:, :], ACT.Tanh, scale=0.5).then_inc(route_exp, 1)

            def body(n, more):
                r = n.par
                up = L != 1 or (isinstance(n.n, int) and n.n == 0)
                for g in range(4):
                    for c, (off, size) in enumerate(M.pieces):
                        k = g * nc_ + c
                        act.wait_ge(units_up, ub + M.units * n.n + k + 1)
                        if up:
                            if ub + M.units * n.least + k - 1 > 0:
                                act.wait_ge(units_h, ub + M.units * n.n + k - 1)
                            act.activation(sg[0:size, k % 2, :], ps[0:size, BANK_G[k % 2], :], ACT.Silu).then_inc(units_silu, 1)
                        else:
                            wait_free_group(act, moe_y, yb, n, g, 2)
                            act.activation(h[0:size, g % 2, c, :], ps[0:size, BANK_G[k % 2], :], ACT.Silu).then_inc(units_h, 1)
                    if more and g == 1:
                        copy_weights(act, M, n.next())
                        copy_rest(act, M, n.next())
                if more:
                    split_scalar(act, M, n.next())
            expert_passes(act, M, body)

        def copy_weights(act, M, n):
            L, r = M.layer, n.par
            if not M.turned:
                return
            act.wait_ge(w_turned, base_turned[L] + n.n + 1)
            wait_free(act, moe_y, 4 * base_passes[L], 4, n)
            wait_free(act, w_low, base_passes[L], 1, n, 1)
            if L == 3:
                act.copy(w_raw[:, :, 0:352], ps[:, BANK_T:BANK_T + 2, 0:352])
                act.copy(w_dn[:, r, 0:2, :], ps[:, BANK_T:BANK_T + 2, 352:480]).then_inc(w_part, 1)
            else:
                wide = 256 if isinstance(n.n, int) and n.n == 0 else 128
                if wide == 256:
                    act.copy(w_raw[:, 0:2, 0:P], ps[:, BANK_T, 0:256].rearrange("p (k q) -> p k q", k=2))
                else:
                    act.copy(w_raw[:, 0, 0:P], ps[:, BANK_T, 0:P])
                act.copy(w_dn[:, r, 0, :], ps[:, BANK_T + 1, 0:P]).then_inc(w_copied, 1)

        def copy_rest(act, M, n):
            if M.layer == 3:
                act.wait_ge(w_turned2, n.n + 1)
                act.copy(w_dn[0:96, n.par, 2, :], ps[0:96, BANK_T, 0:P]).then_inc(w_copied, 1)

        def turn_rest(pe, M, n):
            if M.layer == 3:
                pe.wait_ge(w_part, n.n + 1)
                pe.transpose(ps[0:96, BANK_T, 0:P], w_nat[:, n.par, 2, 256:352], ident).then_inc(w_turned2, 1)

        def split_vector(dve, M, n):
            L, r = M.layer, n.par
            wide = [0, 128, 256, 352][L]
            kinds = slice(0, 1 if L == 1 and not (isinstance(n.n, int) and n.n == 0) else 2)
            if M.turned:
                dve.wait_ge(w_copied, base_turned[L] + n.n + 1)
                src = w_raw[:, kinds, 0:wide]
            else:
                dve.wait_ge(w_loaded[r], 16 * loads_until(L, n, n.half))
                src = w_nat[:, r, kinds, 0:wide]
            wait_free(dve, w_high, base_passes[L], 1, n, 1)
            wait_free(dve, moe_y, 4 * base_passes[L], 4, n)
            mask = w_mask[:, kinds, 0:wide]
            dve.tensor_scalar(mask.bitcast(U32), src.bitcast(U32), HIGH_BITS, None, ALU.bitwise_and).then_inc(w_masked, 1)
            dve.wait_ge(w_masked, base_passes[L] + n.n + 1)
            dve.tensor_tensor(w_lo[:, r, kinds, 0:wide], src, mask, ALU.subtract).then_inc(w_low, 1)

        def split_scalar(act, M, n):
            L, r = M.layer, n.par
            wide = [0, 128, 256, 352][L]
            kinds = slice(0, 1 if L == 1 and not (isinstance(n.n, int) and n.n == 0) else 2)
            act.wait_ge(w_masked, base_passes[L] + n.n + 1)
            wait_free(act, moe_y, 4 * base_passes[L], 4, n)
            act.copy(w_hi[:, r, kinds, 0:wide], w_mask[:, kinds, 0:wide]).then_inc(w_high, 1)

        def moe_vector(dve, M):
            L, nc_ = M.layer, len(M.pieces)
            ub, yb, sub = base_units[L], 4 * base_passes[L], 2 * L + 1
            K, E = {1: 4, 2: 2, 3: 2}[L], M.experts

            dve.wait_ge(x_stats, 16 * (L + 1))
            norm_roots(dve, 0)
            for g in range(4):
                for t in range(4 * g, 4 * g + 4):
                    ins = dve.tensor_scalar(xn_all[:, t, :], x[:, t, :], moments[:, 0, t, 0:1], rstd[:, 0, t:t + 1],
                                            ALU.subtract, ALU.mult)
                ins.then_inc(moe_xn, 1)
            split_vector(dve, M, Pass(0, 0, 0, 0))
            dve.wait_ge(x_turned, 4 * L)
            for g in range(4):
                some = slice(4 * g, 4 * g + 4)
                dve.wait_ge(x_copied, 4 * (L - 1) + g + 1)
                dve.tensor_scalar(xn_all[:, some, :].bitcast(U32), xT[:, some, :].bitcast(U32), HIGH_BITS, None,
                                  ALU.bitwise_and).then_inc(x_masked, 1)
                dve.wait_ge(x_masked, 4 * (L - 1) + g + 1)
                dve.tensor_tensor(x_lo[:, some, :], xT[:, some, :], xn_all[:, some, :], ALU.subtract).then_inc(x_low, 1)

            link = [link_base[L]]

            def linked(ins):
                link[0] += 1
                ins.then_inc(route_link, 1)
                dve.wait_ge(route_link, link[0])
            dve.wait_ge(logits_copied, L)
            wide = lambda col, n: col.unsqueeze(2).broadcast_to([P, TILES, n])
            gate = gates[:, 4 + L:5 + L]
            if L == 1:
                linked(dve.tensor_reduce(rmax[:, :], logit[:, :, :], AX.X, ALU.max))
                dve.tensor_tensor(cent[:, :, :], logit[:, :, :], wide(rmax[:, :], 16), ALU.subtract).then_inc(route_asked, 1)
            else:
                for t in range(TILES):
                    ins = dve.max(best[:, t, :], logit[:, t, 0:E])
                linked(ins)
                if L == 2:
                    dve.tensor_tensor(rmax[:, :], best[:, :, 0], best[:, :, 1], ALU.subtract).then_inc(route_asked, 1)

            if L == 1:
                dve.wait_ge(route_exp, 1)
                linked(dve.tensor_reduce(rz[:, :], ex[:, :, :], AX.X, ALU.add))
                linked(dve.reciprocal(rzi[:, :], rz[:, :]))
                linked(dve.tensor_tensor(logit[:, :, :], ex[:, :, :], wide(rzi[:, :], 16), ALU.mult))
                for t in range(TILES):
                    ins = dve.max(best[:, t, :], logit[:, t, 0:E])
                linked(ins)
            for t in range(TILES):
                ins = dve.max_index(besti[:, t, :], best[:, t, :], logit[:, t, 0:E])
            linked(ins)
            linked(dve.tensor_copy(bestf[:, :, :], besti[:, :, :]))
            if L == 1:
                linked(dve.tensor_reduce(rz[:, :], best[:, :, 0:4], AX.X, ALU.add))
                linked(dve.reciprocal(rzi[:, :], rz[:, :]))
                linked(dve.tensor_scalar(rz[:, :], rzi[:, :], gate, None, ALU.mult))
                linked(dve.tensor_tensor(wk[:, :, :], best[:, :, 0:4], wide(rz[:, :], 4), ALU.mult))
            elif L == 2:
                dve.wait_ge(route_exp, 2)
                linked(dve.tensor_scalar(wk[:, :, 0], rz[:, :], 0.5, 0.5, ALU.mult, ALU.add))
                linked(dve.tensor_scalar(wk[:, :, 1], rz[:, :], -0.5, 0.5, ALU.mult, ALU.add))
                linked(dve.tensor_scalar(wk[:, :, 0:2], wk[:, :, 0:2], gate, None, ALU.mult))
            else:
                linked(dve.tensor_scalar(wk[:, :, 0:2], best[:, :, 0:2], gate, None, ALU.mult))

            def finish_routing():
                first = M.shared
                dst = ew[:, :, first:first + E]
                for k in range(K):
                    number = iota[:, 0:E].unsqueeze(1).broadcast_to([P, TILES, E])
                    linked(dve.tensor_tensor(hit[:, :, 0:E], number, wide(bestf[:, :, k], E), ALU.is_equal))
                    if k == 0:
                        linked(dve.tensor_tensor(dst, hit[:, :, 0:E], wide(wk[:, :, k], E), ALU.mult))
                    else:
                        linked(dve.tensor_tensor(hitw[:, :, 0:E], hit[:, :, 0:E], wide(wk[:, :, k], E), ALU.mult))
                        linked(dve.tensor_tensor(dst, dst, hitw[:, :, 0:E], ALU.add))
                if M.shared:
                    linked(dve.tensor_scalar(ew[:, :, 0], ew[:, :, 1], 0.0, gate, ALU.mult, ALU.add))

            if L > 1:
                finish_routing()

            def body(n, more):
                up = L != 1 or (isinstance(n.n, int) and n.n == 0)

                def add(g):
                    dve.wait_ge(moe_y, yb + 4 * n.n + g + 1)
                    if n.least:
                        wait_free(dve, moe_used, yb + g, 4, n, 1)
                    for j in range(4):
                        t = 4 * g + j
                        last = dve.scalar_tensor_tensor(x[:, t, :], ps[:, BANK_Y[g % 2], P * j:P * j + P], ew[:, t, bass.ds(n.n, 1)],
                                                        x[:, t, :], ALU.mult, ALU.add)
                    last.then_inc(moe_used, 1)
                    if not more and L < 3:
                        dve.wait_ge(moe_used, yb + 4 * n.n + g + 1)
                        for t in range(4 * g, 4 * g + 4):
                            last = dve.bn_stats(stats[:, 0, t, :], x[:, t, :])
                        last.then_inc(moe_stats, 1)

                for g in range(4):
                    for c, (off, size) in enumerate(M.pieces):
                        k = g * nc_ + c
                        if up:
                            dve.wait_ge(units_silu, sb_[L] + M.units * n.n + k + 1)
                            wait_free_group(dve, moe_y, yb, n, g, 2)
                            dve.tensor_tensor(h[0:size, g % 2, c, :], sg[0:size, k % 2, :], ps[0:size, BANK_U[k % 2], :],
                                              ALU.mult).then_inc(units_h, 1)
                    if more and g == 3:
                        split_vector(dve, M, n.next())
                    if L == 1 and isinstance(n.n, int) and n.n == 0 and g == 1:
                        finish_routing()
                    if g:
                        add(g - 1)
                add(3)
            expert_passes(dve, M, body)
            link_base[L + 1] = link[0]

        link_base = {1: 0}
        sb_ = {1: 0, 2: 4, 3: 4 + 8 * 8}

        NAMES = {0: ("L0_xattn_Wq", "L0_xattn_Wk", "L0_xattn_Wv", None),
                 1: ("L1_xattn_Wq", "L1_xattn_Wk", "L1_xattn_Wv", "L1_xattn_Wo"),
                 2: ("L2_xattn_Wq", "L2_xattn_Wk", "L2_xattn_Wv", "L2_xattn_Wo"),
                 3: ("L3_xattn_w_q", "L3_xattn_w_k", "L3_xattn_w_v", "L3_xattn_w_o")}
        COLS = [(0, 0, "L0_xattn_bq"), (0, 1, "L0_xattn_bk"), (1, 0, "L1_xattn_bq"), (1, 1, "L1_xattn_bk"),
                (3, 0, "L3_xattn_b_q"), (3, 1, "L3_xattn_b_k")]
        ROWS = [(0, 0, "L0_xattn_bv"), (1, 0, "L1_xattn_bv"), (1, 1, "L1_xattn_bo"), (2, 1, "L2_xattn_bo"),
                (3, 0, "L3_xattn_b_v"), (3, 1, "L3_xattn_b_o")]
        SETUP = 16 * (3 + 3 + 3)
        LATER = 16 * (12 + 4 + 5 + 4 + 3 + 3)

        def column(name):
            return a[name].rearrange("(p n) -> p n", n=1)

        def row(name):
            return a[name].rearrange("(n p) -> n p", n=1)

        def setup_sync(sp):
            n = [0]
            signal = [setup_loaded]

            def load(to, src):
                n[0] += 16
                sp.dma_start(to, src).then_inc(signal[0], 16)

            def weights(L):
                for k, name in enumerate(NAMES[L]):
                    if name:
                        rows = P if k in (0, 3) else CTX
                        load(att_w[0:rows, L, k, :], a[name])
                for l, k, name in COLS:
                    if l == L:
                        load(att_col[:, L, k:k + 1], column(name))
                for l, k, name in ROWS:
                    if l == L:
                        load(att_row[0:1, L, k, :], row(name))
            sp.dma_start(x[:, :, :], a["x"].rearrange("(t b) s d -> (b s) t d", b=2)).then_inc(x_loaded, 16)
            load(const[:, :], a["const"])
            sp.dma_start(ctx_all[:, :, :], a["ctx_768"].rearrange("(t b) s d -> (b s) t d", b=2)).then_inc(ctx_all_loaded, 16)
            load(gates[:, 0:4], row("g_xattn").broadcast_to([P, 4]))
            load(gates[:, 4:8], row("g_ffn").broadcast_to([P, 4]))
            sp.wait_ge(setup_zero, 3)
            weights(0)
            assert n[0] == SETUP, n
            sp.dma_start(q_nat[:, 0, :].rearrange("p (c d) -> p c d", d=P), a["L0_ffn_w_gate"].rearrange("(c p) d -> p c d", p=P)).then_inc(q_loaded, 16)
            sp.dma_start(q_nat[:, 1, :].rearrange("p (c d) -> p c d", d=P), a["L0_ffn_w_up"].rearrange("(c p) d -> p c d", p=P)).then_inc(q_loaded, 16)
            sp.dma_start(q_nat[:, 2, :], a["L0_ffn_w_down"]).then_inc(q_loaded, 16)
            n[0], signal[0] = 0, later_loaded

            def later():
                for L in range(1, 4):
                    weights(L)
                for L, name in ((1, "L1_xattn_bv"), (3, "L3_xattn_b_v"), (0, "L0_xattn_bv")):
                    load(value_col[:, L:L + 1], column(name))
                load(ln_col[:, 0:1], column("L1_xattn_ln1_g"))
                load(ln_col[:, 1:2], column("L1_xattn_ln1_b"))
                load(ln_col[0:CTX, 2:3], column("L1_xattn_ln2_g"))
                load(ln_col[0:CTX, 3:4], column("L1_xattn_ln2_b"))
                load(gate_nat[:, 0, :], a["L1_ffn_gate_w"])
                load(gate_nat[0:8, 1, :], a["L3_ffn_Wg"])
                load(gate_w[:, 1, 0:8], a["L2_ffn_w_gate"])
                assert n[0] == LATER, (n, LATER)
            return later

        def setup_pool(pool):
            pool.memset(att_w[:, :, :, :], 0.0)
            pool.memset(att_col[:, :, :], 0.0)
            pool.memset(ones[:, :], 1.0)
            pool.memset(ln_col[:, :], 0.0)
            pool.memset(gate_nat[:, :, :], 0.0)
            pool.memset(gate_w[:, :, :], 0.0).then_inc(setup_zero, 3)
            pool.memset(ctx_nat[:, :, :], 0.0)
            pool.memset(ctx_norm[:, :, :], 0.0)
            pool.memset(round_col[:, :], ROUND)
            pool.memset(q_sum[:, :], 0.0)
            pool.memset(qz[:, :, :, :], 0.0)
            pool.memset(vx[:, :, :, :, :], 0.0).then_inc(setup_pad, 1)

        def setup_norms(dve):
            dve.wait_ge(x_loaded, 16)
            all_stats(dve, x)
            norm_roots(dve, 0)

        def setup_vector(dve):
            dve.wait_ge(setup_loaded, SETUP)
            dve.wait_ge(setup_pad, 1)
            dve.tensor_copy(ident16[:, :], ident).then_inc(setup_done, 1)
            dve.tensor_copy(vx[:, :, :, :, 16:18].rearrange("p t b m j -> p (t b) m j"),
                            value_mask.rearrange("p (m j e) -> p m j e", j=2, e=HEAD)[:, :, :, 0].unsqueeze(1)
                            .broadcast_to([P, 2 * TILES, 8, 2]))

        def later_pool(pool):
            pool.wait_ge(later_loaded, LATER)
            for L in range(2, 4):
                pool.tensor_scalar(key_bias4[:, L, :], head_mask, att_col[:, L, 1:2], None, ALU.mult)
            for L in (1, 3):
                ins = pool.tensor_scalar(value_bias[:, L, :], ones[:, :], value_col[:, L:L + 1], None, ALU.mult)
            ins.then_inc(later_done, 1)

        block = ctx.enter_context(nc.Block())

        @block.sync
        def _(sp):
            later = setup_sync(sp)
            sp.wait_ge(setup_pad, 1)
            att_sync(sp, ATT[0])
            later()
            for L in range(1, 4):
                moe_sync(sp, MOES[L])
            for g in range(4):
                sp.wait_ge(moe_used, 4 * (base_passes[3] + 7) + g + 1)
                sp.dma_start(out_d[:, 4 * g:4 * g + 4, :], x[:, 4 * g:4 * g + 4, :]).then_inc(stored, 16)
            sp.wait_ge(stored, 64)

        @block.gpsimd
        def _(pool):
            setup_pool(pool)
            qff_round_weights(pool)
            later_pool(pool)
            for L in (2, 3):
                att_pool(pool, ATT[L])

        @block.scalar
        def _(act):
            act.wait_ge(setup_loaded, SETUP)
            act.activation(gates[:, :], gates[:, :], ACT.Tanh).then_inc(gates_done, 1)
            for L in range(4):
                if L == 1:
                    act.wait_ge(later_loaded, LATER)
                    act.wait_ge(later_done, 1)
                att_scalar(act, ATT[L])
                if L == 0:
                    qff_turn_weights(act)
                qff_scalar(act) if L == 0 else moe_scalar(act, MOES[L])

        @block.tensor
        def _(pe):
            pe.wait_ge(setup_loaded, SETUP)
            pe.wait_ge(setup_pad, 1)
            for L in range(4):
                if L == 1:
                    pe.wait_ge(later_loaded, LATER)
                    pe.wait_ge(later_done, 1)
                att_tensor(pe, ATT[L])
                if L == 0:
                    pe.wait_ge(setup_done, 1)
                    x_ready(pe, 1)
                    qff_prepare_tensor(pe)
                qff_tensor(pe) if L == 0 else moe_tensor(pe, MOES[L])

        @block.vector
        def _(dve):
            setup_norms(dve)
            setup_vector(dve)
            dve.wait_ge(gates_done, 1)
            for L in range(4):
                att_vector(dve, ATT[L])
                qff_vector(dve) if L == 0 else moe_vector(dve, MOES[L])


_INS = ["x", "ctx_768", "g_xattn", "g_ffn",
        "L0_xattn_Wq", "L0_xattn_bq", "L0_xattn_Wk", "L0_xattn_bk", "L0_xattn_Wv", "L0_xattn_bv",
        "L0_ffn_w_gate", "L0_ffn_w_up", "L0_ffn_w_down",
        "L1_xattn_ln1_g", "L1_xattn_ln1_b", "L1_xattn_ln2_g", "L1_xattn_ln2_b",
        "L1_xattn_Wq", "L1_xattn_bq", "L1_xattn_Wk", "L1_xattn_bk", "L1_xattn_Wv", "L1_xattn_bv",
        "L1_xattn_Wo", "L1_xattn_bo",
        "L1_ffn_gate_w", "L1_ffn_w1", "L1_ffn_w2", "L1_ffn_shared_gu", "L1_ffn_shared_down",
        "L2_xattn_Wq", "L2_xattn_Wk", "L2_xattn_Wv", "L2_xattn_Wo", "L2_xattn_bo",
        "L2_ffn_w_gate", "L2_ffn_w1", "L2_ffn_w3", "L2_ffn_w2",
        "L3_xattn_w_q", "L3_xattn_b_q", "L3_xattn_w_k", "L3_xattn_b_k", "L3_xattn_w_v", "L3_xattn_b_v",
        "L3_xattn_w_o", "L3_xattn_b_o",
        "L3_ffn_Wg", "L3_ffn_W1", "L3_ffn_W2", "L3_ffn_W3"]

def kernel(**inputs):
    import numpy as _np
    import concourse.bacc as _bacc
    from concourse import mybir as _mybir
    from concourse.bass_utils import run_bass_kernel_spmd as _run

    nc = _bacc.Bacc("TRN2", target_bir_lowering=False, num_devices=1)
    arrays, aps = {}, {}
    for name in _INS + ["const"]:
        a = constants() if name == "const" else _np.ascontiguousarray(inputs[name])
        arrays[f"in_{name}_dram"] = a
        aps[name] = nc.dram_tensor(f"in_{name}_dram", a.shape, _mybir.dt.from_np(a.dtype), kind="ExternalInput").ap()
    out = nc.dram_tensor("out_0_dram", (SEQS, LEN, DIM), F32, kind="ExternalOutput").ap()
    build(nc, aps, out)
    r = _run(nc, [arrays], core_ids=[0])
    return r.results[0]["out_0_dram"]
```
